# Optimizing a Trainium2 kernel written in Bass

```python
import numpy as np
import jax
import jax.numpy as jnp

def _softmax(x, axis=-1):
    return jax.nn.softmax(x, axis=axis)

def _gelu(x):
    return jax.nn.gelu(x, approximate=True)

def _silu(x):
    return jax.nn.silu(x)

def _sigmoid(x):
    return jax.nn.sigmoid(x)

def _layernorm(x, axis=-1, eps=1e-05):
    m = jnp.mean(x, axis=axis, keepdims=True)
    v = jnp.var(x, axis=axis, keepdims=True)
    return (x - m) / jnp.sqrt(v + eps)

def _scatter_add(tgt, idx, src, axis=0):
    return tgt.at[idx].add(src)

def _segment_sum(src, seg, n):
    return jax.ops.segment_sum(src, seg, n)
kernel_name = 'mk_adaln_d1_jaxref_r4_4c21b2'

def setup_inputs(seed: int=0):
    np.random.seed(seed)
    _w = jnp.asarray

    def _L0_attn_setup():
        import jax, jax.numpy as jnp
        import numpy as np
        key = jax.random.key(seed)
        ks = jax.random.split(key, 5)
        B, S, D = (1, 1024, 512)
        H, Dh = (16, 128)
        scale = 1.0 / np.sqrt(D).astype(np.float32)
        return {'x': jax.random.normal(ks[0], (B, S, D), dtype=jnp.float32), 'W_K': jax.random.normal(ks[1], (H, Dh, D), dtype=jnp.float32) * scale, 'W_Q': jax.random.normal(ks[2], (H, Dh, D), dtype=jnp.float32) * scale, 'W_V': jax.random.normal(ks[3], (H, Dh, D), dtype=jnp.float32) * scale, 'W_O': jax.random.normal(ks[4], (D, H * Dh), dtype=jnp.float32) * scale}
    _L0_attn_in = _L0_attn_setup()

    def _L0_ffn_setup():
        import jax, jax.numpy as jnp
        import numpy as np
        _FP4_LUT = jnp.array([0.0, 0.5, 1.0, 1.5, 2.0, 3.0, 4.0, 6.0, -0.0, -0.5, -1.0, -1.5, -2.0, -3.0, -4.0, -6.0], dtype=jnp.float32)
        GROUP_SIZE = 128
        EPS = 1e-06

        def _dequant_fp4(packed_i32, scales_f16, group_size):
            out_f, in_p = packed_i32.shape
            w = packed_i32.astype(jnp.uint32)
            shifts = jnp.arange(8, dtype=jnp.uint32) * 4
            nib = w[:, :, None] >> shifts & jnp.uint32(15)
            vals = _FP4_LUT[nib.astype(jnp.int32)].reshape(out_f, in_p * 8)
            s = scales_f16.astype(jnp.float32).T
            s_full = jnp.repeat(s, group_size, axis=1)
            return vals * s_full
        key = jax.random.key(seed)
        k1, k2, k3, k4, k5 = jax.random.split(key, 5)
        B, S, H, I = (4, 512, 512, 1408)
        x = jax.random.normal(k1, (B, S, H), dtype=jnp.float32)
        gate_up_packed = jax.random.randint(k2, (2 * I, H // 8), 0, 2147483647, dtype=jnp.int32)
        gate_up_scales = jax.random.uniform(k3, (H // GROUP_SIZE, 2 * I), dtype=jnp.float32).astype(jnp.float16)
        down_packed = jax.random.randint(k4, (H, I // 8), 0, 2147483647, dtype=jnp.int32)
        down_scales = jax.random.uniform(k5, (I // GROUP_SIZE, H), dtype=jnp.float32).astype(jnp.float16)
        return {'x': x, 'gate_up_packed': gate_up_packed, 'gate_up_scales': gate_up_scales, 'down_packed': down_packed, 'down_scales': down_scales}
    _L0_ffn_in = _L0_ffn_setup()
    _L0_c = _w((lambda *s: np.random.randn(*s).astype(np.float32) * 0.05)(1, 512))
    _L0_wmod = _w((lambda *s: np.random.randn(*s).astype(np.float32) * 0.05)(512, 6 * 512) * 512 ** (-0.5))
    _d = {'L0_attn_x': _L0_attn_in['x'], 'L0_attn_W_K': _L0_attn_in['W_K'], 'L0_attn_W_Q': _L0_attn_in['W_Q'], 'L0_attn_W_V': _L0_attn_in['W_V'], 'L0_attn_W_O': _L0_attn_in['W_O'], 'L0_ffn_gate_up_packed': _L0_ffn_in['gate_up_packed'], 'L0_ffn_gate_up_scales': _L0_ffn_in['gate_up_scales'], 'L0_ffn_down_packed': _L0_ffn_in['down_packed'], 'L0_ffn_down_scales': _L0_ffn_in['down_scales'], 'L0_c': _L0_c, 'L0_wmod': _L0_wmod}
    _x0 = _d['L0_attn_x']
    _d['L0_attn_x'] = jax.random.normal(jax.random.fold_in(jax.random.key(seed), 1), (1, 2048, 512), dtype=_x0.dtype)
    del _x0
    return _d

def reference(L0_attn_x, L0_attn_W_K, L0_attn_W_Q, L0_attn_W_V, L0_attn_W_O, L0_ffn_gate_up_packed, L0_ffn_gate_up_scales, L0_ffn_down_packed, L0_ffn_down_scales, L0_c, L0_wmod):

    def _L0_attn_ref(x, W_K, W_Q, W_V, W_O):
        import jax, jax.numpy as jnp
        import numpy as np
        b, pos, d_model = x.shape
        d_head = W_K.shape[1]
        k = jnp.einsum('ihd,bpd->biph', W_K, x)
        q = jnp.einsum('ihd,bpd->biph', W_Q, x)
        v = jnp.einsum('ihd,bpd->biph', W_V, x)
        scores = jnp.einsum('biph,biqh->biqp', k, q)
        mask = jnp.tril(jnp.ones((pos, pos), dtype=x.dtype))
        masked = scores * mask - jnp.float32(10000000000.0) * (1.0 - mask)
        attn = jax.nn.softmax(masked / jnp.sqrt(jnp.float32(d_head)), axis=-1)
        z = jnp.einsum('biqp,biph->biqh', attn, v)
        z_flat = jnp.transpose(z, (0, 2, 1, 3)).reshape(b, pos, -1)
        out = jnp.einsum('df,bqf->bqd', W_O, z_flat)
        return out

    def _L0_ffn_ref(x, gate_up_packed, gate_up_scales, down_packed, down_scales):
        import jax, jax.numpy as jnp
        import numpy as np
        _FP4_LUT = jnp.array([0.0, 0.5, 1.0, 1.5, 2.0, 3.0, 4.0, 6.0, -0.0, -0.5, -1.0, -1.5, -2.0, -3.0, -4.0, -6.0], dtype=jnp.float32)
        GROUP_SIZE = 128
        EPS = 1e-06

        def _dequant_fp4(packed_i32, scales_f16, group_size):
            out_f, in_p = packed_i32.shape
            w = packed_i32.astype(jnp.uint32)
            shifts = jnp.arange(8, dtype=jnp.uint32) * 4
            nib = w[:, :, None] >> shifts & jnp.uint32(15)
            vals = _FP4_LUT[nib.astype(jnp.int32)].reshape(out_f, in_p * 8)
            s = scales_f16.astype(jnp.float32).T
            s_full = jnp.repeat(s, group_size, axis=1)
            return vals * s_full
        I = gate_up_packed.shape[0] // 2
        w_gu = _dequant_fp4(gate_up_packed, gate_up_scales, GROUP_SIZE)
        w_down = _dequant_fp4(down_packed, down_scales, GROUP_SIZE)
        gate_up = jnp.einsum('bsh,oh->bso', x, w_gu)
        gate, up = (gate_up[..., :I], gate_up[..., I:])
        h = jax.nn.silu(gate) * up
        y = jnp.einsum('bsi,hi->bsh', h, w_down)
        rms = jnp.sqrt(jnp.mean(y * y, axis=-1, keepdims=True) + EPS)
        return y / rms
    x = L0_attn_x
    mod = (_silu(L0_c) @ L0_wmod).reshape(L0_c.shape[0], 6, 1, -1)
    sa, ca, ga, sb, cb, gb = (mod[:, 0], mod[:, 1], mod[:, 2], mod[:, 3], mod[:, 4], mod[:, 5])
    ga = (2 * (ga >= 0) - 1) * jnp.maximum(jnp.abs(ga), 0.25)
    gb = (2 * (gb >= 0) - 1) * jnp.maximum(jnp.abs(gb), 0.25)
    h = _layernorm(x, axis=-1) * (1 + ca) + sa
    x = x + ga * _L0_attn_ref(h, L0_attn_W_K, L0_attn_W_Q, L0_attn_W_V, L0_attn_W_O)
    h = _layernorm(x, axis=-1) * (1 + cb) + sb
    x = x + gb * _L0_ffn_ref(h, L0_ffn_gate_up_packed, L0_ffn_gate_up_scales, L0_ffn_down_packed, L0_ffn_down_scales)
    return x

_drawn_inputs = setup_inputs


def setup_inputs(seed=0):
    import zlib

    import numpy as np

    out = dict(_drawn_inputs(seed))
    spreads = {}
    factors = {}
    for name, (base, spread) in spreads.items():
        noise = np.random.default_rng([zlib.crc32(name.encode()), seed]).standard_normal(out[name].shape)
        drawn = base * np.exp(spread * noise) if base else spread * noise
        out[name] = jnp.asarray(drawn.astype(out[name].dtype))
    for name, factor in factors.items():
        out[name] = (out[name] * factor).astype(out[name].dtype)
    return out
```

```python
from contextlib import ExitStack
from typing import NamedTuple

import concourse.bass as bass
from concourse import mybir

F32 = mybir.dt.float32
F32R = mybir.dt.float32r
BF16 = mybir.dt.bfloat16
F16 = mybir.dt.float16
I32 = mybir.dt.int32
ALU = mybir.AluOpType
ACT = mybir.ActivationFunctionType
AX_X = mybir.AxisListType.X

P = 128
S, D = 2048, 512
H, DH = 16, 128
INTER = 1408
DC = D // P
NT = S // P
BT = 512
NB = S // BT
TPB = BT // P
NI = INTER // P
NPAIR = NT // 2
WORDS = P // 8
LN_EPS, RMS_EPS = 1e-5, 1e-6
SOFT = DH ** -0.5
MASKED = 1e10 * SOFT


def n_chunks(i):
    return i // TPB + 1


def chunks_before(i):
    return sum(n_chunks(j) for j in range(i))


CHUNKS = chunks_before(NT)
MULTI = sum(n_chunks(i) for i in range(NT) if n_chunks(i) > 1)

PRE = {0: [("V", 0)], 2: [("VT", 0)], 4: [("VT", 1)], 7: [("VT", 2)], 14: [("VT", 3)]}
POST = {1: [("K", 1)], 2: [("Q", 1)], 3: [("V", 1)], 4: [("K", 2)], 5: [("Q", 2)], 6: [("V", 2)],
        8: [("K", 3)], 10: [("Q", 3)], 12: [("V", 3)], 14: [("Qnext", 0)], 15: [("Knext", 0)]}
UNITS = [u for i in range(NT) for u in PRE.get(i, []) + POST.get(i, [])]
UNIT_AT = {u: n for n, u in enumerate(UNITS)}
SPLIT_UNITS = [u for u in UNITS if u[0] != "V"]
SPLIT_AT = {u: n for n, u in enumerate(SPLIT_UNITS)}
NU, NSU = len(UNITS), len(SPLIT_UNITS)
PREU = 2
MATS = ("Q", "K", "V")
SPLIT_ORDER = ("K", "Q", "V")
PV_AT = {2 * b + 3: b for b in range(NPAIR - 1)}
DEQ_STEP = {4: 0, 10: 1, 15: 2}
PIECES = 3


class Tile(NamedTuple):
    t: object
    parity: int
    k: object

    def before(self):
        return Tile(self.t - 1, 1 - self.parity, self.k if self.parity else self.k - 1)

    def after(self):
        return Tile(self.t + 1, 1 - self.parity, self.k + self.parity)


def token_tiles(eng, step):
    for t in range(3):
        step(Tile(t, t % 2, t // 2), t == 0, False)
    with eng.Fori(1, NT // 2 - 1) as u:
        step(Tile(u * 2 + 1, 1, u), False, False)
        step(Tile(u * 2 + 2, 0, u + 1), False, False)
    step(Tile(NT - 1, 1, NT // 2 - 1), False, True)


def rows_of(t):
    return bass.ds(t * P, P)


FIRST, LAST = Tile(0, 0, 0), Tile(NT - 1, 1, NT // 2 - 1)


def is_first(tile):
    return isinstance(tile.t, int) and tile.t == 0


def split_matmul(nc, dst, stat, mov, start, stop):
    nc.tensor.matmul(dst, stat[0], mov[0], start=start, stop=False)
    nc.tensor.matmul(dst, stat[0], mov[1], start=False, stop=False)
    return nc.tensor.matmul(dst, stat[1], mov[0], start=False, stop=stop)


def wait_for(eng, sem, value):
    if not isinstance(value, int) or value > 0:
        eng.wait_ge(sem, value)


def adaln_kernel(nc, x, w_qkv, w_o, gu_packed, gu_scales, dn_packed, dn_scales, c_cols, w_mod, out):
    with ExitStack() as whole:
        hbm = {}
        for name, shape in (("zT", [H, P, S]), ("sums", [H, P, NT]), ("recips", [2 * P, P]),
                            ("wgu", [NI, P, DC * 2 * P]), ("wdn", [NI, P, D]), ("x1", [NT, P, D])):
            hbm[name] = nc.dram_tensor("scratch_" + name, shape, F32).ap()

        def sb(name, shape, dt, ctx=whole):
            return ctx.enter_context(nc.sbuf_tensor(name, shape, dt))

        ident = sb("ident", [P, P], F32)
        ident_bf = sb("ident_bf", [P, P], BF16)
        gate_a = sb("gate_a", [P, D], F32)
        gate_b = sb("gate_b", [P, D], F32)
        shift_a = sb("shift_a", [P, DC], F32)
        scale_a = sb("scale_a", [P, DC], F32)
        shift_b = sb("shift_b", [P, DC], F32)
        scale_b = sb("scale_b", [P, DC], F32)
        nib_shift = sb("nib_shift", [P, 1], I32)
        hT_hi = sb("hT_hi", [P, DC, S], F32R)
        hT_lo = sb("hT_lo", [P, DC, S], F32R)

        with ExitStack() as ph:
            prologue(nc, ph, x, c_cols, w_mod, ident, ident_bf, gate_a, gate_b, shift_a, scale_a,
                     shift_b, scale_b, nib_shift, hT_hi, hT_lo)
        with ExitStack() as ph:
            attention(nc, ph, hbm, w_qkv, gu_packed, gu_scales, dn_packed, dn_scales, ident,
                      ident_bf, nib_shift, hT_hi, hT_lo)
        with ExitStack() as ph:
            output_projection(nc, ph, hbm, x, w_o, ident, gate_a, shift_b, scale_b, hT_hi, hT_lo)
        with ExitStack() as ph:
            mid = sb("midT", [P, NI, S], F32, ph)
            with ExitStack() as ph2:
                gate_up(nc, ph2, hbm, mid, hT_hi, hT_lo)
            with ExitStack() as ph2:
                down(nc, ph2, hbm, mid, gate_b, hT_hi, hT_lo, out)


def prologue(nc, ph, x, c_cols, w_mod, ident, ident_bf, gate_a, gate_b, shift_a, scale_a, shift_b,
             scale_b, nib_shift, hT_hi, hT_lo):
    def sb(name, shape, dt):
        return ph.enter_context(nc.sbuf_tensor(name, shape, dt))

    def sem(name):
        return ph.enter_context(nc.semaphore(name))

    SECTIONS = 6
    xt = sb("p_x", [P, NB, TPB, D], F32)
    wm = sb("p_wmod", [P, 3, DC, D], F32)
    c_in = sb("p_c", [P, DC], F32)
    c_silu = sb("p_csilu", [P, DC], F32)
    c_wide = sb("p_cwide", [P, DC, P], F32)
    ones = sb("p_ones", [P, P], F32)
    rows = sb("p_rows", [P, 2, D], F32)
    absr = sb("p_absr", [P, 2, D], F32)
    stats = sb("p_stats", [P, NT, 6], F32)
    mv = sb("p_mv", [P, NT, 2], F32)
    vare = sb("p_vare", [P, NT], F32)
    std = sb("p_std", [P, NT], F32)
    rstd = sb("p_rstd", [P, NT], F32)
    xn = sb("p_xn", [P, TPB, D], F32)
    h32 = sb("p_h32", [P, 2, BT], F32)
    pidx = sb("p_idx", [P, 1], I32)
    ps_mod = ph.enter_context(nc.psum_tensor("p_psmod", [P, 2, D], F32))
    ps_col = ph.enter_context(nc.psum_tensor("p_pscol", [P, 2, D], F32))
    ps_t = ph.enter_context(nc.psum_tensor("p_pst", [P, 4, BT], F32))

    c_loaded = sem("p_c_loaded")
    x_loaded = [sem(f"p_x_loaded{b}") for b in range(NB)]
    wm_loaded = [sem(f"p_wm_loaded{b}") for b in range(SECTIONS)]
    const_zeroed = sem("p_const_zeroed")
    const_ready = sem("p_const_ready")
    c_ready = sem("p_c_ready")
    wide_ready = sem("p_wide_ready")
    mod_ready = sem("p_mod_ready")
    row_ready = sem("p_row_ready")
    col_ready = sem("p_col_ready")
    mod_used = sem("p_mod_used")
    gate_step = sem("p_gate_step")
    dve_step = sem("p_dve_step")
    var_ready = sem("p_var_ready")
    std_ready = sem("p_std_ready")
    xn_ready = sem("p_xn_ready")
    t_ready = sem("p_t_ready")
    h_ready = sem("p_h_ready")
    hi_ready = sem("p_hi_ready")
    lo_ready = sem("p_lo_ready")
    idx_step = sem("p_idx_step")

    cols = {0: shift_a, 1: scale_a, 3: shift_b, 4: scale_b}
    col_number = {s: n for n, s in enumerate(cols)}
    rows_kept = {2: gate_a, 5: gate_b}
    block = ph.enter_context(nc.Block())

    @block.sync
    def _(sp):
        sp.dma_start(c_in[:, :], c_cols).then_inc(c_loaded, 16)
        def load_x(b):
            sp.dma_start(xt[:, b, :, :], x[b * BT:(b + 1) * BT, :].rearrange("(t p) d -> p t d", p=P)) \
              .then_inc(x_loaded[b], 16)
        def load_w(s):
            if s >= 3:
                sp.wait_ge(mod_ready, s - 2)
            sp.dma_start(wm[:, s % 3, :, :], w_mod[:, s * D:(s + 1) * D].rearrange("(c p) d -> p c d", p=P)) \
              .then_inc(wm_loaded[s], 16)
        load_x(0)
        load_w(0)
        load_w(1)
        for b in range(1, NB):
            load_x(b)
        for s in range(2, SECTIONS):
            load_w(s)

    @block.gpsimd
    def _(pool):
        nc.gpsimd.memset(ident[:, :], 0.0).then_inc(const_zeroed, 1)
        nc.gpsimd.memset(ident_bf[:, :], 0.0).then_inc(const_zeroed, 1)
        nc.gpsimd.memset(ones[:, :], 1.0).then_inc(const_ready, 1)
        pool.wait_ge(const_zeroed, 2)
        for m in (ident, ident_bf):
            nc.gpsimd.affine_select(out=m[:, :], in_=m[:, :], compare_op=ALU.not_equal, fill=1.0, base=0,
                                    pattern=[[-1, P]], channel_multiplier=1).then_inc(const_ready, 1)
        nc.gpsimd.iota(pidx[:, :], pattern=[[0, 1]], base=0, channel_multiplier=1).then_inc(const_ready, 1)

    @block.scalar
    def _(act):
        act.wait_ge(c_loaded, 16)
        nc.scalar.activation(c_silu[:, :], c_in[:, :], ACT.Silu).then_inc(c_ready, 1)

        def copy_row(s):
            act.wait_ge(mod_ready, s + 1)
            if s in cols:
                n = col_number[s]
                if n >= 2:
                    act.wait_ge(col_ready, n - 1)
                nc.scalar.activation(rows[:, n % 2, :], ps_mod[:, s % 2, :], ACT.Copy).then_inc(row_ready, 1)
        copy_row(0)
        copy_row(1)
        for b in range(NB):
            for s in range(b, min(b + 2, NB)) if b == 0 else range(b + 1, min(b + 2, NB)):
                act.wait_ge(var_ready, s + 1)
                nc.scalar.activation(std[:, s * TPB:(s + 1) * TPB], vare[:, s * TPB:(s + 1) * TPB], ACT.Sqrt) \
                  .then_inc(std_ready, 1)
            for c in range(DC):
                n = b * DC + c
                act.wait_ge(t_ready, n + 1)
                if n == 0:
                    act.wait_ge(mod_used, 2)
                if n >= 2:
                    act.wait_ge(lo_ready, n - 1)
                nc.scalar.activation(h32[:, n % 2, :], ps_t[:, n % 4, :], ACT.Identity,
                                     bias=shift_a[:, c:c + 1], scale=scale_a[:, c:c + 1]).then_inc(h_ready, 1)
                act.wait_ge(h_ready, n + 1)
                nc.scalar.activation(hT_hi[:, c, b * BT:(b + 1) * BT], h32[:, n % 2, :], ACT.Copy) \
                  .then_inc(hi_ready, 1)
        for s in (3, 4):
            copy_row(s)

    @block.vector
    def _(dve):
        dve.wait_ge(const_ready, 4)
        nc.vector.tensor_scalar(pidx[:, :], pidx[:, :], 7, 2, ALU.bitwise_and, ALU.logical_shift_left) \
          .then_inc(idx_step, 1)
        dve.wait_ge(idx_step, 1)
        nc.vector.tensor_copy(nib_shift[:, :], pidx[:, :]).then_inc(idx_step, 1)
        dve.wait_ge(c_ready, 1)
        for c in range(DC):
            nc.vector.tensor_scalar(c_wide[:, c, :], ones[:, :], c_silu[:, c:c + 1], None, ALU.mult) \
              .then_inc(wide_ready, 1)
        steps = [0]

        def done(ins):
            ins.then_inc(dve_step, 1)
            steps[0] += 1
            dve.wait_ge(dve_step, steps[0])

        def normalise(b):
            dve.wait_ge(x_loaded[b], 16)
            for t in range(b * TPB, (b + 1) * TPB):
                last = nc.vector.bn_stats(stats[:, t, :], xt[:, b, t % TPB, :])
            done(last)
            for t in range(b * TPB, (b + 1) * TPB):
                last = nc.vector.bn_aggr(mv[:, t, :], stats[:, t, :])
            done(last)
            blk = slice(b * TPB, (b + 1) * TPB)
            nc.vector.tensor_scalar(vare[:, blk], mv[:, blk, 1], LN_EPS, None, ALU.add).then_inc(var_ready, 1)
            dve.wait_ge(std_ready, b + 1)
            done(nc.vector.reciprocal(rstd[:, blk], std[:, blk]))
            if b:
                dve.wait_ge(t_ready, DC * b)
            for t in range(TPB):
                n = b * TPB + t
                nc.vector.tensor_scalar(xn[:, t, :], xt[:, b, t, :], mv[:, n, 0:1], rstd[:, n:n + 1],
                                        ALU.subtract, ALU.mult).then_inc(xn_ready, 1)

        def use_section(s):
            if s in cols:
                n = col_number[s]
                dve.wait_ge(col_ready, n + 1)
                src = ps_col[:, n % 2, :].rearrange("p (c k) -> p c k", c=DC)[:, :, 0]
                nc.vector.tensor_scalar(cols[s][:, :], src, 1.0 if s in (1, 4) else 0.0, None, ALU.add) \
                  .then_inc(mod_used, 1)
            else:
                dve.wait_ge(mod_ready, s + 1)
                g = ps_mod[:, s % 2, :]
                nc.vector.tensor_scalar(absr[:, 0, :], g, 0.0, 2.0, ALU.is_ge, ALU.mult).then_inc(gate_step, 1)
                nc.vector.tensor_scalar(absr[:, 1, :], g, -1.0, 0.25, ALU.mult, ALU.max).then_inc(gate_step, 1)
                dve.wait_ge(gate_step, 2 if s == 2 else 5)
                nc.vector.tensor_tensor(absr[:, 1, :], g, absr[:, 1, :], ALU.max).then_inc(gate_step, 1)
                dve.wait_ge(gate_step, 3 if s == 2 else 6)
                nc.vector.scalar_tensor_tensor(out=rows_kept[s][:, :], in0=absr[:, 0, :], scalar=-1.0,
                                               in1=absr[:, 1, :], op0=ALU.add, op1=ALU.mult) \
                  .then_inc(mod_used, 1)
                dve.wait_ge(mod_used, s + 1)

        def split(b):
            for c in range(DC):
                n = b * DC + c
                dve.wait_ge(hi_ready, n + 1)
                nc.vector.tensor_tensor(hT_lo[:, c, b * BT:(b + 1) * BT], h32[:, n % 2, :],
                                        hT_hi[:, c, b * BT:(b + 1) * BT].bitcast(F32), ALU.subtract) \
                  .then_inc(lo_ready, 1)
        normalise(0)
        use_section(0)
        use_section(1)
        for b in range(1, NB):
            normalise(b)
            split(b - 1)
        split(NB - 1)
        for s in range(2, SECTIONS):
            use_section(s)

    @block.tensor
    def _(pe):
        pe.wait_ge(const_ready, 4)
        pe.wait_ge(wide_ready, DC)

        def mod_section(s):
            if s >= 2:
                pe.wait_ge(mod_used, s - 1)
                if s - 2 in cols:
                    pe.wait_ge(row_ready, col_number[s - 2] + 1)
            pe.wait_ge(wm_loaded[s], 16)
            for c in range(DC):
                last = nc.tensor.matmul(ps_mod[:, s % 2, :], c_wide[:, c, :], wm[:, s % 3, c, :],
                                        start=(c == 0), stop=(c == DC - 1))
            last.then_inc(mod_ready, 1)

        def to_columns(s):
            n = col_number[s]
            pe.wait_ge(row_ready, n + 1)
            if n >= 2:
                pe.wait_ge(mod_used, n - 1)
            for c in range(DC):
                last = nc.tensor.transpose(ps_col[:, n % 2, c * P:(c + 1) * P],
                                           rows[:, n % 2, c * P:(c + 1) * P], ident[:, :])
            last.then_inc(col_ready, 1)

        mod_section(0)
        mod_section(1)
        to_columns(0)
        to_columns(1)
        for b in range(NB):
            pe.wait_ge(xn_ready, (b + 1) * TPB)
            for c in range(DC):
                n = b * DC + c
                if n >= 4:
                    pe.wait_ge(h_ready, n - 3)
                for t in range(TPB):
                    last = nc.tensor.transpose(ps_t[:, n % 4, t * P:(t + 1) * P],
                                               xn[:, t, c * P:(c + 1) * P], ident[:, :])
                last.then_inc(t_ready, 1)
        for s in (2, 3):
            mod_section(s)
        to_columns(3)
        mod_section(4)
        to_columns(4)
        mod_section(5)


def attention(nc, ph, hbm, w_qkv, gu_packed, gu_scales, dn_packed, dn_scales, ident, ident_bf,
              nib_shift, hT_hi, hT_lo):
    def sb(name, shape, dt):
        return ph.enter_context(nc.sbuf_tensor(name, shape, dt))

    def sem(name):
        return ph.enter_context(nc.semaphore(name))

    causal = sb("causal", [P, P], BF16)
    zeros = sb("zeros", [P, P], F32)
    w_raw = sb("w_raw", [P, 3, DC * DH], F32)
    w_hi = sb("w_hi", [P, 3, DC * DH], F32R)
    w_lo = sb("w_lo", [P, 3, DC * DH], F32R)
    kT = [sb(f"kT_{n}", [P, S], F32R) for n in ("hi", "lo")]
    qT = [sb(f"qT_{n}", [P, 2, BT], F32R) for n in ("hi", "lo")]
    v = [sb(f"v_{n}", [P, NT, DH], F32R) for n in ("hi", "lo")]
    vT = sb("vT", [P, BT], F32)
    probs = sb("probs", [P, 2, S], F32)
    pT = [sb(f"pT_{n}", [P, 3, NT * P], F32R) for n in ("hi", "lo")]
    z = sb("z", [P, 2, 2 * P], F32)
    cmin = sb("cmin", [P, NB], F32)
    rmin = sb("rmin", [P, 2], F32)
    sums = sb("sums", [P, NT], F32)
    words = sb("words", [P, D], I32)
    code = sb("code", [P, D], I32)
    deq_a = sb("deq_a", [P, D], F32)
    deq_b = sb("deq_b", [P, D], F32)
    qscale = sb("qscale", [P, D], F16)
    half_scale = sb("half_scale", [P, D], F32)
    halves = sb("halves", [P, 1], F32)
    ps_s = ph.enter_context(nc.psum_tensor("ps_s", [P, NB, BT], F32))
    ps_t = ph.enter_context(nc.psum_tensor("ps_t", [P, 2, BT], F32))
    ps_z = ph.enter_context(nc.psum_tensor("ps_z", [P, 512], F32))
    ps_p = ph.enter_context(nc.psum_tensor("ps_p", [P, BT], F32))

    w_loaded = sem("w_loaded")
    w_split = sem("w_split")
    consts = sem("consts")
    scores_ready = sem("scores_ready")
    chunk_min = sem("chunk_min")
    min_ready = sem("min_ready")
    exp_ready = sem("exp_ready")
    t_ready = sem("t_ready")
    t_hi = sem("t_hi")
    t_lo = sem("t_lo")
    proj_ready = sem("proj_ready")
    proj_hi = sem("proj_hi")
    proj_lo = sem("proj_lo")
    zero_ready = sem("zero_ready")
    z_ready = sem("z_ready")
    z_copied = sem("z_copied")
    z_saved = [sem(f"z_saved{n}") for n in range(2)]
    sums_saved = sem("sums_saved")
    words_loaded = sem("words_loaded")
    qscale_loaded = sem("qscale_loaded")
    unpacked = sem("unpacked")
    deq_step = sem("deq_step")
    deq_saved = sem("deq_saved")

    Z_DMAS = (1, 2)
    DEQ_OPS = 9
    LOADS = {0: 2, 1: 2, 2: 1}
    LOADS_BEFORE = {0: 0, 1: 2, 2: 4}
    LOADS_ALL = 5

    block = ph.enter_context(nc.Block())
    stretches = [(1, NI), (NI, H - 1)]

    @block.sync
    def _(sp):
        sp.dma_start(w_raw[:, :, :], w_qkv[0]).then_inc(w_loaded, 16)

        def load_piece(h, k):
            sp.wait_ge(deq_step, DEQ_OPS * (PIECES * h + k)) if not (isinstance(h, int) and h + k == 0) else None
            if k < 2:
                for c in range(2):
                    src = gu_packed[bass.ds(h, 1), 2 * k + c, :, :]
                    sp.dma_start(words[:, c * 2 * P:(c + 1) * 2 * P],
                                 replicate(src, 2 * P)).then_inc(words_loaded, 16)
                sp.dma_start(qscale[:, :], gu_scales[bass.ds(h, 1), k, :].to_broadcast([P, D])) \
                  .then_inc(qscale_loaded, 16)
            else:
                sp.dma_start(words[:, :], replicate(dn_packed[bass.ds(h, 1), :, :], D)).then_inc(words_loaded, 16)
                sp.dma_start(qscale[:, :], dn_scales[bass.ds(h, 1), :].to_broadcast([P, D])) \
                  .then_inc(qscale_loaded, 16)

        def replicate(src, n):
            a = src.rearrange("a w n -> (a w) n")
            return a.unsqueeze(1).to_broadcast([WORDS, 8, n])

        def save_piece(h, k):
            sp.wait_ge(deq_step, DEQ_OPS * (PIECES * h + k + 1))
            if k < 2:
                dst = hbm["wgu"][bass.ds(h, 1), :, k * D:(k + 1) * D].rearrange("a p n -> (a p) n")
            else:
                dst = hbm["wdn"][bass.ds(h, 1), :, :].rearrange("a p n -> (a p) n")
            sp.dma_start(dst, deq_a[:, :]).then_inc(deq_saved, 16)

        def save_z(h, b):
            sp.wait_ge(z_copied, NPAIR * h + b + 1)
            dst = hbm["zT"][bass.ds(h, 1), :, b * 2 * P:(b + 1) * 2 * P].rearrange("a p n -> (a p) n")
            if b % 2 == 0:
                sp.dma_start(dst, z[:, 0, :]).then_inc(z_saved[0], 16)
            else:
                sp.dma_start(dst[:, P:2 * P], z[:, 1, 0:P]).then_inc(z_saved[1], 16)
                sp.dma_start(dst[:, 0:P], z[:, 1, P:2 * P]).then_inc(z_saved[1], 16)

        def head(h, decode, last):
            if not last:
                sp.wait_ge(w_split, 6 * (h + 1))
                sp.dma_start(w_raw[:, :, :], w_qkv[bass.ds(h + 1, 1), :, :, :].rearrange("a p m n -> (a p) m n")) \
                  .then_inc(w_loaded, 16)
            for b in range(NPAIR):
                if decode and b == 0:
                    load_piece(h, 0)
                if decode and b == 2:
                    save_piece(h, 0)
                    load_piece(h, 1)
                if decode and b == 5:
                    save_piece(h, 1)
                    load_piece(h, 2)
                save_z(h, b)
            sp.wait_ge(exp_ready, NT * (h + 1))
            sp.dma_start(hbm["sums"][bass.ds(h, 1), :, :].rearrange("a p n -> (a p) n"), sums[:, :]) \
              .then_inc(sums_saved, 16)
            if decode:
                save_piece(h, 2)
        head(0, True, False)
        for n, (a, z_) in enumerate(stretches):
            with sp.Fori(a, z_) as h:
                head(h, n == 0, False)
        head(H - 1, False, True)
        for n in range(2):
            sp.wait_ge(z_saved[n], Z_DMAS[n] * 16 * H * NPAIR // 2)
        sp.wait_ge(sums_saved, 16 * H)
        sp.wait_ge(deq_saved, 16 * PIECES * NI)

    @block.gpsimd
    def _(pool):
        nc.gpsimd.memset(zeros[:, :], 0.0).then_inc(consts, 1)
        nc.gpsimd.memset(halves[:, :], 0.5).then_inc(consts, 1)
        pool.wait_ge(consts, 2)
        nc.gpsimd.affine_select(out=causal[:, :], in_=zeros[:, :], compare_op=ALU.is_ge, fill=MASKED, base=0,
                                pattern=[[-1, P]], channel_multiplier=1).then_inc(consts, 1)

        def split_weights(h, m, n):
            if n == 0:
                pool.wait_ge(w_loaded, 16 * (h + 1))
            if not (isinstance(h, int) and h == 0):
                pool.wait_ge(proj_ready, PREU + NU * (h - 1) + UNIT_AT[(MATS[m], NB - 1)] + 1)
            nc.gpsimd.tensor_tensor(w_hi[:, m, :], w_raw[:, m, :], zeros[:, 0:1].to_broadcast([P, DC * DH]), ALU.add) \
              .then_inc(w_split, 1)
            pool.wait_ge(w_split, 6 * h + 2 * n + 1)
            nc.gpsimd.tensor_tensor(w_lo[:, m, :], w_raw[:, m, :], w_hi[:, m, :].bitcast(F32), ALU.subtract) \
              .then_inc(w_split, 1)

        def zero_block(h, b):
            if b < 2:
                wait_for(pool, z_ready, NPAIR * h)
            else:
                pool.wait_ge(z_ready, NPAIR * h + b - 1)
            for part in pT:
                nc.gpsimd.tensor_tensor(part[:, 2 * (b % 2), (2 * b + 1) * P:(2 * b + 2) * P],
                                        zeros[:, :], zeros[:, :], ALU.add).then_inc(zero_ready, 1)

        def decode_piece(h, k):
            base = PIECES * h + k
            made = DEQ_OPS * base
            code_f, sign_f = code[:, :].bitcast(F32), words[:, :].bitcast(F32)
            pool.wait_ge(unpacked, 3 * (base + 1))
            pool.wait_ge(qscale_loaded, 16 * (base + 1))
            wait_for(pool, deq_saved, 16 * base)
            wait_for(pool, deq_step, made)
            nc.gpsimd.tensor_tensor(half_scale[:, :], qscale[:, :], halves[:, 0:1].to_broadcast([P, D]), ALU.mult) \
              .then_inc(deq_step, 1)
            nc.gpsimd.tensor_scalar(deq_a[:, :], code[:, :], 4.0, -16.0, ALU.max, ALU.add).then_inc(deq_step, 1)
            nc.gpsimd.tensor_scalar(deq_b[:, :], code[:, :], 6.0, 2.0, ALU.max, ALU.mult).then_inc(deq_step, 1)
            pool.wait_ge(deq_step, made + 3)
            nc.gpsimd.tensor_tensor(deq_a[:, :], deq_a[:, :], deq_b[:, :], ALU.add).then_inc(deq_step, 1)
            nc.gpsimd.tensor_scalar(code_f, code[:, :], 1.0, None, ALU.mult).then_inc(deq_step, 1)
            nc.gpsimd.tensor_scalar(sign_f, words[:, :], -0.25, 1.0, ALU.mult, ALU.add).then_inc(deq_step, 1)
            pool.wait_ge(deq_step, made + 6)
            nc.gpsimd.tensor_tensor(deq_a[:, :], deq_a[:, :], code_f, ALU.add).then_inc(deq_step, 1)
            pool.wait_ge(deq_step, made + 7)
            nc.gpsimd.tensor_tensor(deq_a[:, :], deq_a[:, :], sign_f, ALU.mult).then_inc(deq_step, 1)
            pool.wait_ge(deq_step, made + 8)
            nc.gpsimd.tensor_tensor(deq_a[:, :], deq_a[:, :], half_scale[:, :], ALU.mult).then_inc(deq_step, 1)

        def head(h, decode, last):
            zero_block(h, 0)
            zero_block(h, 1)
            zero_block(h, 2)
            if decode:
                decode_piece(h, 0)
            zero_block(h, 3)
            zero_block(h, 4)
            zero_block(h, 5)
            if not last:
                split_weights(h + 1, MATS.index("K"), 0)
                split_weights(h + 1, MATS.index("Q"), 1)
            if decode:
                decode_piece(h, 1)
            zero_block(h, 6)
            if not last:
                split_weights(h + 1, MATS.index("V"), 2)
            zero_block(h, 7)
            if decode:
                decode_piece(h, 2)
        for n, m in enumerate(SPLIT_ORDER):
            split_weights(0, MATS.index(m), n)
        head(0, True, False)
        for n, (a, z_) in enumerate(stretches):
            with pool.Fori(a, z_) as h:
                head(h, n == 0, False)
        head(H - 1, False, True)

    @block.tensor
    def _(pe):
        def project(h, unit):
            kind, b = unit
            if h is None:
                nth = {"Q": 0, "K": 1}[kind]
                if nth:
                    pe.wait_ge(proj_lo, nth)
            else:
                nth = UNIT_AT[unit]
                prev = UNITS[nth - 1] if nth else None
                if prev and prev[0] == "V":
                    pe.wait_ge(proj_hi, PREU + NU * h + nth)
                else:
                    pe.wait_ge(proj_lo, PREU + NSU * h + (SPLIT_AT[prev] + 1 if prev else 0))
            if kind == "VT":
                if prev[0] != "V":
                    pe.wait_ge(proj_hi, PREU + NU * h + UNIT_AT[("V", b)] + 1)
                for t in range(TPB):
                    last = nc.tensor.transpose(ps_p[:, t * P:(t + 1) * P], vT[:, t * P:(t + 1) * P], ident[:, :])
            else:
                m = MATS.index(kind[0])
                if h is None:
                    pe.wait_ge(w_split, 2 * SPLIT_ORDER.index(kind) + 2)
                elif b == 0:
                    pe.wait_ge(w_split, 6 * (h if kind == "V" else h + 1) + 2 * SPLIT_ORDER.index(kind[0]) + 2)
                for c in range(DC):
                    w = [part[:, m, c * DH:(c + 1) * DH] for part in (w_hi, w_lo)]
                    ht = [part[:, c, b * BT:(b + 1) * BT] for part in (hT_hi, hT_lo)]
                    last = split_matmul(nc, ps_p[:, :], w, ht, c == 0, c == DC - 1)
            last.then_inc(proj_ready, 1)

        def lo_count(h, unit):
            if unit[0] in ("Q", "K") and unit[1] == 0:
                return PREU + NSU * h
            return PREU + NSU * h + SPLIT_AT[unit] + 1

        def made_at(unit):
            return SPLIT_AT[unit] if unit in SPLIT_AT else -1

        def scores(h, i):
            pe.wait_ge(exp_ready, NT * h + i) if not (isinstance(h, int) and h + i == 0) else None
            b, r = divmod(i, TPB)
            if r == 0:
                pe.wait_ge(proj_lo, lo_count(h, max((("Q", b), ("K", b)), key=made_at)))
            q = [part[:, b % 2, r * P:(r + 1) * P] for part in qT]
            for c in range(b + 1):
                n = BT if c < b else max(r + 1, 2) * P
                k = [part[:, c * BT:c * BT + n] for part in kT]
                diagonal = c == b
                last = split_matmul(nc, ps_s[:, c, 0:n], q, k, True, True)
                if diagonal:
                    last = nc.tensor.matmul(ps_s[:, c, r * P:(r + 1) * P], ident_bf[:, :], causal[:, :],
                                            start=False, stop=True, skip_group_check=True)
                last.then_inc(scores_ready, 1)

        def transposes(h, i):
            pe.wait_ge(exp_ready, NT * h + i + 1)
            for u in range(n_chunks(i)):
                n = chunks_before(i) + u
                if n >= 2:
                    pe.wait_ge(t_lo, CHUNKS * h + n - 1)
                for k in range(4 * u, min(4 * u + 4, i + 1)):
                    last = nc.tensor.transpose(ps_t[:, n % 2, (k - 4 * u) * P:(k - 4 * u + 1) * P],
                                               probs[:, i % 2, k * P:(k + 1) * P], ident[:, :])
                last.then_inc(t_ready, 1)

        def pv(h, b):
            if not (isinstance(h, int) and h + b == 0):
                pe.wait_ge(z_copied, NPAIR * h + b)
            pe.wait_ge(zero_ready, 2 * (NPAIR * h + b + 1))
            a = b % 2
            for k in range(2 * b + 2):
                if k % 4 == 0:
                    pe.wait_ge(t_lo, CHUNKS * h + chunks_before(2 * b + 1) + k // 4 + 1)
                    pe.wait_ge(proj_lo, lo_count(h, ("VT", k // 4)))
                p = [part[:, a:a + 2, k * P:(k + 1) * P] for part in pT]
                vv = [part[:, k, :] for part in v]
                last = split_matmul(nc, ps_z[:, 0:2 * P], vv, p, k == 0, k == 2 * b + 1)
            last.then_inc(z_ready, 1)

        def head(h, last):
            for i in range(NT):
                scores(h, i)
                for u in PRE.get(i, []):
                    project(h, u)
                if i:
                    transposes(h, i - 1)
                if i in PV_AT:
                    pv(h, PV_AT[i])
                for u in POST.get(i, []):
                    if not (last and u[0].endswith("next")):
                        project(h, u)
            transposes(h, NT - 1)
            pv(h, NPAIR - 1)
        pe.wait_ge(consts, 3)
        project(None, ("Q", 0))
        project(None, ("K", 0))
        head(0, False)
        for a, z_ in stretches:
            with pe.Fori(a, z_) as h:
                head(h, False)
        head(H - 1, True)

    @block.scalar
    def _(act):
        def unit_hi(h, unit):
            kind, b = unit
            if h is None:
                nth = {"Q": 0, "K": 1}[kind]
                act.wait_ge(proj_ready, nth + 1)
            else:
                act.wait_ge(proj_ready, PREU + NU * h + UNIT_AT[unit] + 1)
            if kind == "V":
                ins = nc.scalar.activation(vT[:, :], ps_p[:, :], ACT.Copy)
            elif kind == "VT":
                ins = nc.scalar.activation(v[0][:, b * TPB:(b + 1) * TPB, :],
                                           ps_p[:, :].rearrange("p (t n) -> p t n", t=TPB), ACT.Copy)
            elif kind[0] == "Q":
                ins = nc.scalar.activation(qT[0][:, b % 2, :], ps_p[:, :], ACT.Copy, scale=-SOFT)
            else:
                ins = nc.scalar.activation(kT[0][:, b * BT:(b + 1) * BT], ps_p[:, :], ACT.Copy)
            ins.then_inc(proj_hi, 1)

        def transposed_hi(h, i):
            sub = 1 if i % 2 else 2 * (i // 2 % 2)
            for u in range(n_chunks(i)):
                act.wait_ge(t_ready, CHUNKS * h + chunks_before(i) + u + 1)
                lo, hi = 4 * u * P, min(4 * u + 4, i + 1) * P
                nc.scalar.activation(pT[0][:, sub, lo:hi], ps_t[:, (chunks_before(i) + u) % 2, 0:hi - lo],
                                     ACT.Copy).then_inc(t_hi, 1)

        def exponent(h, i):
            if i == 0:
                wait_for(act, sums_saved, 16 * h)
            act.wait_ge(min_ready, NT * h + i + 1)
            w = (i + 1) * P
            src = ps_s[:, :, :].rearrange("p c n -> p (c n)")[:, 0:w]
            nc.scalar.activation(probs[:, i % 2, 0:w], src, ACT.Exp, bias=rmin[:, i % 2:i % 2 + 1], scale=-1.0,
                                 accum_out=sums[:, i:i + 1]).then_inc(exp_ready, 1)

        def copy_z(h, b):
            act.wait_ge(z_ready, NPAIR * h + b + 1)
            wait_for(act, z_saved[b % 2], Z_DMAS[b % 2] * 16 * (NPAIR // 2 * h + b // 2))
            nc.scalar.activation(z[:, b % 2, :], ps_z[:, 0:2 * P], ACT.Copy).then_inc(z_copied, 1)

        def head(h, last):
            for i in range(NT):
                for u in PRE.get(i, []):
                    unit_hi(h, u)
                if i:
                    transposed_hi(h, i - 1)
                exponent(h, i)
                if i in PV_AT:
                    copy_z(h, PV_AT[i])
                for u in POST.get(i, []):
                    if not (last and u[0].endswith("next")):
                        unit_hi(h, u)
            transposed_hi(h, NT - 1)
            copy_z(h, NPAIR - 1)
        unit_hi(None, ("Q", 0))
        unit_hi(None, ("K", 0))
        head(0, False)
        for a, z_ in stretches:
            with act.Fori(a, z_) as h:
                head(h, False)
        head(H - 1, True)

    @block.vector
    def _(dve):
        def unit_lo(h, unit):
            kind, b = unit
            if kind == "V":
                return
            if h is None:
                nth = {"Q": 0, "K": 1}[kind]
                dve.wait_ge(proj_hi, nth + 1)
            else:
                dve.wait_ge(proj_hi, PREU + NU * h + UNIT_AT[unit] + 1)
            if kind == "VT":
                parts = [part[:, b * TPB:(b + 1) * TPB, :].rearrange("p t n -> p (t n)") for part in v]
            elif kind[0] == "Q":
                parts = [part[:, b % 2, :] for part in qT]
            else:
                parts = [part[:, b * BT:(b + 1) * BT] for part in kT]
            if kind[0] == "Q":
                ins = nc.vector.scalar_tensor_tensor(out=parts[1], in0=ps_p[:, :], scalar=-SOFT,
                                                     in1=parts[0].bitcast(F32), op0=ALU.mult, op1=ALU.subtract)
            else:
                ins = nc.vector.tensor_tensor(parts[1], ps_p[:, :], parts[0].bitcast(F32), ALU.subtract)
            ins.then_inc(proj_lo, 1)

        def minimum(h, i):
            nch = n_chunks(i)
            for c in range(nch):
                dve.wait_ge(scores_ready, CHUNKS * h + chunks_before(i) + c + 1)
                w = BT if c < nch - 1 else (i % TPB + 1) * P
                if nch == 1:
                    nc.vector.tensor_reduce(rmin[:, i % 2:i % 2 + 1], ps_s[:, c, 0:w], AX_X, ALU.min) \
                      .then_inc(min_ready, 1)
                else:
                    nc.vector.tensor_reduce(cmin[:, c:c + 1], ps_s[:, c, 0:w], AX_X, ALU.min) \
                      .then_inc(chunk_min, 1)
            if nch > 1:
                done = sum(n_chunks(j) for j in range(i + 1) if n_chunks(j) > 1)
                dve.wait_ge(chunk_min, MULTI * h + done)
                nc.vector.tensor_reduce(rmin[:, i % 2:i % 2 + 1], cmin[:, 0:nch], AX_X, ALU.min) \
                  .then_inc(min_ready, 1)

        def transposed_lo(h, i):
            sub = 1 if i % 2 else 2 * (i // 2 % 2)
            for u in range(n_chunks(i)):
                dve.wait_ge(t_hi, CHUNKS * h + chunks_before(i) + u + 1)
                lo, hi = 4 * u * P, min(4 * u + 4, i + 1) * P
                nc.vector.tensor_tensor(pT[1][:, sub, lo:hi], ps_t[:, (chunks_before(i) + u) % 2, 0:hi - lo],
                                        pT[0][:, sub, lo:hi].bitcast(F32), ALU.subtract).then_inc(t_lo, 1)

        def unpack(h, k):
            base = PIECES * h + k
            dve.wait_ge(words_loaded, 16 * (LOADS_ALL * h + LOADS_BEFORE[k] + LOADS[k]))
            nc.vector.tensor_tensor(words[:, :], words[:, :], nib_shift[:, 0:1].to_broadcast([P, D]),
                                    ALU.logical_shift_right).then_inc(unpacked, 1)
            dve.wait_ge(unpacked, 3 * base + 1)
            nc.vector.tensor_scalar(code[:, :], words[:, :], 7, None, ALU.bitwise_and).then_inc(unpacked, 1)
            dve.wait_ge(unpacked, 3 * base + 2)
            nc.vector.tensor_scalar(words[:, :], words[:, :], 8, None, ALU.bitwise_and).then_inc(unpacked, 1)

        def head(h, decode, last):
            for i in range(NT):
                minimum(h, i)
                for u in PRE.get(i, []):
                    unit_lo(h, u)
                if i:
                    transposed_lo(h, i - 1)
                for u in POST.get(i, []):
                    if not (last and u[0].endswith("next")):
                        unit_lo(h, u)
                if decode and i in DEQ_STEP:
                    unpack(h, DEQ_STEP[i])
            transposed_lo(h, NT - 1)
        unit_lo(None, ("Q", 0))
        unit_lo(None, ("K", 0))
        head(0, True, False)
        for n, (a, z_) in enumerate(stretches):
            with dve.Fori(a, z_) as h:
                head(h, n == 0, False)
        head(H - 1, False, True)


def output_projection(nc, ph, hbm, x, w_o, ident, gate_a, shift_b, scale_b, hT_hi, hT_lo):
    def sb(name, shape, dt):
        return ph.enter_context(nc.sbuf_tensor(name, shape, dt))

    def sem(name):
        return ph.enter_context(nc.semaphore("o_" + name))

    HH = H // 2
    RW = 2
    wo = [sb(f"wo_{n}", [P, H, D], F32R) for n in ("hi", "lo")]
    stage = sb("wo_stage", [P, 2, RW, D], F32)
    sums = sb("o_sums", [P, H * NT], F32)
    recip = sb("o_recip", [P, H * NT], F32)
    recipT = sb("o_recipT", [P, 2, P], F32)
    zt = sb("o_z", [P, 2, HH, P], F32)
    rt = sb("o_r", [P, 2, HH, P], F32)
    zs = [sb(f"o_z{n}", [P, 2, HH, P], F32R) for n in ("hi", "lo")]
    xt = sb("o_x", [P, 2, D], F32)
    x1 = sb("o_x1", [P, 2, D], F32)
    xn = sb("o_xn", [P, 2, D], F32)
    h32 = sb("o_h32", [P, 2, D], F32)
    hs = [sb(f"o_h{n}", [P, 2, D], F32R) for n in ("hi", "lo")]
    stats = sb("o_stats", [P, 6], F32)
    mv = sb("o_mv", [P, 2], F32)
    vare = sb("o_vare", [P, 1], F32)
    std = sb("o_std", [P, 1], F32)
    rstd = sb("o_rstd", [P, 1], F32)
    ps_r = ph.enter_context(nc.psum_tensor("o_psr", [P, 2, 512], F32))
    ps_o = ph.enter_context(nc.psum_tensor("o_pso", [P, 2, 512], F32))
    ps_t = ph.enter_context(nc.psum_tensor("o_pst", [P, 2, 512], F32))

    sums_loaded = sem("sums_loaded")
    recip_ready = sem("recip_ready")
    recip_t = sem("recip_t")
    recip_row = sem("recip_row")
    recip_saved = sem("recip_saved")
    wo_loaded = [sem(f"wo_loaded{n}") for n in range(2)]
    wo_hi = sem("wo_hi")
    wo_lo = sem("wo_lo")
    z_loaded = [sem(f"z_loaded{n}") for n in range(2)]
    x_loaded = [sem(f"x_loaded{n}") for n in range(2)]
    z_norm = sem("z_norm")
    z_hi = sem("z_hi")
    z_lo = sem("z_lo")
    half_done = sem("half_done")
    dve_step = sem("dve_step")
    x1_ready = sem("x1_ready")
    x1_saved = [sem(f"x1_saved{n}") for n in range(2)]
    var_ready = sem("var_ready")
    std_ready = sem("std_ready")
    xn_ready = sem("xn_ready")
    t_ready = sem("t_ready")
    h_ready = [sem(f"h_ready{n}") for n in range(2)]
    h_hi = sem("h_hi")
    h_lo = sem("h_lo")
    h_saved = [sem(f"h_saved{n}") for n in range(2)]
    STEPS = 4

    block = ph.enter_context(nc.Block())

    @block.sync
    def _(sp):
        sp.dma_start(sums[:, :].rearrange("p (h i) -> p h i", h=H),
                     hbm["sums"].rearrange("h p i -> p h i")).then_inc(sums_loaded, 16)
        for n in range(H // RW):
            if n >= 2:
                sp.wait_ge(wo_lo, n - 1)
            sp.dma_start(stage[:, n % 2, :, :], w_o[:, n * RW:(n + 1) * RW, :]).then_inc(wo_loaded[n % 2], 16)
            if n == 1:
                sp.wait_ge(recip_row, 1)
                sp.dma_start(hbm["recips"].rearrange("(a p) n -> p a n", a=2), recipT[:, :, :]) \
                  .then_inc(recip_saved, 16)
        sp.wait_ge(recip_saved, 16)
        r_view = hbm["recips"].rearrange("(h i) n -> h i n", h=H)

        def load_half(tile, f):
            if not is_first(tile):
                sp.wait_ge(z_lo, 2 * tile.t + f - 1)
            sp.dma_start(zt[:, f, :, :], hbm["zT"][f * HH:(f + 1) * HH, :, rows_of(tile.t)]
                         .rearrange("h p n -> p h n")).then_inc(z_loaded[f], 16)
            src = r_view[f * HH:(f + 1) * HH, bass.ds(tile.t, 1), :].rearrange("h a n -> a h n")
            sp.dma_start(rt[:, f, :, :], src.to_broadcast([P, HH, P])).then_inc(z_loaded[f], 16)

        def load_x(tile):
            if not is_first(tile):
                sp.wait_ge(x1_ready, tile.t - 1)
            sp.dma_start(xt[:, tile.parity, :], x[rows_of(tile.t), :]).then_inc(x_loaded[tile.parity], 16)

        def save_h(tile):
            sp.wait_ge(h_lo, tile.t + 1)
            for part, whole in zip(hs, (hT_hi, hT_lo)):
                sp.dma_start(whole[:, :, rows_of(tile.t)].bitcast(F32),
                             part[:, tile.parity, :].rearrange("p (c n) -> p c n", c=DC).bitcast(F32)) \
                  .then_inc(h_saved[tile.parity], 16)

        def step(tile, first, last):
            if not last:
                load_half(tile.after(), 0)
                load_x(tile.after())
                load_half(tile.after(), 1)
            if not first:
                save_h(tile.before())
            sp.wait_ge(x1_ready, tile.t + 1)
            sp.dma_start(hbm["x1"][bass.ds(tile.t, 1), :, :].rearrange("a p d -> (a p) d"),
                         x1[:, tile.parity, :]).then_inc(x1_saved[tile.parity], 16)
        load_half(FIRST, 0)
        load_half(FIRST, 1)
        load_x(FIRST)
        token_tiles(sp, step)
        save_h(LAST)
        for n in range(2):
            sp.wait_ge(h_saved[n], 2 * 16 * NT // 2)
            sp.wait_ge(x1_saved[n], 16 * NT // 2)

    @block.vector
    def _(dve):
        dve.wait_ge(sums_loaded, 16)
        nc.vector.reciprocal(recip[:, :], sums[:, :]).then_inc(recip_ready, 1)
        for n in range(H // RW):
            dve.wait_ge(wo_hi, n + 1)
            sl = slice(n * RW, (n + 1) * RW)
            nc.vector.tensor_tensor(wo[1][:, sl, :], stage[:, n % 2, :, :], wo[0][:, sl, :].bitcast(F32),
                                    ALU.subtract).then_inc(wo_lo, 1)

        def split_half(tile, f):
            dve.wait_ge(z_loaded[f], 32 * (tile.t + 1))
            nc.vector.tensor_tensor(zt[:, f, :, :], zt[:, f, :, :], rt[:, f, :, :], ALU.mult).then_inc(z_norm, 1)
            dve.wait_ge(z_hi, 2 * tile.t + f + 1)
            nc.vector.tensor_tensor(zs[1][:, f, :, :], zt[:, f, :, :], zs[0][:, f, :, :].bitcast(F32),
                                    ALU.subtract).then_inc(z_lo, 1)

        def split_h(tile):
            dve.wait_ge(h_hi, tile.t + 1)
            nc.vector.tensor_tensor(hs[1][:, tile.parity, :], h32[:, tile.parity, :],
                                    hs[0][:, tile.parity, :].bitcast(F32), ALU.subtract).then_inc(h_lo, 1)

        def step(tile, first, last):
            t, parity, k = tile
            n = [0]

            def done(ins):
                n[0] += 1
                ins.then_inc(dve_step, 1)
                dve.wait_ge(dve_step, STEPS * t + n[0])
            if not last:
                split_half(tile.after(), 0)
                split_half(tile.after(), 1)
            dve.wait_ge(half_done, 2 * t + 2)
            wait_for(dve, x1_saved[parity], 16 * k)
            done(nc.vector.tensor_tensor(x1[:, parity, :], ps_o[:, parity, :], gate_a[:, :], ALU.mult))
            dve.wait_ge(x_loaded[parity], 16 * (k + 1))
            nc.vector.tensor_tensor(x1[:, parity, :], x1[:, parity, :], xt[:, parity, :], ALU.add) \
              .then_inc(x1_ready, 1)
            dve.wait_ge(x1_ready, t + 1)
            done(nc.vector.bn_stats(stats[:, :], x1[:, parity, :]))
            if not first:
                split_h(tile.before())
            done(nc.vector.bn_aggr(mv[:, :], stats[:, :]))
            nc.vector.tensor_scalar(vare[:, :], mv[:, 1:2], LN_EPS, None, ALU.add).then_inc(var_ready, 1)
            dve.wait_ge(std_ready, t + 1)
            done(nc.vector.reciprocal(rstd[:, :], std[:, :]))
            if not first:
                dve.wait_ge(t_ready, t - 1)
            nc.vector.tensor_scalar(xn[:, parity, :], x1[:, parity, :], mv[:, 0:1], rstd[:, 0:1],
                                    ALU.subtract, ALU.mult).then_inc(xn_ready, 1)
            dve.wait_ge(xn_ready, t + 1)
        split_half(FIRST, 0)
        split_half(FIRST, 1)
        token_tiles(dve, step)
        split_h(LAST)

    @block.scalar
    def _(act):
        for n in range(H // RW):
            act.wait_ge(wo_loaded[n % 2], 16 * (n // 2 + 1))
            nc.scalar.activation(wo[0][:, n * RW:(n + 1) * RW, :], stage[:, n % 2, :, :], ACT.Copy) \
              .then_inc(wo_hi, 1)
            if n == 0:
                act.wait_ge(recip_t, 1)
                nc.scalar.activation(recipT[:, :, :], ps_r[:, 0, 0:2 * P].rearrange("p (a n) -> p a n", a=2),
                                     ACT.Copy).then_inc(recip_row, 1)

        def half_hi(tile, f):
            act.wait_ge(z_norm, 2 * tile.t + f + 1)
            if not is_first(tile):
                act.wait_ge(half_done, 2 * tile.t + f - 1)
            nc.scalar.activation(zs[0][:, f, :, :], zt[:, f, :, :], ACT.Copy).then_inc(z_hi, 1)

        def modulate(tile):
            t, parity, k = tile
            act.wait_ge(t_ready, t + 1)
            wait_for(act, h_saved[parity], 32 * k)
            for c in range(DC):
                nc.scalar.activation(h32[:, parity, c * P:(c + 1) * P], ps_t[:, parity, c * P:(c + 1) * P],
                                     ACT.Identity, bias=shift_b[:, c:c + 1], scale=scale_b[:, c:c + 1]) \
                  .then_inc(h_ready[parity], 1)
            act.wait_ge(h_ready[parity], DC * (k + 1))
            nc.scalar.activation(hs[0][:, parity, :], h32[:, parity, :], ACT.Copy).then_inc(h_hi, 1)

        def step(tile, first, last):
            if not last:
                half_hi(tile.after(), 0)
                half_hi(tile.after(), 1)
            if not first:
                modulate(tile.before())
            act.wait_ge(var_ready, tile.t + 1)
            nc.scalar.activation(std[:, :], vare[:, :], ACT.Sqrt).then_inc(std_ready, 1)
        half_hi(FIRST, 0)
        half_hi(FIRST, 1)
        token_tiles(act, step)
        modulate(LAST)

    @block.tensor
    def _(pe):
        pe.wait_ge(recip_ready, 1)
        for n in range(2):
            last = nc.tensor.transpose(ps_r[:, 0, n * P:(n + 1) * P], recip[:, n * P:(n + 1) * P], ident[:, :])
        last.then_inc(recip_t, 1)
        pe.wait_ge(wo_lo, H // RW)

        def transposes(tile):
            t, parity, k = tile
            pe.wait_ge(xn_ready, t + 1)
            wait_for(pe, h_ready[parity], DC * k)
            for c in range(DC):
                last = nc.tensor.transpose(ps_t[:, parity, c * P:(c + 1) * P], xn[:, parity, c * P:(c + 1) * P],
                                           ident[:, :])
            last.then_inc(t_ready, 1)

        def step(tile, first, last):
            t, parity, k = tile
            if not first:
                pe.wait_ge(x1_ready, t - 1)
            for f in range(2):
                pe.wait_ge(z_lo, 2 * t + f + 1)
                for n in range(HH):
                    h = f * HH + n
                    zz = [part[:, f, n, :] for part in zs]
                    w = [part[:, h, :] for part in wo]
                    mm = split_matmul(nc, ps_o[:, parity, :], zz, w, h == 0, h == H - 1)
                mm.then_inc(half_done, 1)
            if not first:
                transposes(tile.before())
        token_tiles(pe, step)
        transposes(LAST)


def gate_up(nc, ph, hbm, mid, hT_hi, hT_lo):
    def sb(name, shape, dt):
        return ph.enter_context(nc.sbuf_tensor(name, shape, dt))

    def sem(name):
        return ph.enter_context(nc.semaphore("g_" + name))

    hT = (hT_hi, hT_lo)
    w_raw = sb("g_wraw", [P, DC, 2, P], F32)
    w = [[sb(f"g_w{m}{n}", [P, DC, P], F32R) for n in ("hi", "lo")] for m in ("gate", "up")]
    sg = sb("g_silu", [P, NB, BT], F32)
    ps = [ph.enter_context(nc.psum_tensor(f"g_ps{m}", [P, NB, BT], F32)) for m in ("gate", "up")]
    w_loaded = sem("w_loaded")
    w_hi = sem("w_hi")
    w_lo = sem("w_lo")
    gate_ready = sem("gate_ready")
    up_ready = sem("up_ready")
    silu_ready = sem("silu_ready")
    mid_ready = sem("mid_ready")
    block = ph.enter_context(nc.Block())

    def feature_tiles(eng, step):
        step(0, False)
        with eng.Fori(1, NI - 1) as n:
            step(n, False)
        step(NI - 1, True)

    @block.sync
    def _(sp):
        def load(n):
            sp.dma_start(w_raw[:, :, :, :].rearrange("p c m n -> p (c m n)"),
                         hbm["wgu"][bass.ds(n, 1), :, :].rearrange("a p n -> (a p) n")).then_inc(w_loaded, 16)
        load(0)

        def step(n, last):
            if not last:
                sp.wait_ge(w_lo, 2 * n + 2)
                load(n + 1)
        feature_tiles(sp, step)

    @block.scalar
    def _(act):
        def hi(n, m):
            act.wait_ge(w_loaded, 16 * (n + 1))
            if not (isinstance(n, int) and n == 0):
                act.wait_ge((gate_ready, up_ready)[m], NB * n)
            nc.scalar.activation(w[m][0][:, :, :], w_raw[:, :, m, :], ACT.Copy).then_inc(w_hi, 1)

        def step(n, last):
            for b in range(NB):
                act.wait_ge(gate_ready, NB * n + b + 1)
                if b == 0:
                    wait_for(act, mid_ready, NB * n)
                nc.scalar.activation(sg[:, b, :], ps[0][:, b, :], ACT.Silu).then_inc(silu_ready, 1)
            if not last:
                hi(n + 1, 0)
                hi(n + 1, 1)

        hi(0, 0)
        hi(0, 1)
        feature_tiles(act, step)

    @block.vector
    def _(dve):
        def lo(n, m):
            dve.wait_ge(w_hi, 2 * n + m + 1)
            nc.vector.tensor_tensor(w[m][1][:, :, :], w_raw[:, :, m, :], w[m][0][:, :, :].bitcast(F32),
                                    ALU.subtract).then_inc(w_lo, 1)

        def step(n, last):
            if not last:
                lo(n + 1, 0)
            for b in range(NB):
                dve.wait_ge(up_ready, NB * n + b + 1)
                dve.wait_ge(silu_ready, NB * n + b + 1)
                dst = mid[:, bass.ds(n, 1), b * BT:(b + 1) * BT].rearrange("p a n -> p (a n)")
                nc.vector.tensor_tensor(dst, sg[:, b, :], ps[1][:, b, :], ALU.mult).then_inc(mid_ready, 1)
            if not last:
                lo(n + 1, 1)
        lo(0, 0)
        lo(0, 1)
        feature_tiles(dve, step)

    @block.tensor
    def _(pe):
        def step(n, last):
            for m in range(2):
                pe.wait_ge(w_lo, 2 * n + m + 1)
                for b in range(NB):
                    wait_for(pe, (silu_ready, mid_ready)[m], NB * n if b == 0 else 0)
                    for c in range(DC):
                        ww = [part[:, c, :] for part in w[m]]
                        hh = [part[:, c, b * BT:(b + 1) * BT] for part in hT]
                        mm = split_matmul(nc, ps[m][:, b, :], ww, hh, c == 0, c == DC - 1)
                    mm.then_inc((gate_ready, up_ready)[m], 1)
        feature_tiles(pe, step)


def down(nc, ph, hbm, mid, gate_b, hT_hi, hT_lo, out):
    def sb(name, shape, dt):
        return ph.enter_context(nc.sbuf_tensor(name, shape, dt))

    def sem(name):
        return ph.enter_context(nc.semaphore("d_" + name))

    wd = [part[:, :, :].rearrange("p c n -> p (c n)")[:, 0:NI * D] for part in (hT_hi, hT_lo)]
    stage = sb("d_stage", [P, 2, D], F32)
    ms = [sb(f"d_m{n}", [P, 2, NI, P], F32R) for n in ("hi", "lo")]
    x1 = sb("d_x1", [P, 2, D], F32)
    y = sb("d_y", [P, 2, D], F32)
    junk = sb("d_junk", [P, D], F32)
    ss = sb("d_ss", [P, 1], F32)
    ms_eps = sb("d_mse", [P, 1], F32)
    rms = sb("d_rms", [P, 1], F32)
    rrms = sb("d_rrms", [P, 1], F32)
    ps_y = ph.enter_context(nc.psum_tensor("d_psy", [P, 2, 512], F32))

    wd_loaded = [sem(f"wd_loaded{n}") for n in range(2)]
    wd_hi = sem("wd_hi")
    wd_lo = sem("wd_lo")
    m_hi = sem("m_hi")
    m_lo = sem("m_lo")
    y_ready = sem("y_ready")
    square_ready = sem("square_ready")
    rms_ready = sem("rms_ready")
    mean_ready = sem("mean_ready")
    dve_step = sem("dve_step")
    y_done = sem("y_done")
    x1_loaded = [sem(f"x1_loaded{n}") for n in range(2)]
    out_saved = [sem(f"out_saved{n}") for n in range(2)]
    STEPS = 2
    block = ph.enter_context(nc.Block())

    @block.sync
    def _(sp):
        for n in range(NI):
            if n >= 2:
                sp.wait_ge(wd_lo, n - 1)
            sp.dma_start(stage[:, n % 2, :], hbm["wdn"][n]).then_inc(wd_loaded[n % 2], 16)

        def load_x1(tile):
            if not is_first(tile):
                sp.wait_ge(y_done, tile.t - 1)
            sp.dma_start(x1[:, tile.parity, :], hbm["x1"][bass.ds(tile.t, 1), :, :].rearrange("a p d -> (a p) d")) \
              .then_inc(x1_loaded[tile.parity], 16)

        def step(tile, first, last):
            if not last:
                load_x1(tile.after())
            sp.wait_ge(y_done, tile.t + 1)
            sp.dma_start(out[rows_of(tile.t), :], y[:, tile.parity, :]).then_inc(out_saved[tile.parity], 16)
        load_x1(FIRST)
        token_tiles(sp, step)
        for n in range(2):
            sp.wait_ge(out_saved[n], 16 * NT // 2)

    @block.scalar
    def _(act):
        for n in range(NI):
            act.wait_ge(wd_loaded[n % 2], 16 * (n // 2 + 1))
            nc.scalar.activation(wd[0][:, n * D:(n + 1) * D], stage[:, n % 2, :], ACT.Copy).then_inc(wd_hi, 1)

        def step(tile, first, last):
            act.wait_ge(y_ready, tile.t + 1)
            if not first:
                act.wait_ge(mean_ready, tile.t)
            nc.scalar.activation(junk[:, :], ps_y[:, tile.parity, :], ACT.Square, accum_out=ss[:, :]) \
              .then_inc(square_ready, 1)
            act.wait_ge(mean_ready, tile.t + 1)
            nc.scalar.activation(rms[:, :], ms_eps[:, :], ACT.Sqrt).then_inc(rms_ready, 1)
        token_tiles(act, step)

    @block.vector
    def _(dve):
        def split(tile):
            if not is_first(tile):
                dve.wait_ge(y_ready, tile.t - 1)
            src = mid[:, :, rows_of(tile.t)]
            nc.vector.tensor_tensor(ms[0][:, tile.parity, :, :], src, src, ALU.max).then_inc(m_hi, 1)
            dve.wait_ge(m_hi, tile.t + 1)
            nc.vector.tensor_tensor(ms[1][:, tile.parity, :, :], src, ms[0][:, tile.parity, :, :].bitcast(F32),
                                    ALU.subtract).then_inc(m_lo, 1)

        def step(tile, first, last):
            t, parity, k = tile
            if not last:
                split(tile.after())
            dve.wait_ge(square_ready, t + 1)
            nc.vector.tensor_scalar(ms_eps[:, :], ss[:, :], 1.0 / D, RMS_EPS, ALU.mult, ALU.add) \
              .then_inc(mean_ready, 1)
            dve.wait_ge(rms_ready, t + 1)
            nc.vector.reciprocal(rrms[:, :], rms[:, :]).then_inc(dve_step, 1)
            dve.wait_ge(dve_step, STEPS * t + 1)
            wait_for(dve, out_saved[parity], 16 * k)
            nc.vector.scalar_tensor_tensor(out=y[:, parity, :], in0=ps_y[:, parity, :], scalar=rrms[:, 0:1],
                                           in1=gate_b[:, :], op0=ALU.mult, op1=ALU.mult).then_inc(dve_step, 1)
            dve.wait_ge(dve_step, STEPS * t + 2)
            dve.wait_ge(x1_loaded[parity], 16 * (k + 1))
            nc.vector.tensor_tensor(y[:, parity, :], y[:, parity, :], x1[:, parity, :], ALU.add).then_inc(y_done, 1)
        split(FIRST)
        for n in range(NI):
            dve.wait_ge(wd_hi, n + 1)
            nc.vector.tensor_tensor(wd[1][:, n * D:(n + 1) * D], stage[:, n % 2, :],
                                    wd[0][:, n * D:(n + 1) * D].bitcast(F32), ALU.subtract).then_inc(wd_lo, 1)
        token_tiles(dve, step)

    @block.tensor
    def _(pe):
        def step(tile, first, last):
            t, parity, k = tile
            pe.wait_ge(m_lo, t + 1)
            if not first:
                pe.wait_ge(y_done, t - 1)
            for n in range(NI):
                if first:
                    pe.wait_ge(wd_lo, n + 1)
                mt = [part[:, parity, n, :] for part in ms]
                w = [part[:, n * D:(n + 1) * D] for part in wd]
                mm = split_matmul(nc, ps_y[:, parity, :], mt, w, n == 0, n == NI - 1)
            mm.then_inc(y_ready, 1)
        token_tiles(pe, step)


def kernel(L0_attn_x, L0_attn_W_K, L0_attn_W_Q, L0_attn_W_V, L0_attn_W_O, L0_ffn_gate_up_packed,
           L0_ffn_gate_up_scales, L0_ffn_down_packed, L0_ffn_down_scales, L0_c, L0_wmod):
    import numpy as np
    import concourse.bacc as bacc
    from concourse.bass_utils import run_bass_kernel_spmd

    def a(v):
        return np.asarray(v)

    def heads(w):
        return a(w).reshape(H, DH, DC, P).transpose(0, 3, 2, 1).reshape(H, P, 1, DC * DH)

    gu = a(L0_ffn_gate_up_packed).reshape(2, NI, P, DC, WORDS)
    gus = a(L0_ffn_gate_up_scales).reshape(DC, 2, NI, P)
    arrays = {
        "x": a(L0_attn_x).reshape(S, D),
        "w_qkv": np.concatenate([heads(w) for w in (L0_attn_W_Q, L0_attn_W_K, L0_attn_W_V)], axis=2),
        "w_o": a(L0_attn_W_O).reshape(D, H, P).transpose(2, 1, 0),
        "gu_packed": gu.transpose(1, 3, 4, 0, 2).reshape(NI, DC, WORDS, 2 * P),
        "gu_scales": gus.transpose(2, 0, 1, 3).reshape(NI, 2, D),
        "dn_packed": a(L0_ffn_down_packed).reshape(D, NI, WORDS).transpose(1, 2, 0),
        "dn_scales": a(L0_ffn_down_scales),
        "c_cols": a(L0_c).reshape(DC, P).transpose(1, 0),
        "w_mod": a(L0_wmod),
    }
    nc = bacc.Bacc("TRN2", target_bir_lowering=False, num_devices=1)
    ins = {}
    arrays = {n: np.ascontiguousarray(v) for n, v in arrays.items()}
    for n, v in arrays.items():
        ins[n] = nc.dram_tensor("in_" + n, v.shape, mybir.dt.from_np(v.dtype), kind="ExternalInput").ap()
    out = nc.dram_tensor("out_x", [S, D], F32, kind="ExternalOutput").ap()
    adaln_kernel(nc, out=out, **ins)
    r = run_bass_kernel_spmd(nc, [{"in_" + n: v for n, v in arrays.items()}], core_ids=[0])
    return r.results[0]["out_x"].reshape(1, S, D)
```

```python
from contextlib import ExitStack
from typing import NamedTuple

import concourse.bass as bass
from concourse import mybir

F32 = mybir.dt.float32
F32R = mybir.dt.float32r
BF16 = mybir.dt.bfloat16
F16 = mybir.dt.float16
I32 = mybir.dt.int32
ALU = mybir.AluOpType
ACT = mybir.ActivationFunctionType
AX_X = mybir.AxisListType.X

P = 128
S, D = 2048, 512
H, DH = 16, 128
INTER = 1408
DC = D // P
NT = S // P
BT = 512
NB = S // BT
TPB = BT // P
NI = INTER // P
NPAIR = NT // 2
WORDS = P // 8
LN_EPS, RMS_EPS = 1e-5, 1e-6
SOFT = DH ** -0.5
MASKED = 1e10 * SOFT


def n_chunks(i):
    return i // TPB + 1


def chunks_before(i):
    return sum(n_chunks(j) for j in range(i))


CHUNKS = chunks_before(NT)
MULTI = sum(n_chunks(i) for i in range(NT) if n_chunks(i) > 1)



def unit(kind, b):
    return [("P", kind, b, c) for c in range(1 if kind == "VT" else DC)]


def pair(b, lo, hi):
    return [("Z", b, k) for k in range(lo, hi, 2)]


FILL = [
    pair(6, 8, 14) + unit("V", 0),
    pair(7, 0, 4) + unit("VT", 0) + pair(7, 4, 8) + unit("K", 1)[:2],
    unit("K", 1)[2:] + pair(7, 8, 14) + unit("Q", 1)[:2],
    unit("Q", 1)[2:] + pair(7, 14, 16) + pair(0, 0, 2),
    unit("V", 1),
    unit("VT", 1) + pair(1, 0, 4) + unit("K", 2)[:2],
    unit("K", 2)[2:],
    unit("Q", 2) + pair(2, 0, 4),
    pair(2, 4, 6) + unit("V", 2),
    unit("VT", 2) + pair(3, 0, 8),
    unit("K", 3),
    unit("Q", 3) + pair(4, 0, 6),
    pair(4, 6, 10) + unit("V", 3),
    unit("VT", 3) + pair(5, 0, 8),
    pair(5, 8, 12) + unit("Qnext", 0),
    unit("Knext", 0) + pair(6, 0, 8),
]
T_AFTER = (0, 1, 2, 4)


def body(i):
    tile = (i - 1) % NT
    transposes = [(T_AFTER[u], ("T", tile, u)) for u in range(n_chunks(tile))]
    ops = []
    for n, op in enumerate(FILL[i] + [None]):
        while transposes and (transposes[0][0] <= n or op is None):
            ops.append(transposes.pop(0)[1])
        if op:
            ops.append(op)
    return ops


BODY = [body(i) for i in range(NT)]


def of_previous(i, op):
    return (op[0] == "T" and op[1] == NT - 1) or (op[0] == "Z" and op[1] >= NPAIR - 2 and i < 4)


def of_next(op):
    return op[0] == "P" and op[1].endswith("next")


def pieces(i, first, last):
    return [(op, of_previous(i, op)) for op in BODY[i]
            if not (first and of_previous(i, op)) and not (last and of_next(op))]


TAIL = [op for i in range(4) for op in BODY[i] if of_previous(i, op)]


def ends(op):
    if op[0] == "P":
        return op[1] == "VT" or op[3] == DC - 1
    return op[0] == "Z" and op[2] == 2 * op[1]


UNITS = [op[1:3] for ops in BODY for op in ops if op[0] == "P" and ends(op)]
UNIT_AT = {u: n for n, u in enumerate(UNITS)}
SPLIT_UNITS = [u for u in UNITS if u[0] != "V"]
SPLIT_AT = {u: n for n, u in enumerate(SPLIT_UNITS)}
NU, NSU = len(UNITS), len(SPLIT_UNITS)
PREU = 2
MATS = ("Q", "K", "V")
SPLIT_ORDER = ("K", "Q", "V")
UNPACK_STEP = {2: 0, 7: 1, 12: 2}
EXP_AFTER = 1
PIECES = 3


class Tile(NamedTuple):
    t: object
    parity: int
    k: object

    def before(self):
        return Tile(self.t - 1, 1 - self.parity, self.k if self.parity else self.k - 1)

    def after(self):
        return Tile(self.t + 1, 1 - self.parity, self.k + self.parity)


def token_tiles(eng, step):
    for t in range(3):
        step(Tile(t, t % 2, t // 2), t == 0, False)
    with eng.Fori(1, NT // 2 - 1) as u:
        step(Tile(u * 2 + 1, 1, u), False, False)
        step(Tile(u * 2 + 2, 0, u + 1), False, False)
    step(Tile(NT - 1, 1, NT // 2 - 1), False, True)


def rows_of(t):
    return bass.ds(t * P, P)


FIRST, LAST = Tile(0, 0, 0), Tile(NT - 1, 1, NT // 2 - 1)


def is_first(tile):
    return isinstance(tile.t, int) and tile.t == 0


def split_matmul(nc, dst, stat, mov, start, stop):
    nc.tensor.matmul(dst, stat[0], mov[0], start=start, stop=False)
    nc.tensor.matmul(dst, stat[0], mov[1], start=False, stop=False)
    return nc.tensor.matmul(dst, stat[1], mov[0], start=False, stop=stop)


def wait_for(eng, sem, value):
    if not isinstance(value, int) or value > 0:
        eng.wait_ge(sem, value)


def adaln_kernel(nc, x, w_qkv, w_o, gu_packed, gu_scales, dn_packed, dn_scales, c_cols, w_mod, out):
    with ExitStack() as whole:
        hbm = {}
        for name, shape in (("zT", [H, P, S]), ("sums", [H, P, NT]), ("recips", [2 * P, P]),
                            ("wgu", [NI, P, DC * 2 * P]), ("wdn", [NI, P, D]), ("x1", [NT, P, D])):
            hbm[name] = nc.dram_tensor("scratch_" + name, shape, F32).ap()

        def sb(name, shape, dt, ctx=whole):
            return ctx.enter_context(nc.sbuf_tensor(name, shape, dt))

        ident = sb("ident", [P, P], F32)
        ident_bf = sb("ident_bf", [P, P], BF16)
        gate_a = sb("gate_a", [P, D], F32)
        gate_b = sb("gate_b", [P, D], F32)
        shift_a = sb("shift_a", [P, DC], F32)
        scale_a = sb("scale_a", [P, DC], F32)
        shift_b = sb("shift_b", [P, DC], F32)
        scale_b = sb("scale_b", [P, DC], F32)
        nib_shift = sb("nib_shift", [P, 1], I32)
        hT_hi = sb("hT_hi", [P, DC, S], F32R)
        hT_lo = sb("hT_lo", [P, DC, S], F32R)

        with ExitStack() as ph:
            prologue(nc, ph, x, c_cols, w_mod, ident, ident_bf, gate_a, gate_b, shift_a, scale_a,
                     shift_b, scale_b, nib_shift, hT_hi, hT_lo)
        with ExitStack() as ph:
            attention(nc, ph, hbm, w_qkv, gu_packed, gu_scales, dn_packed, dn_scales, ident,
                      ident_bf, nib_shift, hT_hi, hT_lo)
        with ExitStack() as ph:
            output_projection(nc, ph, hbm, x, w_o, ident, gate_a, shift_b, scale_b, hT_hi, hT_lo)
        with ExitStack() as ph:
            mid = sb("midT", [P, NI, S], F32, ph)
            with ExitStack() as ph2:
                gate_up(nc, ph2, hbm, mid, hT_hi, hT_lo)
            with ExitStack() as ph2:
                down(nc, ph2, hbm, mid, gate_b, hT_hi, hT_lo, out)


def prologue(nc, ph, x, c_cols, w_mod, ident, ident_bf, gate_a, gate_b, shift_a, scale_a, shift_b,
             scale_b, nib_shift, hT_hi, hT_lo):
    def sb(name, shape, dt):
        return ph.enter_context(nc.sbuf_tensor(name, shape, dt))

    def sem(name):
        return ph.enter_context(nc.semaphore(name))

    SECTIONS = 6
    xt = sb("p_x", [P, NB, TPB, D], F32)
    wm = sb("p_wmod", [P, 3, DC, D], F32)
    c_in = sb("p_c", [P, DC], F32)
    c_silu = sb("p_csilu", [P, DC], F32)
    c_wide = sb("p_cwide", [P, DC, P], F32)
    ones = sb("p_ones", [P, P], F32)
    rows = sb("p_rows", [P, 2, D], F32)
    absr = sb("p_absr", [P, 2, D], F32)
    stats = sb("p_stats", [P, NT, 6], F32)
    mv = sb("p_mv", [P, NT, 2], F32)
    vare = sb("p_vare", [P, NT], F32)
    std = sb("p_std", [P, NT], F32)
    rstd = sb("p_rstd", [P, NT], F32)
    xn = sb("p_xn", [P, TPB, D], F32)
    h32 = sb("p_h32", [P, 2, BT], F32)
    pidx = sb("p_idx", [P, 1], I32)
    ps_mod = ph.enter_context(nc.psum_tensor("p_psmod", [P, 2, D], F32))
    ps_col = ph.enter_context(nc.psum_tensor("p_pscol", [P, 2, D], F32))
    ps_t = ph.enter_context(nc.psum_tensor("p_pst", [P, 4, BT], F32))

    c_loaded = sem("p_c_loaded")
    x_loaded = [sem(f"p_x_loaded{b}") for b in range(NB)]
    wm_loaded = [sem(f"p_wm_loaded{b}") for b in range(SECTIONS)]
    const_zeroed = sem("p_const_zeroed")
    const_ready = sem("p_const_ready")
    c_ready = sem("p_c_ready")
    wide_ready = sem("p_wide_ready")
    mod_ready = sem("p_mod_ready")
    row_ready = sem("p_row_ready")
    col_ready = sem("p_col_ready")
    mod_used = sem("p_mod_used")
    gate_step = sem("p_gate_step")
    dve_step = sem("p_dve_step")
    var_ready = sem("p_var_ready")
    std_ready = sem("p_std_ready")
    xn_ready = sem("p_xn_ready")
    t_ready = sem("p_t_ready")
    h_ready = sem("p_h_ready")
    hi_ready = sem("p_hi_ready")
    lo_ready = sem("p_lo_ready")
    idx_step = sem("p_idx_step")

    cols = {0: shift_a, 1: scale_a, 3: shift_b, 4: scale_b}
    col_number = {s: n for n, s in enumerate(cols)}
    rows_kept = {2: gate_a, 5: gate_b}
    block = ph.enter_context(nc.Block())

    @block.sync
    def _(sp):
        sp.dma_start(c_in[:, :], c_cols).then_inc(c_loaded, 16)
        def load_x(b):
            sp.dma_start(xt[:, b, :, :], x[b * BT:(b + 1) * BT, :].rearrange("(t p) d -> p t d", p=P)) \
              .then_inc(x_loaded[b], 16)
        def load_w(s):
            if s >= 3:
                sp.wait_ge(mod_ready, s - 2)
            sp.dma_start(wm[:, s % 3, :, :], w_mod[:, s * D:(s + 1) * D].rearrange("(c p) d -> p c d", p=P)) \
              .then_inc(wm_loaded[s], 16)
        load_x(0)
        load_w(0)
        load_w(1)
        for b in range(1, NB):
            load_x(b)
        for s in range(2, SECTIONS):
            load_w(s)

    @block.gpsimd
    def _(pool):
        nc.gpsimd.memset(ident[:, :], 0.0).then_inc(const_zeroed, 1)
        nc.gpsimd.memset(ident_bf[:, :], 0.0).then_inc(const_zeroed, 1)
        nc.gpsimd.memset(ones[:, :], 1.0).then_inc(const_ready, 1)
        pool.wait_ge(const_zeroed, 2)
        for m in (ident, ident_bf):
            nc.gpsimd.affine_select(out=m[:, :], in_=m[:, :], compare_op=ALU.not_equal, fill=1.0, base=0,
                                    pattern=[[-1, P]], channel_multiplier=1).then_inc(const_ready, 1)
        nc.gpsimd.iota(pidx[:, :], pattern=[[0, 1]], base=0, channel_multiplier=1).then_inc(const_ready, 1)

    @block.scalar
    def _(act):
        act.wait_ge(c_loaded, 16)
        nc.scalar.activation(c_silu[:, :], c_in[:, :], ACT.Silu).then_inc(c_ready, 1)

        def copy_row(s):
            act.wait_ge(mod_ready, s + 1)
            if s in cols:
                n = col_number[s]
                if n >= 2:
                    act.wait_ge(col_ready, n - 1)
                nc.scalar.activation(rows[:, n % 2, :], ps_mod[:, s % 2, :], ACT.Copy).then_inc(row_ready, 1)
        copy_row(0)
        copy_row(1)
        for b in range(NB):
            for s in range(b, min(b + 2, NB)) if b == 0 else range(b + 1, min(b + 2, NB)):
                act.wait_ge(var_ready, s + 1)
                nc.scalar.activation(std[:, s * TPB:(s + 1) * TPB], vare[:, s * TPB:(s + 1) * TPB], ACT.Sqrt) \
                  .then_inc(std_ready, 1)
            for c in range(DC):
                n = b * DC + c
                act.wait_ge(t_ready, n + 1)
                if n == 0:
                    act.wait_ge(mod_used, 2)
                if n >= 2:
                    act.wait_ge(lo_ready, n - 1)
                nc.scalar.activation(h32[:, n % 2, :], ps_t[:, n % 4, :], ACT.Identity,
                                     bias=shift_a[:, c:c + 1], scale=scale_a[:, c:c + 1]).then_inc(h_ready, 1)
                act.wait_ge(h_ready, n + 1)
                nc.scalar.activation(hT_hi[:, c, b * BT:(b + 1) * BT], h32[:, n % 2, :], ACT.Copy) \
                  .then_inc(hi_ready, 1)
        for s in (3, 4):
            copy_row(s)

    @block.vector
    def _(dve):
        dve.wait_ge(const_ready, 4)
        nc.vector.tensor_scalar(pidx[:, :], pidx[:, :], 7, 2, ALU.bitwise_and, ALU.logical_shift_left) \
          .then_inc(idx_step, 1)
        dve.wait_ge(idx_step, 1)
        nc.vector.tensor_copy(nib_shift[:, :], pidx[:, :]).then_inc(idx_step, 1)
        dve.wait_ge(c_ready, 1)
        for c in range(DC):
            nc.vector.tensor_scalar(c_wide[:, c, :], ones[:, :], c_silu[:, c:c + 1], None, ALU.mult) \
              .then_inc(wide_ready, 1)
        steps = [0]

        def done(ins):
            ins.then_inc(dve_step, 1)
            steps[0] += 1
            dve.wait_ge(dve_step, steps[0])

        def normalise(b):
            dve.wait_ge(x_loaded[b], 16)
            for t in range(b * TPB, (b + 1) * TPB):
                last = nc.vector.bn_stats(stats[:, t, :], xt[:, b, t % TPB, :])
            done(last)
            for t in range(b * TPB, (b + 1) * TPB):
                last = nc.vector.bn_aggr(mv[:, t, :], stats[:, t, :])
            done(last)
            blk = slice(b * TPB, (b + 1) * TPB)
            nc.vector.tensor_scalar(vare[:, blk], mv[:, blk, 1], LN_EPS, None, ALU.add).then_inc(var_ready, 1)
            dve.wait_ge(std_ready, b + 1)
            done(nc.vector.reciprocal(rstd[:, blk], std[:, blk]))
            if b:
                dve.wait_ge(t_ready, DC * b)
            for t in range(TPB):
                n = b * TPB + t
                nc.vector.tensor_scalar(xn[:, t, :], xt[:, b, t, :], mv[:, n, 0:1], rstd[:, n:n + 1],
                                        ALU.subtract, ALU.mult).then_inc(xn_ready, 1)

        def use_section(s):
            if s in cols:
                n = col_number[s]
                dve.wait_ge(col_ready, n + 1)
                src = ps_col[:, n % 2, :].rearrange("p (c k) -> p c k", c=DC)[:, :, 0]
                nc.vector.tensor_scalar(cols[s][:, :], src, 1.0 if s in (1, 4) else 0.0, None, ALU.add) \
                  .then_inc(mod_used, 1)
            else:
                dve.wait_ge(mod_ready, s + 1)
                g = ps_mod[:, s % 2, :]
                nc.vector.tensor_scalar(absr[:, 0, :], g, 0.0, 2.0, ALU.is_ge, ALU.mult).then_inc(gate_step, 1)
                nc.vector.tensor_scalar(absr[:, 1, :], g, -1.0, 0.25, ALU.mult, ALU.max).then_inc(gate_step, 1)
                dve.wait_ge(gate_step, 2 if s == 2 else 5)
                nc.vector.tensor_tensor(absr[:, 1, :], g, absr[:, 1, :], ALU.max).then_inc(gate_step, 1)
                dve.wait_ge(gate_step, 3 if s == 2 else 6)
                nc.vector.scalar_tensor_tensor(out=rows_kept[s][:, :], in0=absr[:, 0, :], scalar=-1.0,
                                               in1=absr[:, 1, :], op0=ALU.add, op1=ALU.mult) \
                  .then_inc(mod_used, 1)
                dve.wait_ge(mod_used, s + 1)

        def split(b):
            for c in range(DC):
                n = b * DC + c
                dve.wait_ge(hi_ready, n + 1)
                nc.vector.tensor_tensor(hT_lo[:, c, b * BT:(b + 1) * BT], h32[:, n % 2, :],
                                        hT_hi[:, c, b * BT:(b + 1) * BT].bitcast(F32), ALU.subtract) \
                  .then_inc(lo_ready, 1)
        normalise(0)
        use_section(0)
        use_section(1)
        for b in range(1, NB):
            normalise(b)
            split(b - 1)
        split(NB - 1)
        for s in range(2, SECTIONS):
            use_section(s)

    @block.tensor
    def _(pe):
        pe.wait_ge(const_ready, 4)
        pe.wait_ge(wide_ready, DC)

        def mod_section(s):
            if s >= 2:
                pe.wait_ge(mod_used, s - 1)
                if s - 2 in cols:
                    pe.wait_ge(row_ready, col_number[s - 2] + 1)
            pe.wait_ge(wm_loaded[s], 16)
            for c in range(DC):
                last = nc.tensor.matmul(ps_mod[:, s % 2, :], c_wide[:, c, :], wm[:, s % 3, c, :],
                                        start=(c == 0), stop=(c == DC - 1))
            last.then_inc(mod_ready, 1)

        def to_columns(s):
            n = col_number[s]
            pe.wait_ge(row_ready, n + 1)
            if n >= 2:
                pe.wait_ge(mod_used, n - 1)
            for c in range(DC):
                last = nc.tensor.transpose(ps_col[:, n % 2, c * P:(c + 1) * P],
                                           rows[:, n % 2, c * P:(c + 1) * P], ident[:, :])
            last.then_inc(col_ready, 1)

        mod_section(0)
        mod_section(1)
        to_columns(0)
        to_columns(1)
        for b in range(NB):
            pe.wait_ge(xn_ready, (b + 1) * TPB)
            for c in range(DC):
                n = b * DC + c
                if n >= 4:
                    pe.wait_ge(h_ready, n - 3)
                for t in range(TPB):
                    last = nc.tensor.transpose(ps_t[:, n % 4, t * P:(t + 1) * P],
                                               xn[:, t, c * P:(c + 1) * P], ident[:, :])
                last.then_inc(t_ready, 1)
        for s in (2, 3):
            mod_section(s)
        to_columns(3)
        mod_section(4)
        to_columns(4)
        mod_section(5)


def attention(nc, ph, hbm, w_qkv, gu_packed, gu_scales, dn_packed, dn_scales, ident, ident_bf,
              nib_shift, hT_hi, hT_lo):
    def sb(name, shape, dt):
        return ph.enter_context(nc.sbuf_tensor(name, shape, dt))

    def sem(name):
        return ph.enter_context(nc.semaphore(name))

    ZBUF = 4
    causal = sb("causal", [P, P], BF16)
    zeros = sb("zeros", [P, P], F32)
    w_raw = sb("w_raw", [P, 3, DC * DH], F32)
    w_hi = sb("w_hi", [P, 3, DC * DH], F32R)
    w_lo = sb("w_lo", [P, 3, DC * DH], F32R)
    kT = [sb(f"kT_{n}", [P, S], F32R) for n in ("hi", "lo")]
    qT = [sb(f"qT_{n}", [P, 2, BT], F32R) for n in ("hi", "lo")]
    v = [sb(f"v_{n}", [P, NT, DH], F32R) for n in ("hi", "lo")]
    vT = sb("vT", [P, BT], F32)
    probs = sb("probs", [P, 2, S], F32)
    pT = [sb(f"pT_{n}", [P, 3, NT * P], F32R) for n in ("hi", "lo")]
    z = sb("z", [P, ZBUF, 2 * P], F32)
    cmin = sb("cmin", [P, NB], F32)
    rmin = sb("rmin", [P, 2], F32)
    sums = sb("sums", [P, NT], F32)
    words = sb("words", [P, D], I32)
    code = sb("code", [P, D], I32)
    deq_a = sb("deq_a", [P, D], F32)
    deq_b = sb("deq_b", [P, D], F32)
    qscale = sb("qscale", [P, D], F16)
    halves = sb("halves", [P, 1], F32)
    ps_s = ph.enter_context(nc.psum_tensor("ps_s", [P, NB, BT], F32))
    ps_t = ph.enter_context(nc.psum_tensor("ps_t", [P, 2, BT], F32))
    ps_z = ph.enter_context(nc.psum_tensor("ps_z", [P, 512], F32))
    ps_p = ph.enter_context(nc.psum_tensor("ps_p", [P, BT], F32))

    w_loaded = sem("w_loaded")
    w_split = sem("w_split")
    consts = sem("consts")
    scores_ready = sem("scores_ready")
    chunk_min = sem("chunk_min")
    min_ready = sem("min_ready")
    exp_ready = sem("exp_ready")
    t_ready = sem("t_ready")
    t_hi = sem("t_hi")
    t_lo = sem("t_lo")
    proj_ready = sem("proj_ready")
    proj_hi = sem("proj_hi")
    proj_lo = sem("proj_lo")
    zero_ready = sem("zero_ready")
    z_ready = sem("z_ready")
    z_copied = sem("z_copied")
    z_saved = [sem(f"z_saved{n}") for n in range(ZBUF)]
    sums_saved = [sem(f"sums_saved{n}") for n in range(2)]
    words_loaded = sem("words_loaded")
    qscale_loaded = sem("qscale_loaded")
    unpacked = sem("unpacked")
    deq_step = sem("deq_step")
    deq_saved = sem("deq_saved")

    Z_DMAS = (1, 2)
    DEQ_OPS = 9
    LOADS = {0: 2, 1: 2, 2: 1}
    LOADS_BEFORE = {0: 0, 1: 2, 2: 4}
    LOADS_ALL = 5

    block = ph.enter_context(nc.Block())
    stretches = [(1, NI), (NI, H - 1)]

    @block.sync
    def _(sp):
        sp.dma_start(w_raw[:, :, :], w_qkv[0]).then_inc(w_loaded, 16)

        def load_piece(h, k):
            sp.wait_ge(deq_step, DEQ_OPS * (PIECES * h + k)) if not (isinstance(h, int) and h + k == 0) else None
            if k < 2:
                for c in range(2):
                    src = gu_packed[bass.ds(h, 1), 2 * k + c, :, :]
                    sp.dma_start(words[:, c * 2 * P:(c + 1) * 2 * P],
                                 replicate(src, 2 * P)).then_inc(words_loaded, 16)
                sp.dma_start(qscale[:, :], gu_scales[bass.ds(h, 1), k, :].to_broadcast([P, D])) \
                  .then_inc(qscale_loaded, 16)
            else:
                sp.dma_start(words[:, :], replicate(dn_packed[bass.ds(h, 1), :, :], D)).then_inc(words_loaded, 16)
                sp.dma_start(qscale[:, :], dn_scales[bass.ds(h, 1), :].to_broadcast([P, D])) \
                  .then_inc(qscale_loaded, 16)

        def replicate(src, n):
            a = src.rearrange("a w n -> (a w) n")
            return a.unsqueeze(1).to_broadcast([WORDS, 8, n])

        def save_piece(h, k):
            sp.wait_ge(deq_step, DEQ_OPS * (PIECES * h + k + 1))
            if k < 2:
                dst = hbm["wgu"][bass.ds(h, 1), :, k * D:(k + 1) * D].rearrange("a p n -> (a p) n")
            else:
                dst = hbm["wdn"][bass.ds(h, 1), :, :].rearrange("a p n -> (a p) n")
            sp.dma_start(dst, deq_a[:, :]).then_inc(deq_saved, 16)

        def save_z(h, b):
            sp.wait_ge(z_copied, NPAIR * h + b + 1)
            dst = hbm["zT"][bass.ds(h, 1), :, b * 2 * P:(b + 1) * 2 * P].rearrange("a p n -> (a p) n")
            n = b % ZBUF
            if b % 2 == 0:
                sp.dma_start(dst, z[:, n, :]).then_inc(z_saved[n], 16)
            else:
                sp.dma_start(dst[:, P:2 * P], z[:, n, 0:P]).then_inc(z_saved[n], 16)
                sp.dma_start(dst[:, 0:P], z[:, n, P:2 * P]).then_inc(z_saved[n], 16)

        def save_sums(h, half):
            sp.wait_ge(exp_ready, NT * h + (half + 1) * NT // 2)
            cols = slice(half * NT // 2, (half + 1) * NT // 2)
            sp.dma_start(hbm["sums"][bass.ds(h, 1), :, cols].rearrange("a p n -> (a p) n"), sums[:, cols]) \
              .then_inc(sums_saved[half], 16)

        def head(h, decode, first, last):
            if not last:
                sp.wait_ge(w_split, 6 * (h + 1))
                sp.dma_start(w_raw[:, :, :], w_qkv[bass.ds(h + 1, 1), :, :, :].rearrange("a p m n -> (a p) m n")) \
                  .then_inc(w_loaded, 16)
            if decode:
                load_piece(h, 0)
            if not first:
                save_z(h - 1, NPAIR - 2)
                save_z(h - 1, NPAIR - 1)
            save_z(h, 0)
            if decode:
                save_piece(h, 0)
                load_piece(h, 1)
            save_z(h, 1)
            save_z(h, 2)
            if decode:
                save_piece(h, 1)
                load_piece(h, 2)
            save_sums(h, 0)
            for b in range(3, NPAIR - 2):
                save_z(h, b)
            if decode:
                save_piece(h, 2)
            save_sums(h, 1)
        head(0, True, True, False)
        for n, (a, z_) in enumerate(stretches):
            with sp.Fori(a, z_) as h:
                head(h, n == 0, False, False)
        head(H - 1, False, False, True)
        save_z(H - 1, NPAIR - 2)
        save_z(H - 1, NPAIR - 1)
        for n in range(ZBUF):
            sp.wait_ge(z_saved[n], Z_DMAS[n % 2] * 16 * H * NPAIR // ZBUF)
        for n in range(2):
            sp.wait_ge(sums_saved[n], 16 * H)
        sp.wait_ge(deq_saved, 16 * PIECES * NI)

    @block.gpsimd
    def _(pool):
        nc.gpsimd.memset(zeros[:, :], 0.0).then_inc(consts, 1)
        nc.gpsimd.memset(halves[:, :], 0.5).then_inc(consts, 1)
        pool.wait_ge(consts, 2)
        nc.gpsimd.affine_select(out=causal[:, :], in_=zeros[:, :], compare_op=ALU.is_ge, fill=MASKED, base=0,
                                pattern=[[-1, P]], channel_multiplier=1).then_inc(consts, 1)

        def split_weights(h, m, n):
            if n == 0:
                pool.wait_ge(w_loaded, 16 * (h + 1))
            if not (isinstance(h, int) and h == 0):
                pool.wait_ge(proj_ready, PREU + NU * (h - 1) + UNIT_AT[(MATS[m], NB - 1)] + 1)
            nc.gpsimd.tensor_tensor(w_hi[:, m, :], w_raw[:, m, :], zeros[:, 0:1].to_broadcast([P, DC * DH]), ALU.add) \
              .then_inc(w_split, 1)
            pool.wait_ge(w_split, 6 * h + 2 * n + 1)
            nc.gpsimd.tensor_tensor(w_lo[:, m, :], w_raw[:, m, :], w_hi[:, m, :].bitcast(F32), ALU.subtract) \
              .then_inc(w_split, 1)

        def zero_block(h, b):
            if not (isinstance(h, int) and NPAIR * h + b < 2):
                pool.wait_ge(z_ready, NPAIR * h + b - 1)
            for part in pT:
                nc.gpsimd.tensor_tensor(part[:, 2 * (b % 2), (2 * b + 1) * P:(2 * b + 2) * P],
                                        zeros[:, :], zeros[:, :], ALU.add).then_inc(zero_ready, 1)

        def decode_piece(h, k):
            base = PIECES * h + k
            made = DEQ_OPS * base
            halves_wide = halves[:, 0:1].to_broadcast([P, D])
            code_f, sign_f = code[:, :].bitcast(F32), words[:, :].bitcast(F32)
            pool.wait_ge(unpacked, 3 * (base + 1))
            pool.wait_ge(qscale_loaded, 16 * (base + 1))
            wait_for(pool, deq_saved, 16 * base)
            wait_for(pool, deq_step, made)
            nc.gpsimd.tensor_tensor(deq_b[:, :], qscale[:, :], halves_wide, ALU.mult).then_inc(deq_step, 1)
            nc.gpsimd.tensor_scalar(sign_f, words[:, :], -0.25, 1.0, ALU.mult, ALU.add).then_inc(deq_step, 1)
            nc.gpsimd.tensor_scalar(deq_a[:, :], code[:, :], 4.0, -16.0, ALU.max, ALU.add).then_inc(deq_step, 1)
            pool.wait_ge(deq_step, made + 3)
            nc.gpsimd.tensor_tensor(sign_f, sign_f, deq_b[:, :], ALU.mult).then_inc(deq_step, 1)
            nc.gpsimd.tensor_scalar(code_f, code[:, :], 1.0, None, ALU.mult).then_inc(deq_step, 1)
            pool.wait_ge(deq_step, made + 5)
            nc.gpsimd.tensor_tensor(deq_a[:, :], deq_a[:, :], code_f, ALU.add).then_inc(deq_step, 1)
            nc.gpsimd.tensor_scalar(deq_b[:, :], code_f, 6.0, 2.0, ALU.max, ALU.mult).then_inc(deq_step, 1)
            pool.wait_ge(deq_step, made + 7)
            nc.gpsimd.tensor_tensor(deq_a[:, :], deq_a[:, :], deq_b[:, :], ALU.add).then_inc(deq_step, 1)
            pool.wait_ge(deq_step, made + 8)
            nc.gpsimd.tensor_tensor(deq_a[:, :], deq_a[:, :], sign_f, ALU.mult).then_inc(deq_step, 1)

        def head(h, decode, last):
            for b in range(3):
                zero_block(h, b)
            if decode:
                decode_piece(h, 0)
            zero_block(h, 3)
            if decode:
                decode_piece(h, 1)
            zero_block(h, 4)
            if not last:
                split_weights(h + 1, MATS.index("K"), 0)
            zero_block(h, 5)
            if not last:
                split_weights(h + 1, MATS.index("Q"), 1)
            zero_block(h, 6)
            if not last:
                split_weights(h + 1, MATS.index("V"), 2)
            if decode:
                decode_piece(h, 2)
            zero_block(h, 7)
        for n, m in enumerate(SPLIT_ORDER):
            split_weights(0, MATS.index(m), n)
        head(0, True, False)
        for n, (a, z_) in enumerate(stretches):
            with pool.Fori(a, z_) as h:
                head(h, n == 0, False)
        head(H - 1, False, True)

    @block.tensor
    def _(pe):
        def project(h, kind, b, c):
            unit = (kind, b)
            if c:
                pass
            elif h is None:
                nth = {"Q": 0, "K": 1}[kind]
                if nth:
                    pe.wait_ge(proj_lo, nth)
            else:
                nth = UNIT_AT[unit]
                prev = UNITS[nth - 1] if nth else None
                if prev and prev[0] == "V":
                    pe.wait_ge(proj_hi, PREU + NU * h + nth)
                else:
                    pe.wait_ge(proj_lo, PREU + NSU * h + (SPLIT_AT[prev] + 1 if prev else 0))
            if kind == "VT":
                if prev[0] != "V":
                    pe.wait_ge(proj_hi, PREU + NU * h + UNIT_AT[("V", b)] + 1)
                for t in range(TPB):
                    last = nc.tensor.transpose(ps_p[:, t * P:(t + 1) * P], vT[:, t * P:(t + 1) * P], ident[:, :])
            else:
                m = MATS.index(kind[0])
                if c:
                    pass
                elif h is None:
                    pe.wait_ge(w_split, 2 * SPLIT_ORDER.index(kind) + 2)
                elif b == 0:
                    pe.wait_ge(w_split, 6 * (h if kind == "V" else h + 1) + 2 * SPLIT_ORDER.index(kind[0]) + 2)
                w = [part[:, m, c * DH:(c + 1) * DH] for part in (w_hi, w_lo)]
                ht = [part[:, c, b * BT:(b + 1) * BT] for part in (hT_hi, hT_lo)]
                last = split_matmul(nc, ps_p[:, :], w, ht, c == 0, c == DC - 1)
            if kind == "VT" or c == DC - 1:
                last.then_inc(proj_ready, 1)

        def lo_count(h, unit):
            if unit[0] in ("Q", "K") and unit[1] == 0:
                return PREU + NSU * h
            return PREU + NSU * h + SPLIT_AT[unit] + 1

        def made_at(unit):
            return SPLIT_AT[unit] if unit in SPLIT_AT else -1

        def scores(h, i):
            pe.wait_ge(exp_ready, NT * h + i) if not (isinstance(h, int) and h + i == 0) else None
            b, r = divmod(i, TPB)
            if r == 0:
                pe.wait_ge(proj_lo, lo_count(h, max((("Q", b), ("K", b)), key=made_at)))
            q = [part[:, b % 2, r * P:(r + 1) * P] for part in qT]
            for c in range(b + 1):
                n = BT if c < b else max(r + 1, 2) * P
                k = [part[:, c * BT:c * BT + n] for part in kT]
                diagonal = c == b
                last = split_matmul(nc, ps_s[:, c, 0:n], q, k, True, True)
                if diagonal:
                    last = nc.tensor.matmul(ps_s[:, c, r * P:(r + 1) * P], ident_bf[:, :], causal[:, :],
                                            start=False, stop=True, skip_group_check=True)
                last.then_inc(scores_ready, 1)

        def transposes(h, i, u):
            if u == 0:
                pe.wait_ge(exp_ready, NT * h + i + 1)
            n = chunks_before(i) + u
            if not (isinstance(h, int) and CHUNKS * h + n < 2):
                pe.wait_ge(t_lo, CHUNKS * h + n - 1)
            for k in range(4 * u, min(4 * u + 4, i + 1)):
                last = nc.tensor.transpose(ps_t[:, n % 2, (k - 4 * u) * P:(k - 4 * u + 1) * P],
                                           probs[:, i % 2, k * P:(k + 1) * P], ident[:, :])
            last.then_inc(t_ready, 1)

        def pv(h, b, k0):
            if k0 == 0:
                if not (isinstance(h, int) and h + b == 0):
                    pe.wait_ge(z_copied, NPAIR * h + b)
                pe.wait_ge(zero_ready, 2 * (NPAIR * h + b + 1))
            if k0 % 4 == 0:
                pe.wait_ge(t_lo, CHUNKS * h + chunks_before(2 * b + 1) + k0 // 4 + 1)
                pe.wait_ge(proj_lo, lo_count(h, ("VT", k0 // 4)))
            a = b % 2
            for k in (k0, k0 + 1):
                p = [part[:, a:a + 2, k * P:(k + 1) * P] for part in pT]
                vv = [part[:, k, :] for part in v]
                last = split_matmul(nc, ps_z[:, 0:2 * P], vv, p, k == 0, k == 2 * b + 1)
            if k == 2 * b + 1:
                last.then_inc(z_ready, 1)

        def run(h, op):
            {"T": transposes, "P": project, "Z": pv}[op[0]](h, *op[1:])

        def head(h, first, last):
            for i in range(NT):
                scores(h, i)
                for op, previous in pieces(i, first, last):
                    run(h - 1 if previous else h, op)
        pe.wait_ge(consts, 3)
        for kind in ("Q", "K"):
            for c in range(DC):
                project(None, kind, 0, c)
        head(0, True, False)
        for a, z_ in stretches:
            with pe.Fori(a, z_) as h:
                head(h, False, False)
        head(H - 1, False, True)
        for op in TAIL:
            run(H - 1, op)

    @block.scalar
    def _(act):
        def unit_hi(h, unit):
            kind, b = unit
            if h is None:
                nth = {"Q": 0, "K": 1}[kind]
                act.wait_ge(proj_ready, nth + 1)
            else:
                act.wait_ge(proj_ready, PREU + NU * h + UNIT_AT[unit] + 1)
            if kind == "V":
                ins = nc.scalar.activation(vT[:, :], ps_p[:, :], ACT.Copy)
            elif kind == "VT":
                ins = nc.scalar.activation(v[0][:, b * TPB:(b + 1) * TPB, :],
                                           ps_p[:, :].rearrange("p (t n) -> p t n", t=TPB), ACT.Copy)
            elif kind[0] == "Q":
                ins = nc.scalar.activation(qT[0][:, b % 2, :], ps_p[:, :], ACT.Copy, scale=-SOFT)
            else:
                ins = nc.scalar.activation(kT[0][:, b * BT:(b + 1) * BT], ps_p[:, :], ACT.Copy)
            ins.then_inc(proj_hi, 1)

        def transposed_hi(h, i, u):
            sub = 1 if i % 2 else 2 * (i // 2 % 2)
            act.wait_ge(t_ready, CHUNKS * h + chunks_before(i) + u + 1)
            lo, hi = 4 * u * P, min(4 * u + 4, i + 1) * P
            nc.scalar.activation(pT[0][:, sub, lo:hi], ps_t[:, (chunks_before(i) + u) % 2, 0:hi - lo],
                                 ACT.Copy).then_inc(t_hi, 1)

        def exponent(h, i):
            if i % (NT // 2) == 0:
                wait_for(act, sums_saved[i // (NT // 2)], 16 * h)
            act.wait_ge(min_ready, NT * h + i + 1)
            w = (i + 1) * P
            src = ps_s[:, :, :].rearrange("p c n -> p (c n)")[:, 0:w]
            nc.scalar.activation(probs[:, i % 2, 0:w], src, ACT.Exp, bias=rmin[:, i % 2:i % 2 + 1], scale=-1.0,
                                 accum_out=sums[:, i:i + 1]).then_inc(exp_ready, 1)

        def copy_z(h, b):
            act.wait_ge(z_ready, NPAIR * h + b + 1)
            wait_for(act, z_saved[b % ZBUF], Z_DMAS[b % 2] * 16 * (NPAIR // ZBUF * h + b // ZBUF))
            nc.scalar.activation(z[:, b % ZBUF, :], ps_z[:, 0:2 * P], ACT.Copy).then_inc(z_copied, 1)

        def finish(h, op):
            if op[0] == "T":
                transposed_hi(h, *op[1:])
            elif ends(op):
                unit_hi(h, op[1:3]) if op[0] == "P" else copy_z(h, op[1])

        def head(h, first, last):
            for i in range(NT):
                for n, (op, previous) in enumerate(pieces(i, first, last)):
                    if n == EXP_AFTER:
                        exponent(h, i)
                    finish(h - 1 if previous else h, op)
        unit_hi(None, ("Q", 0))
        unit_hi(None, ("K", 0))
        head(0, True, False)
        for a, z_ in stretches:
            with act.Fori(a, z_) as h:
                head(h, False, False)
        head(H - 1, False, True)
        for op in TAIL:
            finish(H - 1, op)

    @block.vector
    def _(dve):
        def unit_lo(h, unit):
            kind, b = unit
            if kind == "V":
                return
            if h is None:
                nth = {"Q": 0, "K": 1}[kind]
                dve.wait_ge(proj_hi, nth + 1)
            else:
                dve.wait_ge(proj_hi, PREU + NU * h + UNIT_AT[unit] + 1)
            if kind == "VT":
                parts = [part[:, b * TPB:(b + 1) * TPB, :].rearrange("p t n -> p (t n)") for part in v]
            elif kind[0] == "Q":
                parts = [part[:, b % 2, :] for part in qT]
            else:
                parts = [part[:, b * BT:(b + 1) * BT] for part in kT]
            if kind[0] == "Q":
                ins = nc.vector.scalar_tensor_tensor(out=parts[1], in0=ps_p[:, :], scalar=-SOFT,
                                                     in1=parts[0].bitcast(F32), op0=ALU.mult, op1=ALU.subtract)
            else:
                ins = nc.vector.tensor_tensor(parts[1], ps_p[:, :], parts[0].bitcast(F32), ALU.subtract)
            ins.then_inc(proj_lo, 1)

        def minimum(h, i):
            nch = n_chunks(i)
            for c in range(nch):
                dve.wait_ge(scores_ready, CHUNKS * h + chunks_before(i) + c + 1)
                w = BT if c < nch - 1 else (i % TPB + 1) * P
                if nch == 1:
                    nc.vector.tensor_reduce(rmin[:, i % 2:i % 2 + 1], ps_s[:, c, 0:w], AX_X, ALU.min) \
                      .then_inc(min_ready, 1)
                else:
                    nc.vector.tensor_reduce(cmin[:, c:c + 1], ps_s[:, c, 0:w], AX_X, ALU.min) \
                      .then_inc(chunk_min, 1)
            if nch > 1:
                done = sum(n_chunks(j) for j in range(i + 1) if n_chunks(j) > 1)
                dve.wait_ge(chunk_min, MULTI * h + done)
                nc.vector.tensor_reduce(rmin[:, i % 2:i % 2 + 1], cmin[:, 0:nch], AX_X, ALU.min) \
                  .then_inc(min_ready, 1)

        def transposed_lo(h, i, u):
            sub = 1 if i % 2 else 2 * (i // 2 % 2)
            dve.wait_ge(t_hi, CHUNKS * h + chunks_before(i) + u + 1)
            lo, hi = 4 * u * P, min(4 * u + 4, i + 1) * P
            nc.vector.tensor_tensor(pT[1][:, sub, lo:hi], ps_t[:, (chunks_before(i) + u) % 2, 0:hi - lo],
                                    pT[0][:, sub, lo:hi].bitcast(F32), ALU.subtract).then_inc(t_lo, 1)

        def unpack(h, k):
            base = PIECES * h + k
            dve.wait_ge(words_loaded, 16 * (LOADS_ALL * h + LOADS_BEFORE[k] + LOADS[k]))
            nc.vector.tensor_tensor(words[:, :], words[:, :], nib_shift[:, 0:1].to_broadcast([P, D]),
                                    ALU.logical_shift_right).then_inc(unpacked, 1)
            dve.wait_ge(unpacked, 3 * base + 1)
            nc.vector.tensor_scalar(code[:, :], words[:, :], 7, None, ALU.bitwise_and).then_inc(unpacked, 1)
            dve.wait_ge(unpacked, 3 * base + 2)
            nc.vector.tensor_scalar(words[:, :], words[:, :], 8, None, ALU.bitwise_and).then_inc(unpacked, 1)

        def finish(h, op):
            if op[0] == "T":
                transposed_lo(h, *op[1:])
            elif op[0] == "P" and ends(op):
                unit_lo(h, op[1:3])

        def head(h, decode, first, last):
            for i in range(NT):
                minimum(h, i)
                for op, previous in pieces(i, first, last):
                    finish(h - 1 if previous else h, op)
                if decode and i in UNPACK_STEP:
                    unpack(h, UNPACK_STEP[i])
        unit_lo(None, ("Q", 0))
        unit_lo(None, ("K", 0))
        head(0, True, True, False)
        for n, (a, z_) in enumerate(stretches):
            with dve.Fori(a, z_) as h:
                head(h, n == 0, False, False)
        head(H - 1, False, False, True)
        for op in TAIL:
            finish(H - 1, op)


def output_projection(nc, ph, hbm, x, w_o, ident, gate_a, shift_b, scale_b, hT_hi, hT_lo):
    def sb(name, shape, dt):
        return ph.enter_context(nc.sbuf_tensor(name, shape, dt))

    def sem(name):
        return ph.enter_context(nc.semaphore("o_" + name))

    HH = H // 2
    RW = 2
    wo = [sb(f"wo_{n}", [P, H, D], F32R) for n in ("hi", "lo")]
    stage = sb("wo_stage", [P, 2, RW, D], F32)
    sums = sb("o_sums", [P, H * NT], F32)
    recip = sb("o_recip", [P, H * NT], F32)
    recipT = sb("o_recipT", [P, 2, P], F32)
    zt = sb("o_z", [P, 2, HH, P], F32)
    rt = sb("o_r", [P, 2, HH, P], F32)
    zs = [sb(f"o_z{n}", [P, 2, HH, P], F32R) for n in ("hi", "lo")]
    xt = sb("o_x", [P, 2, D], F32)
    x1 = sb("o_x1", [P, 2, D], F32)
    xn = sb("o_xn", [P, 2, D], F32)
    h32 = sb("o_h32", [P, 2, D], F32)
    hs = [sb(f"o_h{n}", [P, 2, D], F32R) for n in ("hi", "lo")]
    stats = sb("o_stats", [P, 6], F32)
    mv = sb("o_mv", [P, 2], F32)
    vare = sb("o_vare", [P, 1], F32)
    std = sb("o_std", [P, 1], F32)
    rstd = sb("o_rstd", [P, 1], F32)
    ps_r = ph.enter_context(nc.psum_tensor("o_psr", [P, 2, 512], F32))
    ps_o = ph.enter_context(nc.psum_tensor("o_pso", [P, 2, 512], F32))
    ps_t = ph.enter_context(nc.psum_tensor("o_pst", [P, 2, 512], F32))

    sums_loaded = sem("sums_loaded")
    recip_ready = sem("recip_ready")
    recip_t = sem("recip_t")
    recip_row = sem("recip_row")
    recip_saved = sem("recip_saved")
    wo_loaded = [sem(f"wo_loaded{n}") for n in range(2)]
    wo_hi = sem("wo_hi")
    wo_lo = sem("wo_lo")
    z_loaded = [sem(f"z_loaded{n}") for n in range(2)]
    x_loaded = [sem(f"x_loaded{n}") for n in range(2)]
    z_norm = sem("z_norm")
    z_hi = sem("z_hi")
    z_lo = sem("z_lo")
    half_done = sem("half_done")
    dve_step = sem("dve_step")
    x1_ready = sem("x1_ready")
    x1_saved = [sem(f"x1_saved{n}") for n in range(2)]
    var_ready = sem("var_ready")
    std_ready = sem("std_ready")
    xn_ready = sem("xn_ready")
    t_ready = sem("t_ready")
    h_ready = [sem(f"h_ready{n}") for n in range(2)]
    h_hi = sem("h_hi")
    h_lo = sem("h_lo")
    h_saved = [sem(f"h_saved{n}") for n in range(2)]
    STEPS = 4

    block = ph.enter_context(nc.Block())

    @block.sync
    def _(sp):
        sp.dma_start(sums[:, :].rearrange("p (h i) -> p h i", h=H),
                     hbm["sums"].rearrange("h p i -> p h i")).then_inc(sums_loaded, 16)
        for n in range(H // RW):
            if n >= 2:
                sp.wait_ge(wo_lo, n - 1)
            sp.dma_start(stage[:, n % 2, :, :], w_o[:, n * RW:(n + 1) * RW, :]).then_inc(wo_loaded[n % 2], 16)
            if n == 1:
                sp.wait_ge(recip_row, 1)
                sp.dma_start(hbm["recips"].rearrange("(a p) n -> p a n", a=2), recipT[:, :, :]) \
                  .then_inc(recip_saved, 16)
        sp.wait_ge(recip_saved, 16)
        r_view = hbm["recips"].rearrange("(h i) n -> h i n", h=H)

        def load_half(tile, f):
            if not is_first(tile):
                sp.wait_ge(z_lo, 2 * tile.t + f - 1)
            sp.dma_start(zt[:, f, :, :], hbm["zT"][f * HH:(f + 1) * HH, :, rows_of(tile.t)]
                         .rearrange("h p n -> p h n")).then_inc(z_loaded[f], 16)
            src = r_view[f * HH:(f + 1) * HH, bass.ds(tile.t, 1), :].rearrange("h a n -> a h n")
            sp.dma_start(rt[:, f, :, :], src.to_broadcast([P, HH, P])).then_inc(z_loaded[f], 16)

        def load_x(tile):
            if not is_first(tile):
                sp.wait_ge(x1_ready, tile.t - 1)
            sp.dma_start(xt[:, tile.parity, :], x[rows_of(tile.t), :]).then_inc(x_loaded[tile.parity], 16)

        def save_h(tile):
            sp.wait_ge(h_lo, tile.t + 1)
            for part, whole in zip(hs, (hT_hi, hT_lo)):
                sp.dma_start(whole[:, :, rows_of(tile.t)].bitcast(F32),
                             part[:, tile.parity, :].rearrange("p (c n) -> p c n", c=DC).bitcast(F32)) \
                  .then_inc(h_saved[tile.parity], 16)

        def step(tile, first, last):
            if not last:
                load_half(tile.after(), 0)
                load_x(tile.after())
                load_half(tile.after(), 1)
            if not first:
                save_h(tile.before())
            sp.wait_ge(x1_ready, tile.t + 1)
            sp.dma_start(hbm["x1"][bass.ds(tile.t, 1), :, :].rearrange("a p d -> (a p) d"),
                         x1[:, tile.parity, :]).then_inc(x1_saved[tile.parity], 16)
        load_half(FIRST, 0)
        load_half(FIRST, 1)
        load_x(FIRST)
        token_tiles(sp, step)
        save_h(LAST)
        for n in range(2):
            sp.wait_ge(h_saved[n], 2 * 16 * NT // 2)
            sp.wait_ge(x1_saved[n], 16 * NT // 2)

    @block.vector
    def _(dve):
        dve.wait_ge(sums_loaded, 16)
        nc.vector.reciprocal(recip[:, :], sums[:, :]).then_inc(recip_ready, 1)
        for n in range(H // RW):
            dve.wait_ge(wo_hi, n + 1)
            sl = slice(n * RW, (n + 1) * RW)
            nc.vector.tensor_tensor(wo[1][:, sl, :], stage[:, n % 2, :, :], wo[0][:, sl, :].bitcast(F32),
                                    ALU.subtract).then_inc(wo_lo, 1)

        def split_half(tile, f):
            dve.wait_ge(z_loaded[f], 32 * (tile.t + 1))
            nc.vector.tensor_tensor(zt[:, f, :, :], zt[:, f, :, :], rt[:, f, :, :], ALU.mult).then_inc(z_norm, 1)
            dve.wait_ge(z_hi, 2 * tile.t + f + 1)
            nc.vector.tensor_tensor(zs[1][:, f, :, :], zt[:, f, :, :], zs[0][:, f, :, :].bitcast(F32),
                                    ALU.subtract).then_inc(z_lo, 1)

        def split_h(tile):
            dve.wait_ge(h_hi, tile.t + 1)
            nc.vector.tensor_tensor(hs[1][:, tile.parity, :], h32[:, tile.parity, :],
                                    hs[0][:, tile.parity, :].bitcast(F32), ALU.subtract).then_inc(h_lo, 1)

        def step(tile, first, last):
            t, parity, k = tile
            n = [0]

            def done(ins):
                n[0] += 1
                ins.then_inc(dve_step, 1)
                dve.wait_ge(dve_step, STEPS * t + n[0])
            if not last:
                split_half(tile.after(), 0)
                split_half(tile.after(), 1)
            dve.wait_ge(half_done, 2 * t + 2)
            wait_for(dve, x1_saved[parity], 16 * k)
            done(nc.vector.tensor_tensor(x1[:, parity, :], ps_o[:, parity, :], gate_a[:, :], ALU.mult))
            dve.wait_ge(x_loaded[parity], 16 * (k + 1))
            nc.vector.tensor_tensor(x1[:, parity, :], x1[:, parity, :], xt[:, parity, :], ALU.add) \
              .then_inc(x1_ready, 1)
            dve.wait_ge(x1_ready, t + 1)
            done(nc.vector.bn_stats(stats[:, :], x1[:, parity, :]))
            if not first:
                split_h(tile.before())
            done(nc.vector.bn_aggr(mv[:, :], stats[:, :]))
            nc.vector.tensor_scalar(vare[:, :], mv[:, 1:2], LN_EPS, None, ALU.add).then_inc(var_ready, 1)
            dve.wait_ge(std_ready, t + 1)
            done(nc.vector.reciprocal(rstd[:, :], std[:, :]))
            if not first:
                dve.wait_ge(t_ready, t - 1)
            nc.vector.tensor_scalar(xn[:, parity, :], x1[:, parity, :], mv[:, 0:1], rstd[:, 0:1],
                                    ALU.subtract, ALU.mult).then_inc(xn_ready, 1)
            dve.wait_ge(xn_ready, t + 1)
        split_half(FIRST, 0)
        split_half(FIRST, 1)
        token_tiles(dve, step)
        split_h(LAST)

    @block.scalar
    def _(act):
        for n in range(H // RW):
            act.wait_ge(wo_loaded[n % 2], 16 * (n // 2 + 1))
            nc.scalar.activation(wo[0][:, n * RW:(n + 1) * RW, :], stage[:, n % 2, :, :], ACT.Copy) \
              .then_inc(wo_hi, 1)
            if n == 0:
                act.wait_ge(recip_t, 1)
                nc.scalar.activation(recipT[:, :, :], ps_r[:, 0, 0:2 * P].rearrange("p (a n) -> p a n", a=2),
                                     ACT.Copy).then_inc(recip_row, 1)

        def half_hi(tile, f):
            act.wait_ge(z_norm, 2 * tile.t + f + 1)
            if not is_first(tile):
                act.wait_ge(half_done, 2 * tile.t + f - 1)
            nc.scalar.activation(zs[0][:, f, :, :], zt[:, f, :, :], ACT.Copy).then_inc(z_hi, 1)

        def modulate(tile):
            t, parity, k = tile
            act.wait_ge(t_ready, t + 1)
            wait_for(act, h_saved[parity], 32 * k)
            for c in range(DC):
                nc.scalar.activation(h32[:, parity, c * P:(c + 1) * P], ps_t[:, parity, c * P:(c + 1) * P],
                                     ACT.Identity, bias=shift_b[:, c:c + 1], scale=scale_b[:, c:c + 1]) \
                  .then_inc(h_ready[parity], 1)
            act.wait_ge(h_ready[parity], DC * (k + 1))
            nc.scalar.activation(hs[0][:, parity, :], h32[:, parity, :], ACT.Copy).then_inc(h_hi, 1)

        def step(tile, first, last):
            if not last:
                half_hi(tile.after(), 0)
                half_hi(tile.after(), 1)
            if not first:
                modulate(tile.before())
            act.wait_ge(var_ready, tile.t + 1)
            nc.scalar.activation(std[:, :], vare[:, :], ACT.Sqrt).then_inc(std_ready, 1)
        half_hi(FIRST, 0)
        half_hi(FIRST, 1)
        token_tiles(act, step)
        modulate(LAST)

    @block.tensor
    def _(pe):
        pe.wait_ge(recip_ready, 1)
        for n in range(2):
            last = nc.tensor.transpose(ps_r[:, 0, n * P:(n + 1) * P], recip[:, n * P:(n + 1) * P], ident[:, :])
        last.then_inc(recip_t, 1)
        pe.wait_ge(wo_lo, H // RW)

        def transposes(tile):
            t, parity, k = tile
            pe.wait_ge(xn_ready, t + 1)
            wait_for(pe, h_ready[parity], DC * k)
            for c in range(DC):
                last = nc.tensor.transpose(ps_t[:, parity, c * P:(c + 1) * P], xn[:, parity, c * P:(c + 1) * P],
                                           ident[:, :])
            last.then_inc(t_ready, 1)

        def step(tile, first, last):
            t, parity, k = tile
            if not first:
                pe.wait_ge(x1_ready, t - 1)
            for f in range(2):
                pe.wait_ge(z_lo, 2 * t + f + 1)
                for n in range(HH):
                    h = f * HH + n
                    zz = [part[:, f, n, :] for part in zs]
                    w = [part[:, h, :] for part in wo]
                    mm = split_matmul(nc, ps_o[:, parity, :], zz, w, h == 0, h == H - 1)
                mm.then_inc(half_done, 1)
            if not first:
                transposes(tile.before())
        token_tiles(pe, step)
        transposes(LAST)


def gate_up(nc, ph, hbm, mid, hT_hi, hT_lo):
    def sb(name, shape, dt):
        return ph.enter_context(nc.sbuf_tensor(name, shape, dt))

    def sem(name):
        return ph.enter_context(nc.semaphore("g_" + name))

    hT = (hT_hi, hT_lo)
    w_raw = sb("g_wraw", [P, DC, 2, P], F32)
    w = [[sb(f"g_w{m}{n}", [P, DC, P], F32R) for n in ("hi", "lo")] for m in ("gate", "up")]
    sg = sb("g_silu", [P, NB, BT], F32)
    ps = [ph.enter_context(nc.psum_tensor(f"g_ps{m}", [P, NB, BT], F32)) for m in ("gate", "up")]
    w_loaded = sem("w_loaded")
    w_hi = sem("w_hi")
    w_lo = sem("w_lo")
    gate_ready = sem("gate_ready")
    up_ready = sem("up_ready")
    silu_ready = sem("silu_ready")
    mid_ready = sem("mid_ready")
    block = ph.enter_context(nc.Block())

    def feature_tiles(eng, step):
        step(0, False)
        with eng.Fori(1, NI - 1) as n:
            step(n, False)
        step(NI - 1, True)

    @block.sync
    def _(sp):
        def load(n):
            sp.dma_start(w_raw[:, :, :, :].rearrange("p c m n -> p (c m n)"),
                         hbm["wgu"][bass.ds(n, 1), :, :].rearrange("a p n -> (a p) n")).then_inc(w_loaded, 16)
        load(0)

        def step(n, last):
            if not last:
                sp.wait_ge(w_lo, 2 * n + 2)
                load(n + 1)
        feature_tiles(sp, step)

    @block.scalar
    def _(act):
        def hi(n, m):
            act.wait_ge(w_loaded, 16 * (n + 1))
            if not (isinstance(n, int) and n == 0):
                act.wait_ge((gate_ready, up_ready)[m], NB * n)
            nc.scalar.activation(w[m][0][:, :, :], w_raw[:, :, m, :], ACT.Copy).then_inc(w_hi, 1)

        def step(n, last):
            for b in range(NB):
                act.wait_ge(gate_ready, NB * n + b + 1)
                if b == 0:
                    wait_for(act, mid_ready, NB * n)
                nc.scalar.activation(sg[:, b, :], ps[0][:, b, :], ACT.Silu).then_inc(silu_ready, 1)
            if not last:
                hi(n + 1, 0)
                hi(n + 1, 1)

        hi(0, 0)
        hi(0, 1)
        feature_tiles(act, step)

    @block.vector
    def _(dve):
        def lo(n, m):
            dve.wait_ge(w_hi, 2 * n + m + 1)
            nc.vector.tensor_tensor(w[m][1][:, :, :], w_raw[:, :, m, :], w[m][0][:, :, :].bitcast(F32),
                                    ALU.subtract).then_inc(w_lo, 1)

        def step(n, last):
            if not last:
                lo(n + 1, 0)
            for b in range(NB):
                dve.wait_ge(up_ready, NB * n + b + 1)
                dve.wait_ge(silu_ready, NB * n + b + 1)
                dst = mid[:, bass.ds(n, 1), b * BT:(b + 1) * BT].rearrange("p a n -> p (a n)")
                nc.vector.tensor_tensor(dst, sg[:, b, :], ps[1][:, b, :], ALU.mult).then_inc(mid_ready, 1)
            if not last:
                lo(n + 1, 1)
        lo(0, 0)
        lo(0, 1)
        feature_tiles(dve, step)

    @block.tensor
    def _(pe):
        def step(n, last):
            for m in range(2):
                pe.wait_ge(w_lo, 2 * n + m + 1)
                for b in range(NB):
                    wait_for(pe, (silu_ready, mid_ready)[m], NB * n if b == 0 else 0)
                    for c in range(DC):
                        ww = [part[:, c, :] for part in w[m]]
                        hh = [part[:, c, b * BT:(b + 1) * BT] for part in hT]
                        mm = split_matmul(nc, ps[m][:, b, :], ww, hh, c == 0, c == DC - 1)
                    mm.then_inc((gate_ready, up_ready)[m], 1)
        feature_tiles(pe, step)


def down(nc, ph, hbm, mid, gate_b, hT_hi, hT_lo, out):
    def sb(name, shape, dt):
        return ph.enter_context(nc.sbuf_tensor(name, shape, dt))

    def sem(name):
        return ph.enter_context(nc.semaphore("d_" + name))

    wd = [part[:, :, :].rearrange("p c n -> p (c n)")[:, 0:NI * D] for part in (hT_hi, hT_lo)]
    stage = sb("d_stage", [P, 2, D], F32)
    ms = [sb(f"d_m{n}", [P, 2, NI, P], F32R) for n in ("hi", "lo")]
    x1 = sb("d_x1", [P, 2, D], F32)
    y = sb("d_y", [P, 2, D], F32)
    junk = sb("d_junk", [P, D], F32)
    ss = sb("d_ss", [P, 1], F32)
    ms_eps = sb("d_mse", [P, 1], F32)
    rms = sb("d_rms", [P, 1], F32)
    rrms = sb("d_rrms", [P, 1], F32)
    ps_y = ph.enter_context(nc.psum_tensor("d_psy", [P, 2, 512], F32))

    wd_loaded = [sem(f"wd_loaded{n}") for n in range(2)]
    wd_hi = sem("wd_hi")
    wd_lo = sem("wd_lo")
    m_hi = sem("m_hi")
    m_lo = sem("m_lo")
    y_ready = sem("y_ready")
    square_ready = sem("square_ready")
    rms_ready = sem("rms_ready")
    mean_ready = sem("mean_ready")
    dve_step = sem("dve_step")
    y_done = sem("y_done")
    x1_loaded = [sem(f"x1_loaded{n}") for n in range(2)]
    out_saved = [sem(f"out_saved{n}") for n in range(2)]
    STEPS = 2
    block = ph.enter_context(nc.Block())

    @block.sync
    def _(sp):
        for n in range(NI):
            if n >= 2:
                sp.wait_ge(wd_lo, n - 1)
            sp.dma_start(stage[:, n % 2, :], hbm["wdn"][n]).then_inc(wd_loaded[n % 2], 16)

        def load_x1(tile):
            if not is_first(tile):
                sp.wait_ge(y_done, tile.t - 1)
            sp.dma_start(x1[:, tile.parity, :], hbm["x1"][bass.ds(tile.t, 1), :, :].rearrange("a p d -> (a p) d")) \
              .then_inc(x1_loaded[tile.parity], 16)

        def step(tile, first, last):
            if not last:
                load_x1(tile.after())
            sp.wait_ge(y_done, tile.t + 1)
            sp.dma_start(out[rows_of(tile.t), :], y[:, tile.parity, :]).then_inc(out_saved[tile.parity], 16)
        load_x1(FIRST)
        token_tiles(sp, step)
        for n in range(2):
            sp.wait_ge(out_saved[n], 16 * NT // 2)

    @block.scalar
    def _(act):
        for n in range(NI):
            act.wait_ge(wd_loaded[n % 2], 16 * (n // 2 + 1))
            nc.scalar.activation(wd[0][:, n * D:(n + 1) * D], stage[:, n % 2, :], ACT.Copy).then_inc(wd_hi, 1)

        def step(tile, first, last):
            act.wait_ge(y_ready, tile.t + 1)
            if not first:
                act.wait_ge(mean_ready, tile.t)
            nc.scalar.activation(junk[:, :], ps_y[:, tile.parity, :], ACT.Square, accum_out=ss[:, :]) \
              .then_inc(square_ready, 1)
            act.wait_ge(mean_ready, tile.t + 1)
            nc.scalar.activation(rms[:, :], ms_eps[:, :], ACT.Sqrt).then_inc(rms_ready, 1)
        token_tiles(act, step)

    @block.vector
    def _(dve):
        def split(tile):
            if not is_first(tile):
                dve.wait_ge(y_ready, tile.t - 1)
            src = mid[:, :, rows_of(tile.t)]
            nc.vector.tensor_tensor(ms[0][:, tile.parity, :, :], src, src, ALU.max).then_inc(m_hi, 1)
            dve.wait_ge(m_hi, tile.t + 1)
            nc.vector.tensor_tensor(ms[1][:, tile.parity, :, :], src, ms[0][:, tile.parity, :, :].bitcast(F32),
                                    ALU.subtract).then_inc(m_lo, 1)

        def step(tile, first, last):
            t, parity, k = tile
            if not last:
                split(tile.after())
            dve.wait_ge(square_ready, t + 1)
            nc.vector.tensor_scalar(ms_eps[:, :], ss[:, :], 1.0 / D, RMS_EPS, ALU.mult, ALU.add) \
              .then_inc(mean_ready, 1)
            dve.wait_ge(rms_ready, t + 1)
            nc.vector.reciprocal(rrms[:, :], rms[:, :]).then_inc(dve_step, 1)
            dve.wait_ge(dve_step, STEPS * t + 1)
            wait_for(dve, out_saved[parity], 16 * k)
            nc.vector.scalar_tensor_tensor(out=y[:, parity, :], in0=ps_y[:, parity, :], scalar=rrms[:, 0:1],
                                           in1=gate_b[:, :], op0=ALU.mult, op1=ALU.mult).then_inc(dve_step, 1)
            dve.wait_ge(dve_step, STEPS * t + 2)
            dve.wait_ge(x1_loaded[parity], 16 * (k + 1))
            nc.vector.tensor_tensor(y[:, parity, :], y[:, parity, :], x1[:, parity, :], ALU.add).then_inc(y_done, 1)
        split(FIRST)
        for n in range(NI):
            dve.wait_ge(wd_hi, n + 1)
            nc.vector.tensor_tensor(wd[1][:, n * D:(n + 1) * D], stage[:, n % 2, :],
                                    wd[0][:, n * D:(n + 1) * D].bitcast(F32), ALU.subtract).then_inc(wd_lo, 1)
        token_tiles(dve, step)

    @block.tensor
    def _(pe):
        def step(tile, first, last):
            t, parity, k = tile
            pe.wait_ge(m_lo, t + 1)
            if not first:
                pe.wait_ge(y_done, t - 1)
            for n in range(NI):
                if first:
                    pe.wait_ge(wd_lo, n + 1)
                mt = [part[:, parity, n, :] for part in ms]
                w = [part[:, n * D:(n + 1) * D] for part in wd]
                mm = split_matmul(nc, ps_y[:, parity, :], mt, w, n == 0, n == NI - 1)
            mm.then_inc(y_ready, 1)
        token_tiles(pe, step)


def kernel(L0_attn_x, L0_attn_W_K, L0_attn_W_Q, L0_attn_W_V, L0_attn_W_O, L0_ffn_gate_up_packed,
           L0_ffn_gate_up_scales, L0_ffn_down_packed, L0_ffn_down_scales, L0_c, L0_wmod):
    import numpy as np
    import concourse.bacc as bacc
    from concourse.bass_utils import run_bass_kernel_spmd

    def a(v):
        return np.asarray(v)

    def heads(w):
        return a(w).reshape(H, DH, DC, P).transpose(0, 3, 2, 1).reshape(H, P, 1, DC * DH)

    gu = a(L0_ffn_gate_up_packed).reshape(2, NI, P, DC, WORDS)
    gus = a(L0_ffn_gate_up_scales).reshape(DC, 2, NI, P)
    arrays = {
        "x": a(L0_attn_x).reshape(S, D),
        "w_qkv": np.concatenate([heads(w) for w in (L0_attn_W_Q, L0_attn_W_K, L0_attn_W_V)], axis=2),
        "w_o": a(L0_attn_W_O).reshape(D, H, P).transpose(2, 1, 0),
        "gu_packed": gu.transpose(1, 3, 4, 0, 2).reshape(NI, DC, WORDS, 2 * P),
        "gu_scales": gus.transpose(2, 0, 1, 3).reshape(NI, 2, D),
        "dn_packed": a(L0_ffn_down_packed).reshape(D, NI, WORDS).transpose(1, 2, 0),
        "dn_scales": a(L0_ffn_down_scales),
        "c_cols": a(L0_c).reshape(DC, P).transpose(1, 0),
        "w_mod": a(L0_wmod),
    }
    nc = bacc.Bacc("TRN2", target_bir_lowering=False, num_devices=1)
    ins = {}
    arrays = {n: np.ascontiguousarray(v) for n, v in arrays.items()}
    for n, v in arrays.items():
        ins[n] = nc.dram_tensor("in_" + n, v.shape, mybir.dt.from_np(v.dtype), kind="ExternalInput").ap()
    out = nc.dram_tensor("out_x", [S, D], F32, kind="ExternalOutput").ap()
    adaln_kernel(nc, out=out, **ins)
    r = run_bass_kernel_spmd(nc, [{"in_" + n: v for n, v in arrays.items()}], core_ids=[0])
    return r.results[0]["out_x"].reshape(1, S, D)
```

```python
from contextlib import ExitStack
from typing import NamedTuple

import concourse.bass as bass
from concourse import mybir

F32 = mybir.dt.float32
F32R = mybir.dt.float32r
BF16 = mybir.dt.bfloat16
F16 = mybir.dt.float16
I32 = mybir.dt.int32
ALU = mybir.AluOpType
ACT = mybir.ActivationFunctionType
AX_X = mybir.AxisListType.X

P = 128
S, D = 2048, 512
H, DH = 16, 128
INTER = 1408
DC = D // P
NT = S // P
BT = 512
NB = S // BT
TPB = BT // P
NI = INTER // P
NPAIR = NT // 2
WD_STAGE = 6
WO_EARLY = 10
WORDS = P // 8
LN_EPS, RMS_EPS = 1e-5, 1e-6
SOFT = DH ** -0.5
MASKED = 1e10 * SOFT


def n_chunks(i):
    return i // TPB + 1


def chunks_before(i):
    return sum(n_chunks(j) for j in range(i))


CHUNKS = chunks_before(NT)
MULTI = sum(n_chunks(i) for i in range(NT) if n_chunks(i) > 1)



def unit(kind, b):
    return [("P", kind, b, c) for c in range(1 if kind == "VT" else DC)]


def pair(b, lo, hi):
    return [("Z", b, k) for k in range(lo, hi, 2)]


FILL = [
    pair(6, 8, 14) + unit("V", 0),
    pair(7, 0, 4) + unit("VT", 0) + pair(7, 4, 8),
    unit("K", 1) + pair(7, 8, 10),
    unit("Q", 1) + pair(7, 10, 16),
    pair(0, 0, 2) + unit("V", 1),
    unit("VT", 1) + pair(1, 0, 4),
    unit("K", 2),
    unit("Q", 2) + pair(2, 0, 6),
    unit("V", 2),
    unit("VT", 2) + pair(3, 0, 8),
    unit("K", 3),
    unit("Q", 3) + pair(4, 0, 6),
    pair(4, 6, 10) + unit("V", 3),
    unit("VT", 3) + pair(5, 0, 8),
    pair(5, 8, 12) + unit("Qnext", 0),
    unit("Knext", 0) + pair(6, 0, 8),
]
T_AFTER = (0, 2, 4, 6)


def body(i):
    tile = (i - 1) % NT

    def position(u):
        readers = [n + 1 for n, op in enumerate(FILL[i])
                   if op[0] == "Z" and tile == (2 * op[1] + 3) % NT and op[2] // 4 <= u]
        return max([T_AFTER[u]] + readers)
    transposes = [(position(u), ("T", tile, u)) for u in range(n_chunks(tile))]
    ops = []
    for n, op in enumerate(FILL[i] + [None]):
        while transposes and (transposes[0][0] <= n or op is None):
            ops.append(transposes.pop(0)[1])
        if op:
            ops.append(op)
    return ops


BODY = [body(i) for i in range(NT)]


def of_previous(i, op):
    return (op[0] == "T" and op[1] == NT - 1) or (op[0] == "Z" and op[1] >= NPAIR - 2 and i < 4)


def of_next(op):
    return op[0] == "P" and op[1].endswith("next")


def pieces(i, first, last):
    return [(op, of_previous(i, op)) for op in BODY[i]
            if not (first and of_previous(i, op)) and not (last and of_next(op))]


TAIL = [op for i in range(4) for op in BODY[i] if of_previous(i, op)]


def ends(op):
    if op[0] == "P":
        return op[1] == "VT" or op[3] == DC - 1
    return op[0] == "Z" and op[2] == 2 * op[1]


UNITS = [op[1:3] for ops in BODY for op in ops if op[0] == "P" and ends(op)]
UNIT_AT = {u: n for n, u in enumerate(UNITS)}
SPLIT_UNITS = [u for u in UNITS if u[0] != "V"]
SPLIT_AT = {u: n for n, u in enumerate(SPLIT_UNITS)}
NU, NSU = len(UNITS), len(SPLIT_UNITS)
PREU = 2
MATS = ("Q", "K", "V")
SPLIT_ORDER = ("K", "Q", "V")
UNPACK_STEP = {3: 0, 7: 1, 13: 2}
EXP_AFTER = 1
PIECES = 3


class Tile(NamedTuple):
    t: object
    parity: int
    k: object

    def before(self):
        return Tile(self.t - 1, 1 - self.parity, self.k if self.parity else self.k - 1)

    def after(self):
        return Tile(self.t + 1, 1 - self.parity, self.k + self.parity)


def token_tiles(eng, step):
    for t in range(3):
        step(Tile(t, t % 2, t // 2), t == 0, False)
    with eng.Fori(1, NT // 2 - 1) as u:
        step(Tile(u * 2 + 1, 1, u), False, False)
        step(Tile(u * 2 + 2, 0, u + 1), False, False)
    step(Tile(NT - 1, 1, NT // 2 - 1), False, True)


def rows_of(t):
    return bass.ds(t * P, P)


FIRST, LAST = Tile(0, 0, 0), Tile(NT - 1, 1, NT // 2 - 1)


def is_first(tile):
    return isinstance(tile.t, int) and tile.t == 0


def split_matmul(nc, dst, stat, mov, start, stop):
    nc.tensor.matmul(dst, stat[0], mov[0], start=start, stop=False)
    nc.tensor.matmul(dst, stat[0], mov[1], start=False, stop=False)
    return nc.tensor.matmul(dst, stat[1], mov[0], start=False, stop=stop)


def wait_for(eng, sem, value):
    if not isinstance(value, int) or value > 0:
        eng.wait_ge(sem, value)


class GateUpWeights(NamedTuple):
    raw: object
    parts: object
    loaded: object
    hi: object
    lo: object

    def load(self, eng, hbm, n):
        eng.dma_start(self.raw[:, :, :, :].rearrange("p c m n -> p (c m n)"),
                      hbm["wgu"][bass.ds(n, 1), :, :].rearrange("a p n -> (a p) n")).then_inc(self.loaded, 16)

    def make_hi(self, nc, act, n, m):
        act.wait_ge(self.loaded, 16 * (n + 1))
        nc.scalar.activation(self.parts[m][0][:, :, :], self.raw[:, :, m, :], ACT.Copy).then_inc(self.hi, 1)

    def make_lo(self, nc, dve, n, m):
        dve.wait_ge(self.hi, 2 * n + m + 1)
        nc.vector.tensor_tensor(self.parts[m][1][:, :, :], self.raw[:, :, m, :],
                                self.parts[m][0][:, :, :].bitcast(F32), ALU.subtract).then_inc(self.lo, 1)


class AttentionStart(NamedTuple):
    causal: object
    zeros: object
    w_raw: object
    w_hi: object
    w_lo: object
    w_loaded: object
    w_split: object
    consts: object


def split_matrix(nc, pool, st, m, count):
    nc.gpsimd.tensor_tensor(st.w_hi[:, m, :], st.w_raw[:, m, :], st.zeros[:, 0:1].to_broadcast([P, DC * DH]), ALU.add) \
      .then_inc(st.w_split, 1)
    pool.wait_ge(st.w_split, count + 1)
    nc.gpsimd.tensor_tensor(st.w_lo[:, m, :], st.w_raw[:, m, :], st.w_hi[:, m, :].bitcast(F32), ALU.subtract) \
      .then_inc(st.w_split, 1)


def adaln_kernel(nc, x, w_qkv, w_o, gu_packed, gu_scales, dn_packed, dn_scales, c_cols, w_mod, out):
    with ExitStack() as whole:
        hbm = {}
        for name, shape in (("zT", [NT, P, H, P]), ("recips", [H, NPAIR, 2 * P]),
                            ("wgu", [NI, P, DC * 2 * P]), ("wdn", [NI, P, D]), ("x1", [NT, P, D])):
            hbm[name] = nc.dram_tensor("scratch_" + name, shape, F32).ap()

        def sb(name, shape, dt, ctx=whole):
            return ctx.enter_context(nc.sbuf_tensor(name, shape, dt))

        ident = sb("ident", [P, P], F32)
        ident_bf = sb("ident_bf", [P, P], BF16)
        gate_a = sb("gate_a", [P, D], F32)
        gate_b = sb("gate_b", [P, D], F32)
        shift_a = sb("shift_a", [P, DC], F32)
        scale_a = sb("scale_a", [P, DC], F32)
        shift_b = sb("shift_b", [P, DC], F32)
        scale_b = sb("scale_b", [P, DC], F32)
        nib_shift = sb("nib_shift", [P, 1], I32)
        with ExitStack() as first:
            hT_hi, hT_lo = [sb(f"hT_{n}", [P, DC, S], F32R, first) for n in ("hi", "lo")]
            with ExitStack() as both:
                start = AttentionStart(
                    causal=sb("causal", [P, P], BF16, both), zeros=sb("zeros", [P, P], F32, both),
                    w_raw=sb("w_raw", [P, 3, DC * DH], F32, both), w_hi=sb("w_hi", [P, 3, DC * DH], F32R, both),
                    w_lo=sb("w_lo", [P, 3, DC * DH], F32R, both),
                    **{name: both.enter_context(nc.semaphore(name)) for name in ("w_loaded", "w_split", "consts")})
                with ExitStack() as ph:
                    prologue(nc, ph, start, x, w_qkv, c_cols, w_mod, ident, ident_bf, gate_a, gate_b, shift_a,
                             scale_a, shift_b, scale_b, nib_shift, hT_hi, hT_lo)
                with ExitStack() as ph:
                    attention(nc, ph, start, hbm, w_qkv, w_o, gu_packed, gu_scales, dn_packed, dn_scales, ident,
                              ident_bf, nib_shift, hT_hi, hT_lo)
            hT2 = [whole.enter_context(nc.sbuf_tensor(f"hT2_{n}", [P, DC, S], F32R, side="right"))
                   for n in ("hi", "lo")]
            until_down = ExitStack()
            gu = GateUpWeights(
                raw=until_down.enter_context(nc.sbuf_tensor("g_wraw", [P, DC, 2, P], F32, side="right")),
                parts=[[until_down.enter_context(nc.sbuf_tensor(f"g_w{m}{n}", [P, DC, P], F32R, side="right"))
                        for n in ("hi", "lo")] for m in ("gate", "up")],
                **{name: whole.enter_context(nc.semaphore("g_" + name)) for name in ("loaded", "hi", "lo")})
            with ExitStack() as ph:
                output_projection(nc, ph, gu, hbm, x, w_o, ident, gate_a, shift_b, scale_b, hT_hi, hT_lo, hT2)
        mid = sb("mid", [P, NI, S], F32)
        wd_stage = sb("wd_stage", [P, WD_STAGE, D], F32)
        wd_loaded = [whole.enter_context(nc.semaphore(f"wd_loaded{n}")) for n in range(WD_STAGE)]
        with until_down, ExitStack() as ph:
            gate_up(nc, ph, gu, hbm, mid, hT2, wd_stage, wd_loaded)
        with ExitStack() as ph:
            down(nc, ph, hbm, mid, gate_b, hT2, wd_stage, wd_loaded, out)


def prologue(nc, ph, start, x, w_qkv, c_cols, w_mod, ident, ident_bf, gate_a, gate_b, shift_a, scale_a,
             shift_b, scale_b, nib_shift, hT_hi, hT_lo):
    def sb(name, shape, dt):
        return ph.enter_context(nc.sbuf_tensor(name, shape, dt))

    def sem(name):
        return ph.enter_context(nc.semaphore(name))

    SECTIONS = 6
    xt = sb("p_x", [P, NB, TPB, D], F32)
    wm = sb("p_wmod", [P, 3, DC, D], F32)
    c_in = sb("p_c", [P, DC], F32)
    c_silu = sb("p_csilu", [P, DC], F32)
    c_wide = sb("p_cwide", [P, DC, P], F32)
    ones = sb("p_ones", [P, P], F32)
    diag = sb("p_diag", [P, DC, P], F32)
    picked = sb("p_picked", [P, DC], F32)
    absr = sb("p_absr", [P, 2, D], F32)
    stats = sb("p_stats", [P, NT, 6], F32)
    mv = sb("p_mv", [P, NT, 2], F32)
    vare = sb("p_vare", [P, NT], F32)
    std = sb("p_std", [P, NT], F32)
    rstd = sb("p_rstd", [P, NT], F32)
    xn = sb("p_xn", [P, TPB, D], F32)
    h32 = sb("p_h32", [P, DC, BT], F32)
    pidx = sb("p_idx", [P, 1], I32)
    ps_mod = ph.enter_context(nc.psum_tensor("p_psmod", [P, 2, D], F32))
    ps_t = ph.enter_context(nc.psum_tensor("p_pst", [P, 4, BT], F32))

    c_loaded = sem("p_c_loaded")
    x_loaded = [sem(f"p_x_loaded{b}") for b in range(NB)]
    wm_loaded = [sem(f"p_wm_loaded{b}") for b in range(SECTIONS)]
    const_zeroed = sem("p_const_zeroed")
    const_ready = sem("p_const_ready")
    c_ready = sem("p_c_ready")
    wide_ready = sem("p_wide_ready")
    mod_ready = sem("p_mod_ready")
    mod_used = sem("p_mod_used")
    gate_step = sem("p_gate_step")
    dve_step = sem("p_dve_step")
    var_ready = sem("p_var_ready")
    std_ready = sem("p_std_ready")
    xn_ready = sem("p_xn_ready")
    t_ready = sem("p_t_ready")
    h_ready = sem("p_h_ready")
    hi_ready = sem("p_hi_ready")
    lo_ready = sem("p_lo_ready")
    lo_odd = sem("p_lo_odd")
    idx_step = sem("p_idx_step")

    cols = {0: shift_a, 1: scale_a, 3: shift_b, 4: scale_b}
    rows_kept = {2: gate_a, 5: gate_b}

    def make_lo(eng, alu, b, c, done):
        eng.wait_ge(hi_ready, b * DC + c + 1)
        place = (slice(None), c, slice(b * BT, (b + 1) * BT))
        alu.tensor_tensor(hT_lo[place], h32[:, c, :], hT_hi[place].bitcast(F32), ALU.subtract).then_inc(done, 1)

    block = ph.enter_context(nc.Block())

    @block.sync
    def _(sp):
        sp.dma_start(c_in[:, :], c_cols).then_inc(c_loaded, 16)
        def load_x(b):
            sp.dma_start(xt[:, b, :, :], x[b * BT:(b + 1) * BT, :].rearrange("(t p) d -> p t d", p=P)) \
              .then_inc(x_loaded[b], 16)
        def load_w(s):
            if s >= 3:
                sp.wait_ge(mod_ready, s - 2)
            sp.dma_start(wm[:, s % 3, :, :], w_mod[:, s * D:(s + 1) * D].rearrange("(c p) d -> p c d", p=P)) \
              .then_inc(wm_loaded[s], 16)
        load_x(0)
        load_w(0)
        load_w(1)
        for b in range(1, NB):
            load_x(b)
        sp.dma_start(start.w_raw[:, :, :], w_qkv[0]).then_inc(start.w_loaded, 16)
        for s in range(2, SECTIONS):
            load_w(s)

    @block.gpsimd
    def _(pool):
        nc.gpsimd.memset(ident[:, :], 0.0).then_inc(const_zeroed, 1)
        nc.gpsimd.memset(ident_bf[:, :], 0.0).then_inc(const_zeroed, 1)
        nc.gpsimd.memset(ones[:, :], 1.0).then_inc(const_ready, 1)
        pool.wait_ge(const_zeroed, 2)
        for m in (ident, ident_bf):
            nc.gpsimd.affine_select(out=m[:, :], in_=m[:, :], compare_op=ALU.not_equal, fill=1.0, base=0,
                                    pattern=[[-1, P]], channel_multiplier=1).then_inc(const_ready, 1)
        nc.gpsimd.iota(pidx[:, :], pattern=[[0, 1]], base=0, channel_multiplier=1).then_inc(const_ready, 1)
        nc.gpsimd.memset(start.zeros[:, :], 0.0).then_inc(start.consts, 1)
        pool.wait_ge(start.consts, 1)
        nc.gpsimd.affine_select(out=start.causal[:, :], in_=start.zeros[:, :], compare_op=ALU.is_ge, fill=MASKED,
                                base=0, pattern=[[-1, P]], channel_multiplier=1).then_inc(start.consts, 1)
        for b in range(NB):
            if b == 1:
                pool.wait_ge(start.w_loaded, 16)
            if b:
                split_matrix(nc, pool, start, MATS.index(SPLIT_ORDER[b - 1]), 2 * (b - 1))
            for c in range(1, DC, 2):
                make_lo(pool, nc.gpsimd, b, c, lo_odd)

    @block.scalar
    def _(act):
        act.wait_ge(c_loaded, 16)
        nc.scalar.activation(c_silu[:, :], c_in[:, :], ACT.Silu).then_inc(c_ready, 1)

        for b in range(NB):
            for s in range(b, min(b + 2, NB)) if b == 0 else range(b + 1, min(b + 2, NB)):
                act.wait_ge(var_ready, s + 1)
                nc.scalar.activation(std[:, s * TPB:(s + 1) * TPB], vare[:, s * TPB:(s + 1) * TPB], ACT.Sqrt) \
                  .then_inc(std_ready, 1)
            for c in range(DC):
                n = b * DC + c
                act.wait_ge(t_ready, n + 1)
                if n == 0:
                    act.wait_ge(mod_used, 2)
                if n >= DC:
                    act.wait_ge((lo_ready, lo_odd)[c % 2], (n - DC) // 2 + 1)
                nc.scalar.activation(h32[:, c, :], ps_t[:, n % 4, :], ACT.Identity,
                                     bias=shift_a[:, c:c + 1], scale=scale_a[:, c:c + 1]).then_inc(h_ready, 1)
                act.wait_ge(h_ready, n + 1)
                nc.scalar.activation(hT_hi[:, c, b * BT:(b + 1) * BT], h32[:, c, :], ACT.Copy) \
                  .then_inc(hi_ready, 1)

    @block.vector
    def _(dve):
        dve.wait_ge(const_ready, 4)
        nc.vector.tensor_scalar(pidx[:, :], pidx[:, :], 7, 2, ALU.bitwise_and, ALU.logical_shift_left) \
          .then_inc(idx_step, 1)
        dve.wait_ge(idx_step, 1)
        nc.vector.tensor_copy(nib_shift[:, :], pidx[:, :]).then_inc(idx_step, 1)
        dve.wait_ge(c_ready, 1)
        for c in range(DC):
            nc.vector.tensor_scalar(c_wide[:, c, :], ones[:, :], c_silu[:, c:c + 1], None, ALU.mult) \
              .then_inc(wide_ready, 1)
        steps = [0]

        def done(ins):
            ins.then_inc(dve_step, 1)
            steps[0] += 1
            dve.wait_ge(dve_step, steps[0])

        def statistics(b):
            dve.wait_ge(x_loaded[b], 16)
            for t in range(b * TPB, (b + 1) * TPB):
                last = nc.vector.bn_stats(stats[:, t, :], xt[:, b, t % TPB, :])
            done(last)
            for t in range(b * TPB, (b + 1) * TPB):
                last = nc.vector.bn_aggr(mv[:, t, :], stats[:, t, :])
            done(last)
            blk = slice(b * TPB, (b + 1) * TPB)
            nc.vector.tensor_scalar(vare[:, blk], mv[:, blk, 1], LN_EPS, None, ALU.add).then_inc(var_ready, 1)

        def normalise(b):
            blk = slice(b * TPB, (b + 1) * TPB)
            dve.wait_ge(std_ready, b + 1)
            done(nc.vector.reciprocal(rstd[:, blk], std[:, blk]))
            if b:
                dve.wait_ge(t_ready, DC * b)
            for t in range(TPB):
                n = b * TPB + t
                nc.vector.tensor_scalar(xn[:, t, :], xt[:, b, t, :], mv[:, n, 0:1], rstd[:, n:n + 1],
                                        ALU.subtract, ALU.mult).then_inc(xn_ready, 1)

        def use_section(s):
            dve.wait_ge(mod_ready, s + 1)
            if s in cols:
                done(nc.vector.tensor_tensor(diag[:, :, :], ps_mod[:, s % 2, :].rearrange("p (c k) -> p c k", c=DC),
                                             ident[:, :].unsqueeze(1).to_broadcast([P, DC, P]), ALU.mult))
                done(nc.vector.tensor_reduce(picked[:, :], diag[:, :, :], AX_X, ALU.add))
                nc.vector.tensor_scalar(cols[s][:, :], picked[:, :], 1.0 if s in (1, 4) else 0.0, None, ALU.add) \
                  .then_inc(mod_used, 1)
            else:
                g = ps_mod[:, s % 2, :]
                nc.vector.tensor_scalar(absr[:, 0, :], g, 0.0, 2.0, ALU.is_ge, ALU.mult).then_inc(gate_step, 1)
                nc.vector.tensor_scalar(absr[:, 1, :], g, -1.0, 0.25, ALU.mult, ALU.max).then_inc(gate_step, 1)
                dve.wait_ge(gate_step, 2 if s == 2 else 5)
                nc.vector.tensor_tensor(absr[:, 1, :], g, absr[:, 1, :], ALU.max).then_inc(gate_step, 1)
                dve.wait_ge(gate_step, 3 if s == 2 else 6)
                nc.vector.scalar_tensor_tensor(out=rows_kept[s][:, :], in0=absr[:, 0, :], scalar=-1.0,
                                               in1=absr[:, 1, :], op0=ALU.add, op1=ALU.mult) \
                  .then_inc(mod_used, 1)
                dve.wait_ge(mod_used, s + 1)

        def split(b):
            for c in range(0, DC, 2):
                make_lo(dve, nc.vector, b, c, lo_ready)

        statistics(0)
        normalise(0)
        statistics(1)
        use_section(0)
        use_section(1)
        for b in range(1, NB):
            if b < NB - 1:
                statistics(b + 1)
            normalise(b)
            split(b - 1)
            use_section(b + 1)
        split(NB - 1)
        use_section(5)

    @block.tensor
    def _(pe):
        pe.wait_ge(const_ready, 4)
        pe.wait_ge(wide_ready, DC)

        def mod_section(s):
            if s >= 2:
                pe.wait_ge(mod_used, s - 1)
            pe.wait_ge(wm_loaded[s], 16)
            for c in range(DC):
                last = nc.tensor.matmul(ps_mod[:, s % 2, :], c_wide[:, c, :], wm[:, s % 3, c, :],
                                        start=(c == 0), stop=(c == DC - 1))
            last.then_inc(mod_ready, 1)

        mod_section(0)
        mod_section(1)
        for b in range(NB):
            pe.wait_ge(xn_ready, (b + 1) * TPB)
            for c in range(DC):
                n = b * DC + c
                if n >= 4:
                    pe.wait_ge(h_ready, n - 3)
                for t in range(TPB):
                    last = nc.tensor.transpose(ps_t[:, n % 4, t * P:(t + 1) * P],
                                               xn[:, t, c * P:(c + 1) * P], ident[:, :])
                last.then_inc(t_ready, 1)
            mod_section(b + 2)


def attention(nc, ph, start, hbm, w_qkv, w_o, gu_packed, gu_scales, dn_packed, dn_scales, ident, ident_bf,
              nib_shift, hT_hi, hT_lo):
    def sb(name, shape, dt):
        return ph.enter_context(nc.sbuf_tensor(name, shape, dt))

    def sem(name):
        return ph.enter_context(nc.semaphore(name))

    ZBUF = 2
    causal, zeros, w_raw, w_hi, w_lo, w_loaded, w_split, consts = start
    kT = [sb(f"kT_{n}", [P, S], F32R) for n in ("hi", "lo")]
    qT = [sb(f"qT_{n}", [P, 2, BT], F32R) for n in ("hi", "lo")]
    v = [sb(f"v_{n}", [P, NT, DH], F32R) for n in ("hi", "lo")]
    vT = sb("vT", [P, BT], F32)
    probs = sb("probs", [P, 2, S], F32)
    pT = [sb(f"pT_{n}", [P, 3, NT * P], F32R) for n in ("hi", "lo")]
    z = sb("z", [P, ZBUF, 2 * P], F32)
    cmin = sb("cmin", [P, NB], F32)
    rmin = sb("rmin", [P, 2], F32)
    sums = sb("sums", [P, NT], F32)
    recips = sb("recips", [P, NT], F32)
    scales = sb("scales", [P, 2, 2 * P], F32)
    words = sb("words", [P, D], I32)
    code = sb("code", [P, D], I32)
    deq_a = sb("deq_a", [P, D], F32)
    deq_b = sb("deq_b", [P, D], F32)
    qscale = sb("qscale", [P, D], F16)
    halves = sb("halves", [P, 1], F32)
    ps_s = ph.enter_context(nc.psum_tensor("ps_s", [P, NB, BT], F32))
    ps_t = ph.enter_context(nc.psum_tensor("ps_t", [P, 2, BT], F32))
    ps_z = ph.enter_context(nc.psum_tensor("ps_z", [P, 512], F32))
    ps_p = ph.enter_context(nc.psum_tensor("ps_p", [P, BT], F32))

    scores_ready = sem("scores_ready")
    chunk_min = sem("chunk_min")
    min_ready = sem("min_ready")
    exp_ready = sem("exp_ready")
    t_ready = sem("t_ready")
    t_hi = sem("t_hi")
    t_lo = sem("t_lo")
    proj_ready = sem("proj_ready")
    proj_hi = sem("proj_hi")
    proj_lo = sem("proj_lo")
    zero_ready = sem("zero_ready")
    z_ready = sem("z_ready")
    z_scaled = sem("z_scaled")
    recip_ready = sem("recip_ready")
    recip_saved = sem("recip_saved")
    scales_loaded = [sem(f"scales_loaded{n}") for n in range(2)]
    z_saved = [sem(f"z_saved{n}") for n in range(ZBUF)]
    words_loaded = sem("words_loaded")
    qscale_loaded = sem("qscale_loaded")
    unpacked = sem("unpacked")
    deq_step = sem("deq_step")
    deq_saved = sem("deq_saved")

    SAVE_AFTER = (1, 4, 5)
    Z_DMAS = 2
    DEQ_OPS = 9
    LOADS = {0: 2, 1: 2, 2: 1}
    LOADS_BEFORE = {0: 0, 1: 2, 2: 4}
    LOADS_ALL = 5

    wo = [part[:, :, :].rearrange("p c (a n) -> p (c a) n", n=D) for part in (hT_hi, hT_lo)]
    wo_loaded = [sem(f"wo_loaded{n}") for n in range(3)]
    wo_split = sem("wo_split")
    hT_used = PREU + NU * (H - 1) + UNIT_AT[("V", NB - 1)] + 1

    block = ph.enter_context(nc.Block())
    stretches = [(1, NI), (NI, H - 1)]

    @block.sync
    def _(sp):
        def load_piece(h, k):
            sp.wait_ge(deq_step, DEQ_OPS * (PIECES * h + k)) if not (isinstance(h, int) and h + k == 0) else None
            if k < 2:
                for c in range(2):
                    src = gu_packed[bass.ds(h, 1), 2 * k + c, :, :]
                    sp.dma_start(words[:, c * 2 * P:(c + 1) * 2 * P],
                                 replicate(src, 2 * P)).then_inc(words_loaded, 16)
                sp.dma_start(qscale[:, :], gu_scales[bass.ds(h, 1), k, :].to_broadcast([P, D])) \
                  .then_inc(qscale_loaded, 16)
            else:
                sp.dma_start(words[:, :], replicate(dn_packed[bass.ds(h, 1), :, :], D)).then_inc(words_loaded, 16)
                sp.dma_start(qscale[:, :], dn_scales[bass.ds(h, 1), :].to_broadcast([P, D])) \
                  .then_inc(qscale_loaded, 16)

        def replicate(src, n):
            a = src.rearrange("a w n -> (a w) n")
            return a.unsqueeze(1).to_broadcast([WORDS, 8, n])

        def save_piece(h, k):
            sp.wait_ge(deq_step, DEQ_OPS * (PIECES * h + k + 1))
            if k < 2:
                dst = hbm["wgu"][bass.ds(h, 1), :, k * D:(k + 1) * D].rearrange("a p n -> (a p) n")
            else:
                dst = hbm["wdn"][bass.ds(h, 1), :, :].rearrange("a p n -> (a p) n")
            sp.dma_start(dst, deq_a[:, :]).then_inc(deq_saved, 16)

        def save_z(h, b):
            sp.wait_ge(z_scaled, NPAIR * h + b + 1)
            n = b % ZBUF
            for order in range(2):
                t = 2 * b + (order + b) % 2
                sp.dma_start(hbm["zT"][t, :, bass.ds(h, 1), :].rearrange("p a n -> p (a n)"),
                             z[:, n, order * P:(order + 1) * P]).then_inc(z_saved[n], 16)

        def spread_recips(h, b):
            count = NPAIR * h + b
            row = hbm["recips"][bass.ds(h, 1), b, :]
            sp.wait_ge(recip_ready, count + 1)
            sp.dma_start(row.rearrange("a (t p) -> p (a t)", p=P), recips[:, 2 * b:2 * b + 2],
                         allow_slow_non_contiguous=True).then_inc(recip_saved, 16)
            sp.wait_ge(recip_saved, 16 * (count + 1))
            sp.dma_start(scales[:, b % 2, :], row.to_broadcast([P, 2 * P])).then_inc(scales_loaded[b % 2], 16)

        def load_wo(n):
            sp.dma_start(w_raw[:, n % 3, :], w_o[:, n, :]).then_inc(wo_loaded[n % 3], 16)

        def head(h, decode, first, last):
            if last:
                sp.wait_ge(w_split, 6 * H)
                for n in range(3):
                    load_wo(n)
            if not last:
                sp.wait_ge(w_split, 6 * (h + 1))
                sp.dma_start(w_raw[:, :, :], w_qkv[bass.ds(h + 1, 1), :, :, :].rearrange("a p m n -> (a p) m n")) \
                  .then_inc(w_loaded, 16)
            if decode:
                load_piece(h, 0)
            if not first:
                save_z(h - 1, NPAIR - 2)
                spread_recips(h - 1, NPAIR - 1)
            spread_recips(h, 0)
            if not first:
                save_z(h - 1, NPAIR - 1)
            for b in range(NPAIR - 2):
                save_z(h, b)
                spread_recips(h, b + 1)
                if decode and b in SAVE_AFTER:
                    k = SAVE_AFTER.index(b)
                    save_piece(h, k)
                    if k < PIECES - 1:
                        load_piece(h, k + 1)
        head(0, True, True, False)
        for n, (a, z_) in enumerate(stretches):
            with sp.Fori(a, z_) as h:
                head(h, n == 0, False, False)
        head(H - 1, False, False, True)
        for n in range(3, WO_EARLY):
            sp.wait_ge(wo_split, 2 * (n - 2))
            load_wo(n)
        save_z(H - 1, NPAIR - 2)
        spread_recips(H - 1, NPAIR - 1)
        save_z(H - 1, NPAIR - 1)
        for n in range(ZBUF):
            sp.wait_ge(z_saved[n], Z_DMAS * 16 * H * NPAIR // ZBUF)
        sp.wait_ge(deq_saved, 16 * PIECES * NI)

    @block.gpsimd
    def _(pool):
        nc.gpsimd.memset(halves[:, :], 0.5).then_inc(consts, 1)
        pool.wait_ge(consts, 3)

        def split_weights(h, m, n):
            if n == 0:
                pool.wait_ge(w_loaded, 16 * (h + 1))
            pool.wait_ge(proj_ready, PREU + NU * (h - 1) + UNIT_AT[(MATS[m], NB - 1)] + 1)
            split_matrix(nc, pool, start, m, 6 * h + 2 * n)

        def zero_block(h, b):
            if not (isinstance(h, int) and NPAIR * h + b < 2):
                pool.wait_ge(z_ready, NPAIR * h + b - 1)
            for part in pT:
                nc.gpsimd.tensor_tensor(part[:, 2 * (b % 2), (2 * b + 1) * P:(2 * b + 2) * P],
                                        zeros[:, :], zeros[:, :], ALU.add).then_inc(zero_ready, 1)

        def decode_piece(h, k):
            base = PIECES * h + k
            made = DEQ_OPS * base
            halves_wide = halves[:, 0:1].to_broadcast([P, D])
            code_f, sign_f = code[:, :].bitcast(F32), words[:, :].bitcast(F32)
            pool.wait_ge(unpacked, 3 * (base + 1))
            pool.wait_ge(qscale_loaded, 16 * (base + 1))
            wait_for(pool, deq_saved, 16 * base)
            wait_for(pool, deq_step, made)
            nc.gpsimd.tensor_tensor(deq_b[:, :], qscale[:, :], halves_wide, ALU.mult).then_inc(deq_step, 1)
            nc.gpsimd.tensor_scalar(sign_f, words[:, :], -0.25, 1.0, ALU.mult, ALU.add).then_inc(deq_step, 1)
            nc.gpsimd.tensor_scalar(deq_a[:, :], code[:, :], 4.0, -16.0, ALU.max, ALU.add).then_inc(deq_step, 1)
            pool.wait_ge(deq_step, made + 3)
            nc.gpsimd.tensor_tensor(sign_f, sign_f, deq_b[:, :], ALU.mult).then_inc(deq_step, 1)
            nc.gpsimd.tensor_scalar(code_f, code[:, :], 1.0, None, ALU.mult).then_inc(deq_step, 1)
            pool.wait_ge(deq_step, made + 5)
            nc.gpsimd.tensor_tensor(deq_a[:, :], deq_a[:, :], code_f, ALU.add).then_inc(deq_step, 1)
            nc.gpsimd.tensor_scalar(deq_b[:, :], code_f, 6.0, 2.0, ALU.max, ALU.mult).then_inc(deq_step, 1)
            pool.wait_ge(deq_step, made + 7)
            nc.gpsimd.tensor_tensor(deq_a[:, :], deq_a[:, :], deq_b[:, :], ALU.add).then_inc(deq_step, 1)
            pool.wait_ge(deq_step, made + 8)
            nc.gpsimd.tensor_tensor(deq_a[:, :], deq_a[:, :], sign_f, ALU.mult).then_inc(deq_step, 1)

        def split_wo(n):
            pool.wait_ge(wo_loaded[n % 3], 16 * (n // 3 + 1))
            pool.wait_ge(proj_ready, hT_used)
            nc.gpsimd.tensor_tensor(wo[0][:, n, :], w_raw[:, n % 3, :], zeros[:, 0:1].to_broadcast([P, D]), ALU.add) \
              .then_inc(wo_split, 1)
            pool.wait_ge(wo_split, 2 * n + 1)
            nc.gpsimd.tensor_tensor(wo[1][:, n, :], w_raw[:, n % 3, :], wo[0][:, n, :].bitcast(F32), ALU.subtract) \
              .then_inc(wo_split, 1)

        def head(h, decode, last):
            for b in range(3):
                zero_block(h, b)
            if decode:
                decode_piece(h, 0)
            zero_block(h, 3)
            zero_block(h, 4)
            if decode:
                decode_piece(h, 1)
            if not last:
                split_weights(h + 1, MATS.index("K"), 0)
            zero_block(h, 5)
            if not last:
                split_weights(h + 1, MATS.index("Q"), 1)
            zero_block(h, 6)
            if last:
                for n in range(2):
                    split_wo(n)
            if not last:
                split_weights(h + 1, MATS.index("V"), 2)
            if decode:
                decode_piece(h, 2)
            zero_block(h, 7)
            if last:
                for n in range(2, WO_EARLY):
                    split_wo(n)
        head(0, True, False)
        for n, (a, z_) in enumerate(stretches):
            with pool.Fori(a, z_) as h:
                head(h, n == 0, False)
        head(H - 1, False, True)

    @block.tensor
    def _(pe):
        def project(h, kind, b, c):
            unit = (kind, b)
            if c:
                pass
            elif h is None:
                nth = {"Q": 0, "K": 1}[kind]
                if nth:
                    pe.wait_ge(proj_lo, nth)
            else:
                nth = UNIT_AT[unit]
                prev = UNITS[nth - 1] if nth else None
                if prev and prev[0] == "V":
                    pe.wait_ge(proj_hi, PREU + NU * h + nth)
                else:
                    pe.wait_ge(proj_lo, PREU + NSU * h + (SPLIT_AT[prev] + 1 if prev else 0))
            if kind == "VT":
                if prev[0] != "V":
                    pe.wait_ge(proj_hi, PREU + NU * h + UNIT_AT[("V", b)] + 1)
                for t in range(TPB):
                    last = nc.tensor.transpose(ps_p[:, t * P:(t + 1) * P], vT[:, t * P:(t + 1) * P], ident[:, :])
            else:
                m = MATS.index(kind[0])
                if c:
                    pass
                elif h is None:
                    pe.wait_ge(w_split, 2 * SPLIT_ORDER.index(kind) + 2)
                elif b == 0:
                    pe.wait_ge(w_split, 6 * (h if kind == "V" else h + 1) + 2 * SPLIT_ORDER.index(kind[0]) + 2)
                w = [part[:, m, c * DH:(c + 1) * DH] for part in (w_hi, w_lo)]
                ht = [part[:, c, b * BT:(b + 1) * BT] for part in (hT_hi, hT_lo)]
                last = split_matmul(nc, ps_p[:, :], w, ht, c == 0, c == DC - 1)
            if kind == "VT" or c == DC - 1:
                last.then_inc(proj_ready, 1)

        def lo_count(h, unit):
            if unit[0] in ("Q", "K") and unit[1] == 0:
                return PREU + NSU * h
            return PREU + NSU * h + SPLIT_AT[unit] + 1

        def made_at(unit):
            return SPLIT_AT[unit] if unit in SPLIT_AT else -1

        def scores(h, i):
            pe.wait_ge(exp_ready, NT * h + i) if not (isinstance(h, int) and h + i == 0) else None
            b, r = divmod(i, TPB)
            if r == 0:
                pe.wait_ge(proj_lo, lo_count(h, max((("Q", b), ("K", b)), key=made_at)))
            q = [part[:, b % 2, r * P:(r + 1) * P] for part in qT]
            for c in range(b + 1):
                n = BT if c < b else max(r + 1, 2) * P
                k = [part[:, c * BT:c * BT + n] for part in kT]
                diagonal = c == b
                last = split_matmul(nc, ps_s[:, c, 0:n], q, k, True, True)
                if diagonal:
                    last = nc.tensor.matmul(ps_s[:, c, r * P:(r + 1) * P], ident_bf[:, :], causal[:, :],
                                            start=False, stop=True, skip_group_check=True)
                last.then_inc(scores_ready, 1)

        def transposes(h, i, u):
            if u == 0:
                pe.wait_ge(exp_ready, NT * h + i + 1)
            n = chunks_before(i) + u
            if not (isinstance(h, int) and CHUNKS * h + n < 2):
                pe.wait_ge(t_lo, CHUNKS * h + n - 1)
            for k in range(4 * u, min(4 * u + 4, i + 1)):
                last = nc.tensor.transpose(ps_t[:, n % 2, (k - 4 * u) * P:(k - 4 * u + 1) * P],
                                           probs[:, i % 2, k * P:(k + 1) * P], ident[:, :])
            last.then_inc(t_ready, 1)

        def pv(h, b, k0):
            if k0 == 0:
                if not (isinstance(h, int) and h + b == 0):
                    pe.wait_ge(z_scaled, NPAIR * h + b)
                pe.wait_ge(zero_ready, 2 * (NPAIR * h + b + 1))
            if k0 % 4 == 0:
                pe.wait_ge(t_lo, CHUNKS * h + chunks_before(2 * b + 1) + k0 // 4 + 1)
                pe.wait_ge(proj_lo, lo_count(h, ("VT", k0 // 4)))
            a = b % 2
            for k in (k0, k0 + 1):
                p = [part[:, a:a + 2, k * P:(k + 1) * P] for part in pT]
                vv = [part[:, k, :] for part in v]
                last = split_matmul(nc, ps_z[:, 0:2 * P], vv, p, k == 0, k == 2 * b + 1)
            if k == 2 * b + 1:
                last.then_inc(z_ready, 1)

        def run(h, op):
            {"T": transposes, "P": project, "Z": pv}[op[0]](h, *op[1:])

        def head(h, first, last):
            for i in range(NT):
                scores(h, i)
                for op, previous in pieces(i, first, last):
                    run(h - 1 if previous else h, op)
        pe.wait_ge(consts, 2)
        for kind in ("Q", "K"):
            for c in range(DC):
                project(None, kind, 0, c)
        head(0, True, False)
        for a, z_ in stretches:
            with pe.Fori(a, z_) as h:
                head(h, False, False)
        head(H - 1, False, True)
        for op in TAIL:
            run(H - 1, op)

    @block.scalar
    def _(act):
        def unit_hi(h, unit):
            kind, b = unit
            if h is None:
                nth = {"Q": 0, "K": 1}[kind]
                act.wait_ge(proj_ready, nth + 1)
            else:
                act.wait_ge(proj_ready, PREU + NU * h + UNIT_AT[unit] + 1)
            if kind == "V":
                ins = nc.scalar.activation(vT[:, :], ps_p[:, :], ACT.Copy)
            elif kind == "VT":
                ins = nc.scalar.activation(v[0][:, b * TPB:(b + 1) * TPB, :],
                                           ps_p[:, :].rearrange("p (t n) -> p t n", t=TPB), ACT.Copy)
            elif kind[0] == "Q":
                ins = nc.scalar.activation(qT[0][:, b % 2, :], ps_p[:, :], ACT.Copy, scale=-SOFT)
            else:
                ins = nc.scalar.activation(kT[0][:, b * BT:(b + 1) * BT], ps_p[:, :], ACT.Copy)
            ins.then_inc(proj_hi, 1)

        def transposed_hi(h, i, u):
            sub = 1 if i % 2 else 2 * (i // 2 % 2)
            act.wait_ge(t_ready, CHUNKS * h + chunks_before(i) + u + 1)
            lo, hi = 4 * u * P, min(4 * u + 4, i + 1) * P
            nc.scalar.activation(pT[0][:, sub, lo:hi], ps_t[:, (chunks_before(i) + u) % 2, 0:hi - lo],
                                 ACT.Copy).then_inc(t_hi, 1)

        def exponent(h, i):
            act.wait_ge(min_ready, NT * h + i + 1)
            w = (i + 1) * P
            at = i ^ (i // 2 % 2)
            src = ps_s[:, :, :].rearrange("p c n -> p (c n)")[:, 0:w]
            nc.scalar.activation(probs[:, i % 2, 0:w], src, ACT.Exp, bias=rmin[:, i % 2:i % 2 + 1], scale=-1.0,
                                 accum_out=sums[:, at:at + 1]).then_inc(exp_ready, 1)

        def finish(h, op):
            if op[0] == "T":
                transposed_hi(h, *op[1:])
            elif op[0] == "P" and ends(op):
                unit_hi(h, op[1:3])

        def head(h, first, last):
            for i in range(NT):
                for n, (op, previous) in enumerate(pieces(i, first, last)):
                    if n == EXP_AFTER:
                        exponent(h, i)
                    finish(h - 1 if previous else h, op)
        unit_hi(None, ("Q", 0))
        unit_hi(None, ("K", 0))
        head(0, True, False)
        for a, z_ in stretches:
            with act.Fori(a, z_) as h:
                head(h, False, False)
        head(H - 1, False, True)
        for op in TAIL:
            finish(H - 1, op)

    @block.vector
    def _(dve):
        def unit_lo(h, unit):
            kind, b = unit
            if kind == "V":
                return
            if h is None:
                nth = {"Q": 0, "K": 1}[kind]
                dve.wait_ge(proj_hi, nth + 1)
            else:
                dve.wait_ge(proj_hi, PREU + NU * h + UNIT_AT[unit] + 1)
            if kind == "VT":
                parts = [part[:, b * TPB:(b + 1) * TPB, :].rearrange("p t n -> p (t n)") for part in v]
            elif kind[0] == "Q":
                parts = [part[:, b % 2, :] for part in qT]
            else:
                parts = [part[:, b * BT:(b + 1) * BT] for part in kT]
            if kind[0] == "Q":
                ins = nc.vector.scalar_tensor_tensor(out=parts[1], in0=ps_p[:, :], scalar=-SOFT,
                                                     in1=parts[0].bitcast(F32), op0=ALU.mult, op1=ALU.subtract)
            else:
                ins = nc.vector.tensor_tensor(parts[1], ps_p[:, :], parts[0].bitcast(F32), ALU.subtract)
            ins.then_inc(proj_lo, 1)

        def minimum(h, i):
            nch = n_chunks(i)
            for c in range(nch):
                dve.wait_ge(scores_ready, CHUNKS * h + chunks_before(i) + c + 1)
                w = BT if c < nch - 1 else (i % TPB + 1) * P
                if nch == 1:
                    nc.vector.tensor_reduce(rmin[:, i % 2:i % 2 + 1], ps_s[:, c, 0:w], AX_X, ALU.min) \
                      .then_inc(min_ready, 1)
                else:
                    nc.vector.tensor_reduce(cmin[:, c:c + 1], ps_s[:, c, 0:w], AX_X, ALU.min) \
                      .then_inc(chunk_min, 1)
            if nch > 1:
                done = sum(n_chunks(j) for j in range(i + 1) if n_chunks(j) > 1)
                dve.wait_ge(chunk_min, MULTI * h + done)
                nc.vector.tensor_reduce(rmin[:, i % 2:i % 2 + 1], cmin[:, 0:nch], AX_X, ALU.min) \
                  .then_inc(min_ready, 1)

        def transposed_lo(h, i, u):
            sub = 1 if i % 2 else 2 * (i // 2 % 2)
            dve.wait_ge(t_hi, CHUNKS * h + chunks_before(i) + u + 1)
            lo, hi = 4 * u * P, min(4 * u + 4, i + 1) * P
            nc.vector.tensor_tensor(pT[1][:, sub, lo:hi], ps_t[:, (chunks_before(i) + u) % 2, 0:hi - lo],
                                    pT[0][:, sub, lo:hi].bitcast(F32), ALU.subtract).then_inc(t_lo, 1)

        def recip(h, b):
            dve.wait_ge(exp_ready, NT * h + 2 * b + 2)
            nc.vector.reciprocal(recips[:, 2 * b:2 * b + 2], sums[:, 2 * b:2 * b + 2]).then_inc(recip_ready, 1)

        def scale_z(h, b):
            dve.wait_ge(z_ready, NPAIR * h + b + 1)
            dve.wait_ge(scales_loaded[b % 2], 16 * (NPAIR // 2 * h + b // 2 + 1))
            wait_for(dve, z_saved[b % ZBUF], Z_DMAS * 16 * (NPAIR // ZBUF * h + b // ZBUF))
            nc.vector.tensor_tensor(z[:, b % ZBUF, :], ps_z[:, 0:2 * P], scales[:, b % 2, :], ALU.mult) \
              .then_inc(z_scaled, 1)

        def unpack(h, k):
            base = PIECES * h + k
            dve.wait_ge(words_loaded, 16 * (LOADS_ALL * h + LOADS_BEFORE[k] + LOADS[k]))
            nc.vector.tensor_tensor(words[:, :], words[:, :], nib_shift[:, 0:1].to_broadcast([P, D]),
                                    ALU.logical_shift_right).then_inc(unpacked, 1)
            dve.wait_ge(unpacked, 3 * base + 1)
            nc.vector.tensor_scalar(code[:, :], words[:, :], 7, None, ALU.bitwise_and).then_inc(unpacked, 1)
            dve.wait_ge(unpacked, 3 * base + 2)
            nc.vector.tensor_scalar(words[:, :], words[:, :], 8, None, ALU.bitwise_and).then_inc(unpacked, 1)

        def finish(h, op):
            if op[0] == "T":
                transposed_lo(h, *op[1:])
            elif ends(op):
                unit_lo(h, op[1:3]) if op[0] == "P" else scale_z(h, op[1])

        def head(h, decode, first, last):
            for i in range(NT):
                minimum(h, i)
                if i % 2 == 0 and not (first and i == 0):
                    recip(h if i else h - 1, (i // 2 - 1) % NPAIR)
                for op, previous in pieces(i, first, last):
                    finish(h - 1 if previous else h, op)
                if decode and i in UNPACK_STEP:
                    unpack(h, UNPACK_STEP[i])
        unit_lo(None, ("Q", 0))
        unit_lo(None, ("K", 0))
        head(0, True, True, False)
        for n, (a, z_) in enumerate(stretches):
            with dve.Fori(a, z_) as h:
                head(h, n == 0, False, False)
        head(H - 1, False, False, True)
        recip(H - 1, NPAIR - 1)
        for op in TAIL:
            finish(H - 1, op)


def output_projection(nc, ph, gu, hbm, x, w_o, ident, gate_a, shift_b, scale_b, hT_hi, hT_lo, hT):
    def sb(name, shape, dt):
        return ph.enter_context(nc.sbuf_tensor(name, shape, dt))

    def sem(name):
        return ph.enter_context(nc.semaphore("o_" + name))

    HH = H // 2
    RW = 2
    WO_STAGES = (H - WO_EARLY) // RW
    wo = [part[:, :, :].rearrange("p c (a n) -> p (c a) n", n=D) for part in (hT_hi, hT_lo)]
    stage = sb("wo_stage", [P, 2, RW, D], F32)
    zt = sb("o_z", [P, 2, HH, P], F32)
    zs = [sb(f"o_z{n}", [P, 2, HH, P], F32R) for n in ("hi", "lo")]
    xt = sb("o_x", [P, 2, D], F32)
    x1 = sb("o_x1", [P, 2, D], F32)
    xn = sb("o_xn", [P, 2, D], F32)
    h32 = sb("o_h32", [P, 2, D], F32)
    hs = [sb(f"o_h{n}", [P, 2, D], F32R) for n in ("hi", "lo")]
    stats = sb("o_stats", [P, 6], F32)
    mv = sb("o_mv", [P, 2], F32)
    vare = sb("o_vare", [P, 1], F32)
    std = sb("o_std", [P, 1], F32)
    rstd = sb("o_rstd", [P, 1], F32)
    ps_o = ph.enter_context(nc.psum_tensor("o_pso", [P, 2, 512], F32))
    ps_t = ph.enter_context(nc.psum_tensor("o_pst", [P, 2, 512], F32))

    wo_loaded = [sem(f"wo_loaded{n}") for n in range(2)]
    wo_hi = sem("wo_hi")
    wo_lo = sem("wo_lo")
    z_loaded = [sem(f"z_loaded{n}") for n in range(2)]
    x_loaded = [sem(f"x_loaded{n}") for n in range(2)]
    z_hi = sem("z_hi")
    z_lo = sem("z_lo")
    half_done = sem("half_done")
    dve_step = sem("dve_step")
    x1_ready = sem("x1_ready")
    x1_saved = [sem(f"x1_saved{n}") for n in range(2)]
    var_ready = sem("var_ready")
    std_ready = sem("std_ready")
    xn_ready = sem("xn_ready")
    t_ready = sem("t_ready")
    h_ready = [sem(f"h_ready{n}") for n in range(2)]
    h_hi = sem("h_hi")
    h_lo = sem("h_lo")
    h_saved = [sem(f"h_saved{n}") for n in range(2)]
    STEPS = 4

    def by_chunk(buffer, tile):
        return buffer[:, tile.parity, :].rearrange("p (c n) -> p c n", c=DC)

    def split_places(tile):
        if isinstance(tile.t, int) and tile.t == NT - 1:
            return [part[:, :, rows_of(tile.t)] for part in hT]
        return [by_chunk(part, tile) for part in hs]

    block = ph.enter_context(nc.Block())

    @block.sync
    def _(sp):
        def load_wo(n):
            if n >= 2:
                sp.wait_ge(wo_lo, n - 1)
            h = WO_EARLY + n * RW
            sp.dma_start(stage[:, n % 2, :, :], w_o[:, h:h + RW, :]).then_inc(wo_loaded[n % 2], 16)

        def load_half(tile, f):
            if not is_first(tile):
                sp.wait_ge(z_lo, 2 * tile.t + f - 1)
            sp.dma_start(zt[:, f, :, :], hbm["zT"][bass.ds(tile.t, 1), :, f * HH:(f + 1) * HH, :]
                         .rearrange("a p h n -> (a p) h n")).then_inc(z_loaded[f], 16)

        def load_x(tile):
            if not is_first(tile):
                sp.wait_ge(x1_ready, tile.t - 1)
            sp.dma_start(xt[:, tile.parity, :], x[rows_of(tile.t), :]).then_inc(x_loaded[tile.parity], 16)

        def step(tile, first, last):
            if not last:
                load_half(tile.after(), 0)
                load_x(tile.after())
                load_half(tile.after(), 1)
        load_half(FIRST, 0)
        load_wo(0)
        load_half(FIRST, 1)
        load_wo(1)
        load_x(FIRST)
        for n in range(2, WO_STAGES):
            load_wo(n)
        gu.load(sp, hbm, 0)
        token_tiles(sp, step)
        for n in range(2):
            sp.wait_ge(h_saved[n], 2 * 16 * (NT // 2 - n))
            sp.wait_ge(x1_saved[n], 16 * NT // 2)

    @block.vector
    def _(dve):
        def wo_part(n):
            dve.wait_ge(wo_hi, n + 1)
            sl = slice(WO_EARLY + n * RW, WO_EARLY + (n + 1) * RW)
            nc.vector.tensor_tensor(wo[1][:, sl, :], stage[:, n % 2, :, :], wo[0][:, sl, :].bitcast(F32),
                                    ALU.subtract).then_inc(wo_lo, 1)

        def split_half(tile, f):
            dve.wait_ge(z_hi, 2 * tile.t + f + 1)
            nc.vector.tensor_tensor(zs[1][:, f, :, :], zt[:, f, :, :], zs[0][:, f, :, :].bitcast(F32),
                                    ALU.subtract).then_inc(z_lo, 1)

        def split_h(tile):
            dve.wait_ge(h_hi, tile.t + 1)
            hi, lo = split_places(tile)
            nc.vector.tensor_tensor(lo, by_chunk(h32, tile), hi.bitcast(F32), ALU.subtract).then_inc(h_lo, 1)

        def step(tile, first, last):
            t, parity, k = tile
            n = [0]

            def done(ins):
                n[0] += 1
                ins.then_inc(dve_step, 1)
                dve.wait_ge(dve_step, STEPS * t + n[0])
            if not last:
                split_half(tile.after(), 0)
                split_half(tile.after(), 1)
            dve.wait_ge(half_done, 2 * t + 2)
            wait_for(dve, x1_saved[parity], 16 * k)
            done(nc.vector.tensor_tensor(x1[:, parity, :], ps_o[:, parity, :], gate_a[:, :], ALU.mult))
            dve.wait_ge(x_loaded[parity], 16 * (k + 1))
            nc.vector.tensor_tensor(x1[:, parity, :], x1[:, parity, :], xt[:, parity, :], ALU.add) \
              .then_inc(x1_ready, 1)
            dve.wait_ge(x1_ready, t + 1)
            done(nc.vector.bn_stats(stats[:, :], x1[:, parity, :]))
            if not first:
                split_h(tile.before())
            done(nc.vector.bn_aggr(mv[:, :], stats[:, :]))
            nc.vector.tensor_scalar(vare[:, :], mv[:, 1:2], LN_EPS, None, ALU.add).then_inc(var_ready, 1)
            dve.wait_ge(std_ready, t + 1)
            done(nc.vector.reciprocal(rstd[:, :], std[:, :]))
            if not first:
                dve.wait_ge(t_ready, t - 1)
            nc.vector.tensor_scalar(xn[:, parity, :], x1[:, parity, :], mv[:, 0:1], rstd[:, 0:1],
                                    ALU.subtract, ALU.mult).then_inc(xn_ready, 1)
            dve.wait_ge(xn_ready, t + 1)
            if isinstance(t, int) and t == 1:
                for m in range(2):
                    gu.make_lo(nc, dve, 0, m)
        split_half(FIRST, 0)
        wo_part(0)
        split_half(FIRST, 1)
        for n in range(1, WO_STAGES):
            wo_part(n)
        token_tiles(dve, step)
        split_h(LAST)

    @block.scalar
    def _(act):
        def wo_part(n):
            act.wait_ge(wo_loaded[n % 2], 16 * (n // 2 + 1))
            sl = slice(WO_EARLY + n * RW, WO_EARLY + (n + 1) * RW)
            nc.scalar.activation(wo[0][:, sl, :], stage[:, n % 2, :, :], ACT.Copy).then_inc(wo_hi, 1)

        def half_hi(tile, f):
            act.wait_ge(z_loaded[f], 16 * (tile.t + 1))
            if not is_first(tile):
                act.wait_ge(half_done, 2 * tile.t + f - 1)
            nc.scalar.activation(zs[0][:, f, :, :], zt[:, f, :, :], ACT.Copy).then_inc(z_hi, 1)

        def save_h(tile):
            act.wait_ge(h_lo, tile.t + 1)
            for part, whole in zip(hs, hT):
                act.dma_start(whole[:, :, rows_of(tile.t)].bitcast(F32),
                              part[:, tile.parity, :].rearrange("p (c n) -> p c n", c=DC).bitcast(F32)) \
                   .then_inc(h_saved[tile.parity], 16)

        def modulate(tile):
            t, parity, k = tile
            act.wait_ge(t_ready, t + 1)
            wait_for(act, h_saved[parity], 32 * k)
            for c in range(DC):
                nc.scalar.activation(h32[:, parity, c * P:(c + 1) * P], ps_t[:, parity, c * P:(c + 1) * P],
                                     ACT.Identity, bias=shift_b[:, c:c + 1], scale=scale_b[:, c:c + 1]) \
                  .then_inc(h_ready[parity], 1)
            act.wait_ge(h_ready[parity], DC * (k + 1))
            nc.scalar.activation(split_places(tile)[0], by_chunk(h32, tile), ACT.Copy).then_inc(h_hi, 1)

        def step(tile, first, last):
            if not last:
                half_hi(tile.after(), 0)
                half_hi(tile.after(), 1)
            if not first:
                modulate(tile.before())
            act.wait_ge(var_ready, tile.t + 1)
            nc.scalar.activation(std[:, :], vare[:, :], ACT.Sqrt).then_inc(std_ready, 1)
            if not first:
                save_h(tile.before())
            act.wait_ge(x1_ready, tile.t + 1)
            act.dma_start(hbm["x1"][bass.ds(tile.t, 1), :, :].rearrange("a p d -> (a p) d"),
                          x1[:, tile.parity, :]).then_inc(x1_saved[tile.parity], 16)
            if isinstance(tile.t, int) and tile.t == 1:
                for m in range(2):
                    gu.make_hi(nc, act, 0, m)
        half_hi(FIRST, 0)
        wo_part(0)
        half_hi(FIRST, 1)
        for n in range(1, WO_STAGES):
            wo_part(n)
        token_tiles(act, step)
        modulate(LAST)

    @block.tensor
    def _(pe):
        def transposes(tile):
            t, parity, k = tile
            pe.wait_ge(xn_ready, t + 1)
            wait_for(pe, h_ready[parity], DC * k)
            for c in range(DC):
                last = nc.tensor.transpose(ps_t[:, parity, c * P:(c + 1) * P], xn[:, parity, c * P:(c + 1) * P],
                                           ident[:, :])
            last.then_inc(t_ready, 1)

        def step(tile, first, last):
            t, parity, k = tile
            if not first:
                pe.wait_ge(x1_ready, t - 1)
            for f in range(2):
                pe.wait_ge(z_lo, 2 * t + f + 1)
                for n in range(HH):
                    h = f * HH + n
                    if first and h >= WO_EARLY and (h - WO_EARLY) % RW == 0:
                        pe.wait_ge(wo_lo, (h - WO_EARLY) // RW + 1)
                    zz = [part[:, f, n, :] for part in zs]
                    w = [part[:, h, :] for part in wo]
                    mm = split_matmul(nc, ps_o[:, parity, :], zz, w, h == 0, h == H - 1)
                mm.then_inc(half_done, 1)
            if not first:
                transposes(tile.before())
        token_tiles(pe, step)
        transposes(LAST)


def gate_up(nc, ph, gu, hbm, mid, hT, wd_stage, wd_loaded):
    def sb(name, shape, dt):
        return ph.enter_context(nc.sbuf_tensor(name, shape, dt))

    def sem(name):
        return ph.enter_context(nc.semaphore("g_" + name))

    w = gu.parts
    sg = sb("g_silu", [P, NB, BT], F32)
    ps = [ph.enter_context(nc.psum_tensor(f"g_ps{m}", [P, NB, BT], F32)) for m in ("gate", "up")]
    gate_ready = sem("gate_ready")
    up_ready = sem("up_ready")
    silu_ready = sem("silu_ready")
    mid_ready = sem("mid_ready")
    block = ph.enter_context(nc.Block())

    def feature_tiles(eng, step):
        step(0, False)
        with eng.Fori(1, NI - 1) as n:
            step(n, False)
        step(NI - 1, True)

    @block.sync
    def _(sp):
        for n in range(WD_STAGE):
            sp.dma_start(wd_stage[:, n, :], hbm["wdn"][n]).then_inc(wd_loaded[n], 16)

        def step(n, last):
            if not last:
                sp.wait_ge(gu.lo, 2 * n + 2)
                gu.load(sp, hbm, n + 1)
        feature_tiles(sp, step)

    @block.scalar
    def _(act):
        def hi(n, m):
            act.wait_ge((gate_ready, up_ready)[m], NB * n)
            gu.make_hi(nc, act, n, m)

        def step(n, last):
            for b in range(NB):
                act.wait_ge(gate_ready, NB * n + b + 1)
                if b == 0:
                    wait_for(act, mid_ready, NB * n)
                nc.scalar.activation(sg[:, b, :], ps[0][:, b, :], ACT.Silu).then_inc(silu_ready, 1)
            if not last:
                hi(n + 1, 0)
                hi(n + 1, 1)

        feature_tiles(act, step)

    @block.vector
    def _(dve):
        def step(n, last):
            if not last:
                gu.make_lo(nc, dve, n + 1, 0)
            for b in range(NB):
                dve.wait_ge(up_ready, NB * n + b + 1)
                dve.wait_ge(silu_ready, NB * n + b + 1)
                dst = mid[:, bass.ds(n, 1), b * BT:(b + 1) * BT].rearrange("p a n -> p (a n)")
                nc.vector.tensor_tensor(dst, sg[:, b, :], ps[1][:, b, :], ALU.mult).then_inc(mid_ready, 1)
            if not last:
                gu.make_lo(nc, dve, n + 1, 1)
        feature_tiles(dve, step)

    @block.tensor
    def _(pe):
        def step(n, last):
            for m in range(2):
                pe.wait_ge(gu.lo, 2 * n + m + 1)
                for b in range(NB):
                    wait_for(pe, (silu_ready, mid_ready)[m], NB * n if b == 0 else 0)
                    for c in range(DC):
                        ww = [part[:, c, :] for part in w[m]]
                        hh = [part[:, c, b * BT:(b + 1) * BT] for part in hT]
                        mm = split_matmul(nc, ps[m][:, b, :], ww, hh, c == 0, c == DC - 1)
                    mm.then_inc((gate_ready, up_ready)[m], 1)
        feature_tiles(pe, step)


def down(nc, ph, hbm, mid, gate_b, hT, stage, wd_loaded, out):
    def sb(name, shape, dt):
        return ph.enter_context(nc.sbuf_tensor(name, shape, dt))

    def sem(name):
        return ph.enter_context(nc.semaphore("d_" + name))

    wd = [part[:, :, :].rearrange("p c n -> p (c n)")[:, 0:NI * D] for part in hT]
    ms = [sb(f"d_m{n}", [P, 2, NI, P], F32R) for n in ("hi", "lo")]
    x1 = sb("d_x1", [P, 2, D], F32)
    y = sb("d_y", [P, 2, D], F32)
    junk = sb("d_junk", [P, D], F32)
    ss = sb("d_ss", [P, 1], F32)
    ms_eps = sb("d_mse", [P, 1], F32)
    rms = sb("d_rms", [P, 1], F32)
    rrms = sb("d_rrms", [P, 1], F32)
    ps_y = ph.enter_context(nc.psum_tensor("d_psy", [P, 2, 512], F32))

    wd_hi = sem("wd_hi")
    wd_lo = sem("wd_lo")
    m_hi = sem("m_hi")
    m_lo = sem("m_lo")
    y_ready = sem("y_ready")
    square_ready = sem("square_ready")
    rms_ready = sem("rms_ready")
    mean_ready = sem("mean_ready")
    dve_step = sem("dve_step")
    y_done = sem("y_done")
    x1_loaded = [sem(f"x1_loaded{n}") for n in range(2)]
    out_saved = [sem(f"out_saved{n}") for n in range(2)]
    STEPS = 2
    block = ph.enter_context(nc.Block())

    @block.sync
    def _(sp):
        for n in range(WD_STAGE, NI):
            sp.wait_ge(wd_lo, n - WD_STAGE + 1)
            sp.dma_start(stage[:, n % WD_STAGE, :], hbm["wdn"][n]).then_inc(wd_loaded[n % WD_STAGE], 16)

        def load_x1(tile):
            if not is_first(tile):
                sp.wait_ge(y_done, tile.t - 1)
            sp.dma_start(x1[:, tile.parity, :], hbm["x1"][bass.ds(tile.t, 1), :, :].rearrange("a p d -> (a p) d")) \
              .then_inc(x1_loaded[tile.parity], 16)

        def step(tile, first, last):
            if not last:
                load_x1(tile.after())
            sp.wait_ge(y_done, tile.t + 1)
            sp.dma_start(out[rows_of(tile.t), :], y[:, tile.parity, :]).then_inc(out_saved[tile.parity], 16)
        load_x1(FIRST)
        token_tiles(sp, step)
        for n in range(2):
            sp.wait_ge(out_saved[n], 16 * NT // 2)

    @block.scalar
    def _(act):
        for n in range(NI):
            act.wait_ge(wd_loaded[n % WD_STAGE], 16 * (n // WD_STAGE + 1))
            nc.scalar.activation(wd[0][:, n * D:(n + 1) * D], stage[:, n % WD_STAGE, :], ACT.Copy).then_inc(wd_hi, 1)

        def step(tile, first, last):
            act.wait_ge(y_ready, tile.t + 1)
            if not first:
                act.wait_ge(mean_ready, tile.t)
            nc.scalar.activation(junk[:, :], ps_y[:, tile.parity, :], ACT.Square, accum_out=ss[:, :]) \
              .then_inc(square_ready, 1)
            act.wait_ge(mean_ready, tile.t + 1)
            nc.scalar.activation(rms[:, :], ms_eps[:, :], ACT.Sqrt).then_inc(rms_ready, 1)
        token_tiles(act, step)

    @block.vector
    def _(dve):
        def split(tile):
            if not is_first(tile):
                dve.wait_ge(y_ready, tile.t - 1)
            src = mid[:, :, rows_of(tile.t)]
            nc.vector.tensor_tensor(ms[0][:, tile.parity, :, :], src, src, ALU.max).then_inc(m_hi, 1)
            dve.wait_ge(m_hi, tile.t + 1)
            nc.vector.tensor_tensor(ms[1][:, tile.parity, :, :], src, ms[0][:, tile.parity, :, :].bitcast(F32),
                                    ALU.subtract).then_inc(m_lo, 1)

        def step(tile, first, last):
            t, parity, k = tile
            if not last:
                split(tile.after())
            dve.wait_ge(square_ready, t + 1)
            nc.vector.tensor_scalar(ms_eps[:, :], ss[:, :], 1.0 / D, RMS_EPS, ALU.mult, ALU.add) \
              .then_inc(mean_ready, 1)
            dve.wait_ge(rms_ready, t + 1)
            nc.vector.reciprocal(rrms[:, :], rms[:, :]).then_inc(dve_step, 1)
            dve.wait_ge(dve_step, STEPS * t + 1)
            wait_for(dve, out_saved[parity], 16 * k)
            nc.vector.scalar_tensor_tensor(out=y[:, parity, :], in0=ps_y[:, parity, :], scalar=rrms[:, 0:1],
                                           in1=gate_b[:, :], op0=ALU.mult, op1=ALU.mult).then_inc(dve_step, 1)
            dve.wait_ge(dve_step, STEPS * t + 2)
            dve.wait_ge(x1_loaded[parity], 16 * (k + 1))
            nc.vector.tensor_tensor(y[:, parity, :], y[:, parity, :], x1[:, parity, :], ALU.add).then_inc(y_done, 1)
        split(FIRST)
        for n in range(NI):
            dve.wait_ge(wd_hi, n + 1)
            nc.vector.tensor_tensor(wd[1][:, n * D:(n + 1) * D], stage[:, n % WD_STAGE, :],
                                    wd[0][:, n * D:(n + 1) * D].bitcast(F32), ALU.subtract).then_inc(wd_lo, 1)
        token_tiles(dve, step)

    @block.tensor
    def _(pe):
        def step(tile, first, last):
            t, parity, k = tile
            pe.wait_ge(m_lo, t + 1)
            if not first:
                pe.wait_ge(y_done, t - 1)
            for n in range(NI):
                if first:
                    pe.wait_ge(wd_lo, n + 1)
                mt = [part[:, parity, n, :] for part in ms]
                w = [part[:, n * D:(n + 1) * D] for part in wd]
                mm = split_matmul(nc, ps_y[:, parity, :], mt, w, n == 0, n == NI - 1)
            mm.then_inc(y_ready, 1)
        token_tiles(pe, step)


def kernel(L0_attn_x, L0_attn_W_K, L0_attn_W_Q, L0_attn_W_V, L0_attn_W_O, L0_ffn_gate_up_packed,
           L0_ffn_gate_up_scales, L0_ffn_down_packed, L0_ffn_down_scales, L0_c, L0_wmod):
    import numpy as np
    import concourse.bacc as bacc
    from concourse.bass_utils import run_bass_kernel_spmd

    def a(v):
        return np.asarray(v)

    def heads(w):
        return a(w).reshape(H, DH, DC, P).transpose(0, 3, 2, 1).reshape(H, P, 1, DC * DH)

    gu = a(L0_ffn_gate_up_packed).reshape(2, NI, P, DC, WORDS)
    gus = a(L0_ffn_gate_up_scales).reshape(DC, 2, NI, P)
    arrays = {
        "x": a(L0_attn_x).reshape(S, D),
        "w_qkv": np.concatenate([heads(w) for w in (L0_attn_W_Q, L0_attn_W_K, L0_attn_W_V)], axis=2),
        "w_o": a(L0_attn_W_O).reshape(D, H, P).transpose(2, 1, 0),
        "gu_packed": gu.transpose(1, 3, 4, 0, 2).reshape(NI, DC, WORDS, 2 * P),
        "gu_scales": gus.transpose(2, 0, 1, 3).reshape(NI, 2, D),
        "dn_packed": a(L0_ffn_down_packed).reshape(D, NI, WORDS).transpose(1, 2, 0),
        "dn_scales": a(L0_ffn_down_scales),
        "c_cols": a(L0_c).reshape(DC, P).transpose(1, 0),
        "w_mod": a(L0_wmod),
    }
    nc = bacc.Bacc("TRN2", target_bir_lowering=False, num_devices=1)
    ins = {}
    arrays = {n: np.ascontiguousarray(v) for n, v in arrays.items()}
    for n, v in arrays.items():
        ins[n] = nc.dram_tensor("in_" + n, v.shape, mybir.dt.from_np(v.dtype), kind="ExternalInput").ap()
    out = nc.dram_tensor("out_x", [S, D], F32, kind="ExternalOutput").ap()
    adaln_kernel(nc, out=out, **ins)
    r = run_bass_kernel_spmd(nc, [{"in_" + n: v for n, v in arrays.items()}], core_ids=[0])
    return r.results[0]["out_x"].reshape(1, S, D)
```
